# Optimizing a Trainium2 kernel written in Bass

```python
import numpy as np
import jax
import jax.numpy as jnp

def _softmax(x, axis=-1):
    return jax.nn.softmax(x, axis=axis)

def _gelu(x):
    return jax.nn.gelu(x, approximate=True)

def _silu(x):
    return jax.nn.silu(x)

def _sigmoid(x):
    return jax.nn.sigmoid(x)

def _layernorm(x, axis=-1, eps=1e-05):
    m = jnp.mean(x, axis=axis, keepdims=True)
    v = jnp.var(x, axis=axis, keepdims=True)
    return (x - m) / jnp.sqrt(v + eps)

def _scatter_add(tgt, idx, src, axis=0):
    return tgt.at[idx].add(src)

def _segment_sum(src, seg, n):
    return jax.ops.segment_sum(src, seg, n)
kernel_name = 'mk_gnn_preln_d2_gnn_r32_c346f4'

def setup_inputs(seed: int=0):
    np.random.seed(seed)
    _w = jnp.asarray

    def _rec_inputs():
        import jax
        import jax.numpy as jnp
        _gk = jax.random.key(seed)
        x = -0.0003713 + 1 * jax.random.normal(jax.random.fold_in(_gk, 1), (3125, 128), jnp.float32)
        src = jax.random.randint(jax.random.fold_in(_gk, 2), (100000,), 0, 3125, jnp.int32)
        dst = jnp.minimum((3125 * jax.random.uniform(jax.random.fold_in(_gk, 3), (100000,)) ** 2.0).astype(jnp.int32), 99999)
        _o = jnp.argsort(dst, stable=True)
        src = src[_o]
        dst = dst[_o]
        edge_type_5 = jax.random.randint(jax.random.fold_in(_gk, 13), (100000,), 0, 5, jnp.int32)
        return (x, src, dst, edge_type_5)
    x, src, dst, edge_type_5 = _rec_inputs()

    def _L0_gnn_setup():
        import jax, jax.numpy as jnp
        import numpy as np
        N_NODES = 3125
        N_EDGES = 50000
        D = 128
        H = 8
        DH = D // H
        DFF = 2 * D
        EPS_LN = 1e-05

        def _ln(x, g, b):
            mu = jnp.mean(x, axis=-1, keepdims=True)
            var = jnp.var(x, axis=-1, keepdims=True)
            return (x - mu) * jax.lax.rsqrt(var + EPS_LN) * g + b
        key = jax.random.key(seed)
        ks = jax.random.split(key, 12)
        s = 1.0 / np.sqrt(D)
        inp = {'h': jax.random.normal(ks[0], (N_NODES, D), jnp.float32), 'src': jax.random.randint(ks[1], (N_EDGES,), 0, N_NODES, jnp.int32), 'dst': jax.random.randint(ks[2], (N_EDGES,), 0, N_NODES, jnp.int32), 'Wq': jax.random.normal(ks[3], (D, D), jnp.float32) * s, 'Wk': jax.random.normal(ks[4], (D, D), jnp.float32) * s, 'Wv': jax.random.normal(ks[5], (D, D), jnp.float32) * s, 'Wo': jax.random.normal(ks[6], (D, D), jnp.float32) * s, 'bo': jnp.zeros((D,), jnp.float32), 'ln1_g': jnp.ones((D,), jnp.float32), 'ln1_b': jnp.zeros((D,), jnp.float32), 'W1': jax.random.normal(ks[7], (D, DFF), jnp.float32) * s, 'b1': jnp.zeros((DFF,), jnp.float32), 'W2': jax.random.normal(ks[8], (DFF, D), jnp.float32) * (1.0 / np.sqrt(DFF)), 'b2': jnp.zeros((D,), jnp.float32), 'ln2_g': jnp.ones((D,), jnp.float32), 'ln2_b': jnp.zeros((D,), jnp.float32)}
        return inp
    _L0_gnn_all = _L0_gnn_setup()
    _L0_gnn_in = {k: v for k, v in _L0_gnn_all.items() if k in ('Wq', 'Wk', 'Wv', 'Wo', 'bo', 'ln1_g', 'ln1_b', 'W1', 'b1', 'W2', 'b2', 'ln2_g', 'ln2_b')}
    del _L0_gnn_all

    def _L1_gnn_setup():
        import jax, jax.numpy as jnp
        import numpy as np
        N = 50000
        E = 20000
        HIDDEN = 128
        R = 5
        HEADS = 8
        HEAD_DIM = HIDDEN // HEADS
        LN_EPS = 1e-05

        def _fused_forward(node_embeddings, W_Q, W_K, W_V, attn_bias, out_proj_w, out_proj_b, ln_gamma, ln_beta, edge_index, edge_types):
            src, dst = (edge_index[0], edge_index[1])
            n = node_embeddings.shape[0]
            x_src = node_embeddings[src]
            x_dst = node_embeddings[dst]
            scale = HEAD_DIM ** 0.5
            NEG = jnp.float32(-1000000000.0)
            out = jnp.zeros((n, HEADS, HEAD_DIM), dtype=node_embeddings.dtype)
            for r in range(R):
                mask = edge_types == r
                q = jnp.einsum('eh,khd->ekd', x_dst, W_Q[r])
                k = jnp.einsum('eh,khd->ekd', x_src, W_K[r])
                v = jnp.einsum('eh,khd->ekd', x_src, W_V[r])
                logits = (q * k).sum(-1) / scale + attn_bias[r][None, :]
                masked_logits = jnp.where(mask[:, None], logits, NEG)
                max_v = jax.ops.segment_max(masked_logits, dst, num_segments=n)
                max_v = jnp.maximum(max_v, NEG)
                exp_l = jnp.where(mask[:, None], jnp.exp(masked_logits - max_v[dst]), 0.0)
                sum_exp = jax.ops.segment_sum(exp_l, dst, num_segments=n)
                attn = exp_l / (sum_exp[dst] + 1e-12)
                out = out + jax.ops.segment_sum(attn[:, :, None] * v, dst, num_segments=n)
            out = out.reshape(n, HIDDEN)
            out = out @ out_proj_w.T + out_proj_b
            h = out + node_embeddings
            mu = h.mean(-1, keepdims=True)
            var = ((h - mu) ** 2).mean(-1, keepdims=True)
            return (h - mu) / jnp.sqrt(var + LN_EPS) * ln_gamma + ln_beta
        key = jax.random.key(seed)
        ks = jax.random.split(key, 10)
        bound = float(np.sqrt(6.0 / (HIDDEN + HEAD_DIM)))
        pbound = float(np.sqrt(1.0 / HIDDEN))
        return {'node_embeddings': jax.random.normal(ks[0], (N, HIDDEN), dtype=jnp.float32), 'edge_index': jax.random.randint(ks[1], (2, E), 0, N, dtype=jnp.int64), 'edge_types': jax.random.randint(ks[2], (E,), 0, R, dtype=jnp.int64), 'W_Q': jax.random.uniform(ks[3], (R, HEADS, HIDDEN, HEAD_DIM), minval=-bound, maxval=bound, dtype=jnp.float32), 'W_K': jax.random.uniform(ks[4], (R, HEADS, HIDDEN, HEAD_DIM), minval=-bound, maxval=bound, dtype=jnp.float32), 'W_V': jax.random.uniform(ks[5], (R, HEADS, HIDDEN, HEAD_DIM), minval=-bound, maxval=bound, dtype=jnp.float32), 'attn_bias': jnp.zeros((R, HEADS), dtype=jnp.float32), 'out_proj_w': jax.random.uniform(ks[6], (HIDDEN, HIDDEN), minval=-pbound, maxval=pbound, dtype=jnp.float32), 'out_proj_b': jax.random.uniform(ks[7], (HIDDEN,), minval=-pbound, maxval=pbound, dtype=jnp.float32), 'ln_gamma': jnp.ones((HIDDEN,), dtype=jnp.float32), 'ln_beta': jnp.zeros((HIDDEN,), dtype=jnp.float32)}
    _L1_gnn_all = _L1_gnn_setup()
    _L1_gnn_in = {k: v for k, v in _L1_gnn_all.items() if k in ('W_Q', 'W_K', 'W_V', 'attn_bias', 'out_proj_w', 'out_proj_b', 'ln_gamma', 'ln_beta')}
    del _L1_gnn_all
    return {'x': x, 'src': src, 'dst': dst, 'edge_type_5': edge_type_5, 'L0_gnn_Wq': _L0_gnn_in['Wq'], 'L0_gnn_Wk': _L0_gnn_in['Wk'], 'L0_gnn_Wv': _L0_gnn_in['Wv'], 'L0_gnn_Wo': _L0_gnn_in['Wo'], 'L0_gnn_bo': _L0_gnn_in['bo'], 'L0_gnn_ln1_g': _L0_gnn_in['ln1_g'], 'L0_gnn_ln1_b': _L0_gnn_in['ln1_b'], 'L0_gnn_W1': _L0_gnn_in['W1'], 'L0_gnn_b1': _L0_gnn_in['b1'], 'L0_gnn_W2': _L0_gnn_in['W2'], 'L0_gnn_b2': _L0_gnn_in['b2'], 'L0_gnn_ln2_g': _L0_gnn_in['ln2_g'], 'L0_gnn_ln2_b': _L0_gnn_in['ln2_b'], 'L1_gnn_W_Q': _L1_gnn_in['W_Q'], 'L1_gnn_W_K': _L1_gnn_in['W_K'], 'L1_gnn_W_V': _L1_gnn_in['W_V'], 'L1_gnn_attn_bias': _L1_gnn_in['attn_bias'], 'L1_gnn_out_proj_w': _L1_gnn_in['out_proj_w'], 'L1_gnn_out_proj_b': _L1_gnn_in['out_proj_b'], 'L1_gnn_ln_gamma': _L1_gnn_in['ln_gamma'], 'L1_gnn_ln_beta': _L1_gnn_in['ln_beta']}

def reference(x, src, dst, edge_type_5, L0_gnn_Wq, L0_gnn_Wk, L0_gnn_Wv, L0_gnn_Wo, L0_gnn_bo, L0_gnn_ln1_g, L0_gnn_ln1_b, L0_gnn_W1, L0_gnn_b1, L0_gnn_W2, L0_gnn_b2, L0_gnn_ln2_g, L0_gnn_ln2_b, L1_gnn_W_Q, L1_gnn_W_K, L1_gnn_W_V, L1_gnn_attn_bias, L1_gnn_out_proj_w, L1_gnn_out_proj_b, L1_gnn_ln_gamma, L1_gnn_ln_beta):
    import jax
    import jax.numpy as jnp

    def _L0_gnn_ref(h, src, dst, Wq, Wk, Wv, Wo, bo, ln1_g, ln1_b, W1, b1, W2, b2, ln2_g, ln2_b):
        import jax, jax.numpy as jnp
        import numpy as np
        N_NODES = 3125
        N_EDGES = 50000
        D = 128
        H = 8
        DH = D // H
        DFF = 2 * D
        EPS_LN = 1e-05

        def _ln(x, g, b):
            mu = jnp.mean(x, axis=-1, keepdims=True)
            var = jnp.var(x, axis=-1, keepdims=True)
            return (x - mu) * jax.lax.rsqrt(var + EPS_LN) * g + b
        n = h.shape[0]
        Q = (h @ Wq).reshape(n, H, DH)
        K = (h @ Wk).reshape(n, H, DH)
        V = (h @ Wv).reshape(n, H, DH)
        score = jnp.einsum('ehd,ehd->eh', K[src], Q[dst]) / np.sqrt(DH)
        score = jnp.exp(jnp.clip(score, -5.0, 5.0))
        m = V[src] * score[:, :, None]
        wV = jax.ops.segment_sum(m, dst, num_segments=n)
        z = jax.ops.segment_sum(score, dst, num_segments=n)
        h_attn = (wV / (z[:, :, None] + 1e-06)).reshape(n, D)
        x = h + (h_attn @ Wo + bo)
        x = _ln(x, ln1_g, ln1_b)
        y = jax.nn.relu(x @ W1 + b1) @ W2 + b2
        x = _ln(x + y, ln2_g, ln2_b)
        return x

    def _L1_gnn_ref(node_embeddings, edge_index, edge_types, W_Q, W_K, W_V, attn_bias, out_proj_w, out_proj_b, ln_gamma, ln_beta):
        import jax, jax.numpy as jnp
        import numpy as np
        N = 50000
        E = 20000
        HIDDEN = 128
        R = 5
        HEADS = 8
        HEAD_DIM = HIDDEN // HEADS
        LN_EPS = 1e-05

        def _fused_forward(node_embeddings, W_Q, W_K, W_V, attn_bias, out_proj_w, out_proj_b, ln_gamma, ln_beta, edge_index, edge_types):
            src, dst = (edge_index[0], edge_index[1])
            n = node_embeddings.shape[0]
            x_src = node_embeddings[src]
            x_dst = node_embeddings[dst]
            scale = HEAD_DIM ** 0.5
            NEG = jnp.float32(-1000000000.0)
            out = jnp.zeros((n, HEADS, HEAD_DIM), dtype=node_embeddings.dtype)
            for r in range(R):
                mask = edge_types == r
                q = jnp.einsum('eh,khd->ekd', x_dst, W_Q[r])
                k = jnp.einsum('eh,khd->ekd', x_src, W_K[r])
                v = jnp.einsum('eh,khd->ekd', x_src, W_V[r])
                logits = (q * k).sum(-1) / scale + attn_bias[r][None, :]
                masked_logits = jnp.where(mask[:, None], logits, NEG)
                max_v = jax.ops.segment_max(masked_logits, dst, num_segments=n)
                max_v = jnp.maximum(max_v, NEG)
                exp_l = jnp.where(mask[:, None], jnp.exp(masked_logits - max_v[dst]), 0.0)
                sum_exp = jax.ops.segment_sum(exp_l, dst, num_segments=n)
                attn = exp_l / (sum_exp[dst] + 1e-12)
                out = out + jax.ops.segment_sum(attn[:, :, None] * v, dst, num_segments=n)
            out = out.reshape(n, HIDDEN)
            out = out @ out_proj_w.T + out_proj_b
            h = out + node_embeddings
            mu = h.mean(-1, keepdims=True)
            var = ((h - mu) ** 2).mean(-1, keepdims=True)
            return (h - mu) / jnp.sqrt(var + LN_EPS) * ln_gamma + ln_beta
        return _fused_forward(node_embeddings, W_Q, W_K, W_V, attn_bias, out_proj_w, out_proj_b, ln_gamma, ln_beta, edge_index, edge_types)
    edge_index = jnp.stack([src, dst])
    h = jnp.maximum(_layernorm(x, axis=-1), 0.0)
    x = x + _L0_gnn_ref(h, src, dst, L0_gnn_Wq, L0_gnn_Wk, L0_gnn_Wv, L0_gnn_Wo, L0_gnn_bo, L0_gnn_ln1_g, L0_gnn_ln1_b, L0_gnn_W1, L0_gnn_b1, L0_gnn_W2, L0_gnn_b2, L0_gnn_ln2_g, L0_gnn_ln2_b)
    h = jnp.maximum(_layernorm(x, axis=-1), 0.0)
    x = x + _L1_gnn_ref(h, edge_index, edge_type_5, L1_gnn_W_Q, L1_gnn_W_K, L1_gnn_W_V, L1_gnn_attn_bias, L1_gnn_out_proj_w, L1_gnn_out_proj_b, L1_gnn_ln_gamma, L1_gnn_ln_beta)
    return x

_drawn_inputs = setup_inputs


def setup_inputs(seed=0):
    import zlib

    import numpy as np

    out = dict(_drawn_inputs(seed))
    spreads = {'L0_gnn_bo': (0.0, 0.1),
     'L0_gnn_ln1_g': (1.0, 0.2),
     'L0_gnn_ln1_b': (0.0, 0.1),
     'L0_gnn_b1': (0.0, 0.271),
     'L0_gnn_b2': (0.0, 0.1),
     'L0_gnn_ln2_g': (1.0, 0.2),
     'L0_gnn_ln2_b': (0.0, 0.1),
     'L1_gnn_attn_bias': (0.0, 0.8),
     'L1_gnn_ln_gamma': (1.0, 0.2),
     'L1_gnn_ln_beta': (0.0, 0.1)}
    factors = {'L1_gnn_out_proj_b': 3.054}
    for name, (base, spread) in spreads.items():
        noise = np.random.default_rng([zlib.crc32(name.encode()), seed]).standard_normal(out[name].shape)
        drawn = base * np.exp(spread * noise) if base else spread * noise
        out[name] = jnp.asarray(drawn.astype(out[name].dtype))
    for name, factor in factors.items():
        out[name] = (out[name] * factor).astype(out[name].dtype)
    return out
```

```python
from contextlib import ExitStack

import numpy as np

import concourse.bass as bass
from concourse import mybir

ALU = mybir.AluOpType
ACT = mybir.ActivationFunctionType
AX_X = mybir.AxisListType.X
PE = mybir.EngineType.PE
F32, BF16, F16, I32 = mybir.dt.float32, mybir.dt.bfloat16, mybir.dt.float16, mybir.dt.int32

P = 128
N = 3125
E = 100000
D = 128
H = 8
DH = D // H
R = 5
RH = R * H
DFF = 2 * D
NB = -(-N // P)
LAST = N - (NB - 1) * P
NPAD = NB * P
T = -(-E // P)
JT = -(-T // P)
TPAD = JT * P
G = 4
RING = 4
GP = G * P
TURN = G * RING
TURNS = -(-(T + NB - 1) // TURN)
STEPS = TURNS * RING
ITEMS = TURNS * TURN
BANK = 512
EPS = 1e-5
BIG = float(2.0 ** 100)
NEG = -1e9
PAD_DST = NPAD - 1
SPITCH = 64
KW = 4


def over_turns(eng, step):
    for s in range(RING):
        step(s, s, 0)
    with eng.Fori(1, TURNS) as turn:
        for s in range(RING):
            step(turn * RING + s, s, turn)


def over_blocks(eng, body):
    body(0, 0, True)
    body(1, 1, True)
    with eng.Fori(1, (NB - 1) // 2) as i:
        body(i * 2, 0, False)
        body(i * 2 + 1, 1, False)
    body(NB - 1, 0, False)


def over_blocks_unrolled(pe, body):
    for b in range(NB):
        body(b, b % 2, b < 2)


def there(n):
    return not isinstance(n, int) or n >= 0


def settle(eng, passed):
    eng.sem_inc(passed, 1)


def cols(start, size):
    return bass.ds(start, size)


def spread(ap, shape):
    return ap.broadcast_to(shape)


class Net:
    pass


def build(nc, a, out):
    with ExitStack() as ctx:
        net = Net()
        net.nc, net.a, net.out = nc, a, out

        def sb(name, shape, dt):
            return ctx.enter_context(nc.sbuf_tensor(name, shape, dt))

        net.psum = ctx.enter_context(nc.psum_tensor("psum", [P, 8 * BANK], F32))
        net.edges = nc.dram_tensor("edges", [TPAD, KW * P], I32).ap()
        net.local_rows = nc.dram_tensor("local_rows", [TPAD * P], F16).ap()
        net.key_rows = nc.dram_tensor("key_rows", [TPAD * P], F16).ap()
        net.start_rows = nc.dram_tensor("start_rows", [TPAD * P], BF16).ap()
        net.block_row = nc.dram_tensor("block_row", [TPAD], I32).ap()
        net.kv0 = nc.dram_tensor("kv0", [NPAD, 2 * D], F32).ap()
        net.kv1 = nc.dram_tensor("kv1", [NPAD * R, 2 * D], F32).ap()
        net.v_spill = nc.dram_tensor("v_spill", [STEPS, P, G, D], F32).ap()
        net.l_spill = nc.dram_tensor("l_spill", [STEPS, P, G * RH], F32).ap()
        net.m_spill = nc.dram_tensor("m_spill", [STEPS, RH, GP], F32).ap()

        net.ident = sb("ident", [P, P], F32)
        net.ones = sb("ones", [P, P], F32)
        net.lane = sb("lane", [P, P], F32)
        net.part = sb("part", [P, R], F32)
        net.part1 = sb("part1", [P, 1], F32)
        net.zeros = sb("zeros", [P, BANK], BF16)
        net.local = sb("local", [P, TPAD], F32)
        net.rel = sb("rel", [P, TPAD], F32)
        net.src0 = sb("src0", [P, TPAD], I32)
        net.src1 = sb("src1", [P, TPAD], I32)
        net.blocks = sb("blocks", [1, TPAD], I32)
        net.x = sb("x", [P, NB, D], F32)
        net.h = sb("h", [P, NB, D], F32)
        net.mv = sb("mv", [P, NB, 2], F32)
        net.tmp = sb("tmp", [P, 2, NB], F32)
        net.st = sb("st", [P, NB, 6], F32)
        net.rstd = sb("rstd", [P, NB], F32)
        net.shift = sb("shift", [P, NB], F32)

        constants(net)
        items(net)
        with nc.sbuf_tensor("q0", [P, NB * 3 * D], BF16) as q0:
            nodes0(net, q0)
            edges0(net, q0)
        with nc.sbuf_tensor("q1", [P, NB * 3 * R * D], BF16) as q1:
            nodes1(net, q1)
            logits1(net, q1)
        with nc.sbuf_tensor("probs", [P, ITEMS * RH], F32) as probs:
            with nc.sbuf_tensor("rsum", [P, NB * 3 * RH], BF16) as rsum:
                sums1(net, probs, rsum)
                values1(net, probs, rsum)
        nodes2(net)


def sems(ctx, nc, stage, *names):
    return [ctx.enter_context(nc.semaphore(f"{stage}_{x}")) for x in names]


def constants(net):
    nc = net.nc
    with ExitStack() as ctx:
        blank, rows = sems(ctx, nc, "c", "blank", "rows")
        block = ctx.enter_context(nc.Block())

        @block.gpsimd
        def _(pool):
            pool.memset(net.ident[:, :], 0.0).then_inc(blank, 1)
            pool.memset(net.ones[:, :], 1.0)
            pool.memset(net.zeros[:, :], 0.0)
            pool.wait_ge(blank, 1)
            pool.affine_select(out=net.ident[:, :], in_=net.ident[:, :], compare_op=ALU.not_equal, fill=1.0,
                               base=0, pattern=[[-1, P]], channel_multiplier=1)
            pool.iota(net.lane[:, :], [[1, P]], base=0, channel_multiplier=0,
                      allow_small_or_imprecise_dtypes=True)
            pool.iota(net.part[:, :], [[1, R]], base=0, channel_multiplier=R,
                      allow_small_or_imprecise_dtypes=True)
            pool.iota(net.part1[:, :], [[0, 1]], base=0, channel_multiplier=1,
                      allow_small_or_imprecise_dtypes=True)


def items(net):
    nc, a = net.nc, net.a
    full = (T - 1) // P
    rows = (E - full * P * P) // P
    rest = E - (full * P + rows) * P
    with ExitStack() as ctx:
        def sb(name, shape, dt):
            return ctx.enter_context(nc.sbuf_tensor(name, shape, dt))

        (padded, loaded, v_done, flagged, counted, spread_, located, gathered, rows_ready, stored,
         turned, copied, got_blocks, kept) = sems(
            ctx, nc, "i", "padded", "loaded", "vector_done", "flagged", "counted", "spread", "located",
            "gathered", "rows_ready", "stored", "turned", "copied", "got_blocks", "kept")
        raw = sb("raw", [P, JT, KW, P], I32)
        own = sb("own", [P, JT, KW, P], I32)
        w1 = sb("w1", [P, JT, P], F32)
        w2 = sb("w2", [P, JT, P], F32)
        w3 = sb("w3", [P, JT, P], F32)
        key = sb("key", [P, JT, P], F32)
        localf = sb("localf", [P, JT, P], F32)
        relf = sb("relf", [P, JT, P], F32)
        srcf = sb("srcf", [P, JT, P], F32)
        local16 = sb("local16", [P, JT, P], F16)
        key16 = sb("key16", [P, JT, P], F16)
        start16 = sb("start16", [P, JT, P], BF16)
        diag = sb("diag", [P, JT, P], F32)
        blk = sb("blk", [P, JT], I32)
        lastitem = sb("lastitem", [P, JT], F32)
        number = sb("number", [P, JT], F32)
        tile_of = sb("tile_of", [P, JT], F32)
        block_of = sb("block_of", [P, JT], F32)
        tile_i = sb("tile_i", [P, JT], I32)
        block_i = sb("block_i", [P, JT], I32)
        ps = net.psum
        block = ctx.enter_context(nc.Block())

        @block.gpsimd
        def _(pool):
            pool.memset(raw[:, full, 0, :], PAD_DST).then_inc(padded, 1)
            pool.memset(raw[:, full, 1:3, :], 0).then_inc(padded, 1)
            pool.memset(raw[:, full, 3, :], PAD_DST).then_inc(padded, 1)
            pool.memset(raw[0:1, 0, 3, 0:1], -1).then_inc(padded, 1)
            pool.iota(number[:, :], [[P, JT]], base=0, channel_multiplier=1,
                      allow_small_or_imprecise_dtypes=True).then_inc(padded, 1)
            pool.wait_ge(kept, 16)
            pool.wait_ge(located, 1)
            for j in range(JT):
                pool.indirect_dma_start(own[:, j, :, :].rearrange("p k e -> p (k e)"), None, net.edges,
                                        bass.IndirectOffsetOnAxis(ap=tile_i[:, j:j + 1], axis=0))\
                    .then_inc(gathered, 16)

        @block.sync
        def _(sp):
            sp.wait_ge(padded, 4)
            body = full * P * P
            for k, name in enumerate(("dst", "src", "edge_type_5")):
                v = a[name]
                sp.dma_start(raw[:, 0:full, k, :],
                             v[0:body].rearrange("(j p e) -> p j e", p=P, e=P)).then_inc(loaded, 16)
                sp.dma_start(raw[0:rows, full, k, :],
                             v[body:body + rows * P].rearrange("(p e) -> p e", e=P)).then_inc(loaded, 16)
                sp.dma_start(raw[rows:rows + 1, full, k, 0:rest],
                             v[E - rest:E].rearrange("(p e) -> p e", p=1)).then_inc(loaded, 16)
            v = a["dst"]
            sp.dma_start(raw[1:P, 0, 3, :],
                         v[P - 1:P * P - 1].rearrange("(p e) -> p e", e=P)).then_inc(loaded, 16)
            sp.dma_start(raw[0:1, 0, 3, 1:P],
                         v[0:P - 1].rearrange("(p e) -> p e", p=1)).then_inc(loaded, 16)
            sp.dma_start(raw[:, 1:full, 3, :],
                         v[P * P - 1:body - 1].rearrange("(j p e) -> p j e", p=P, e=P)).then_inc(loaded, 16)
            sp.dma_start(raw[0:rows, full, 3, :],
                         v[body - 1:body - 1 + rows * P].rearrange("(p e) -> p e", e=P)).then_inc(loaded, 16)
            sp.dma_start(raw[rows:rows + 1, full, 3, 0:rest + 1],
                         v[E - rest - 1:E].rearrange("(p e) -> p e", p=1)).then_inc(loaded, 16)
            sp.wait_ge(loaded, 16 * 14)
            sp.dma_start(net.edges.rearrange("(j p) c -> p j c", p=P),
                         raw[:, :, :, :].rearrange("p j k e -> p j (k e)")).then_inc(kept, 16)
            sp.wait_ge(located, 2)
            with nc.allow_non_contiguous_dma(reason="one word for each item"):
                sp.dma_start(net.block_row.rearrange("(j p) -> p j", p=P), block_i[:, :]).then_inc(stored, 16)
            sp.wait_ge(stored, 16)
            sp.dma_start(net.blocks[:, :], net.block_row.rearrange("(a n) -> a n", a=1)).then_inc(got_blocks, 16)
            for n, (rows_d, tile) in enumerate(((net.local_rows, local16), (net.key_rows, key16),
                                                (net.start_rows, start16))):
                sp.wait_ge(rows_ready, n + 1)
                sp.dma_start(rows_d.rearrange("(j p e) -> p j e", p=P, e=P), tile[:, :, :]).then_inc(stored, 16)
            sp.wait_ge(stored, 16 * 4)
            sp.wait_ge(got_blocks, 16)

        @block.vector
        def _(dve):
            done = [0]

            def chain(ins):
                done[0] += 1
                ins.then_inc(v_done, 1)
                dve.wait_ge(v_done, done[0])

            dve.wait_ge(loaded, 16 * 14)
            dve.wait_ge(padded, 5)
            chain(dve.tensor_scalar(blk[:, :], raw[:, :, 0, P - 1], 7, None, ALU.logical_shift_right))
            chain(dve.tensor_copy(lastitem[:, :], blk[:, :]))
            chain(dve.tensor_tensor(lastitem[:, :], lastitem[:, :], number[:, :], ALU.add))
            dve.tensor_tensor(diag[:, :, :], spread(net.ident[:, :].unsqueeze(1), [P, JT, P]),
                              spread(lastitem[:, :].unsqueeze(2), [P, JT, P]), ALU.mult).then_inc(counted, 1)
            dve.wait_ge(spread_, 1)
            for j in range(JT):
                chain(dve.tensor_scalar(w1[:, :, :].rearrange("p j e -> p (j e)"), ps[:, 0:TPAD],
                                        number[:, j:j + 1], None, ALU.is_lt))
                chain(dve.tensor_reduce(tile_of[:, j:j + 1], w1[:, :, :].rearrange("p j e -> p (j e)"),
                                        AX_X, ALU.add))
            dve.tensor_copy(tile_i[:, :], tile_of[:, :]).then_inc(located, 1)
            chain(dve.tensor_tensor(block_of[:, :], number[:, :], tile_of[:, :], ALU.subtract))
            dve.tensor_copy(block_i[:, :], block_of[:, :]).then_inc(located, 1)
            chain(dve.tensor_scalar(block_of[:, :], block_of[:, :], -float(P), None, ALU.mult))
            dve.wait_ge(gathered, 16 * JT)
            chain(dve.tensor_copy(w1[:, :, :], own[:, :, 0, :]))
            chain(dve.tensor_tensor(localf[:, :, :], w1[:, :, :],
                                    spread(block_of[:, :].unsqueeze(2), [P, JT, P]), ALU.add))
            dve.tensor_copy(local16[:, :, :], localf[:, :, :]).then_inc(rows_ready, 1)
            chain(dve.tensor_copy(w2[:, :, :], own[:, :, 2, :]))
            chain(dve.scalar_tensor_tensor(out=w3[:, :, :], in0=localf[:, :, :], scalar=float(R), in1=w2[:, :, :],
                                           op0=ALU.mult, op1=ALU.add))
            dve.tensor_copy(key16[:, :, :], w3[:, :, :]).then_inc(rows_ready, 1)
            chain(dve.tensor_copy(srcf[:, :, :], own[:, :, 3, :]))
            chain(dve.tensor_tensor(key[:, :, :], w1[:, :, :], srcf[:, :, :], ALU.is_equal))
            dve.tensor_scalar(start16[:, :, :], key[:, :, :], -1.0, BIG, ALU.add, ALU.mult).then_inc(rows_ready, 1)
            chain(dve.tensor_scalar(w1[:, :, :], localf[:, :, :], 0.0, 16.0, ALU.is_lt, ALU.mult))
            chain(dve.tensor_tensor(w1[:, :, :], w1[:, :, :], w2[:, :, :], ALU.add))
            chain(dve.tensor_scalar(w3[:, :, :], localf[:, :, :], float(P - 1), 16.0, ALU.is_gt, ALU.mult))
            chain(dve.tensor_tensor(relf[:, :, :], w1[:, :, :], w3[:, :, :], ALU.add))
            chain(dve.tensor_copy(srcf[:, :, :], own[:, :, 1, :]))
            dve.scalar_tensor_tensor(out=key[:, :, :], in0=srcf[:, :, :], scalar=float(R), in1=w2[:, :, :],
                                     op0=ALU.mult, op1=ALU.add).then_inc(counted, 1)
            for n, out in enumerate((net.local, net.rel, net.src0, net.src1)):
                base = (n % 2) * 2 * BANK
                dve.wait_ge(turned, n + 1)
                dve.tensor_copy(out[:, :], ps[:, base:base + TPAD]).then_inc(copied, 1)

        @block.tensor
        def _(pe):
            pe.wait_ge(counted, 1)
            for j in range(JT):
                last = pe.matmul(ps[:, j * P:(j + 1) * P], net.ones[:, :], diag[:, j, :], start=True, stop=True)
            last.then_inc(spread_, 1)
            pe.wait_ge(counted, 2)
            for n, tile in enumerate((localf, relf, srcf, key)):
                if n >= 2:
                    pe.wait_ge(copied, n - 1)
                for j in range(JT):
                    base = (n % 2) * 2 * BANK + j * P
                    last = pe.transpose(ps[:, base:base + P], tile[:, j, :], net.ident[:, :])
                last.then_inc(turned, 1)


def layer_norm_stats(dve, net, src, stats, aggr, turn):
    over_blocks(dve, lambda b, k, first: dve.bn_stats(block_of(net.st, b), block_of(src, b)).then_inc(stats, 1))
    dve.wait_ge(stats, NB * turn)
    st, mv, tmp = net.st, net.mv, net.tmp
    mean, var, half, both = mv[:, :, 0], mv[:, :, 1], tmp[:, 0, :], tmp[:, 1, :]
    steps = (
        lambda: dve.tensor_tensor(mean, st[:, :, 1], st[:, :, 4], ALU.add),
        lambda: dve.tensor_tensor(half, st[:, :, 1], st[:, :, 4], ALU.subtract),
        lambda: dve.tensor_tensor(both, st[:, :, 2], st[:, :, 5], ALU.add),
        lambda: dve.tensor_scalar(mean, mean, 0.5, None, ALU.mult),
        lambda: dve.tensor_tensor(half, half, half, ALU.mult),
        lambda: dve.tensor_scalar(both, both, 1.0 / D, None, ALU.mult),
        lambda: dve.scalar_tensor_tensor(out=var, in0=half, scalar=0.25, in1=both, op0=ALU.mult, op1=ALU.add),
    )
    for n, step in enumerate(steps):
        if n >= 3:
            dve.wait_ge(aggr, len(steps) * (turn - 1) + n - (0 if n == 6 else 2))
        step().then_inc(aggr, 1)


AGGR = 7


def layer_norm_scale(dve, net, std_ready, scale_ready, turn):
    dve.wait_ge(std_ready, turn)
    dve.reciprocal(net.rstd[:, :], net.rstd[:, :]).then_inc(scale_ready, 1)
    dve.wait_ge(scale_ready, 2 * turn - 1)
    dve.scalar_tensor_tensor(out=net.shift[:, :], in0=net.mv[:, :, 0], scalar=-1.0, in1=net.rstd[:, :],
                             op0=ALU.mult, op1=ALU.mult).then_inc(scale_ready, 1)


def layer_norm_std(act, net, eps, aggr, std_ready, turn):
    act.wait_ge(aggr, AGGR * turn)
    act.activation(net.rstd[:, :], net.mv[:, :, 1], ACT.Sqrt, bias=eps[:, 0:1], scale=1.0).then_inc(std_ready, 1)


def normalize(act, net, dst, src, func, scale_ready, turn, normed):
    act.wait_ge(scale_ready, 2 * turn)
    over_blocks(act, lambda b, k, first: act.activation(
        dst[:, cols(b, 1), :].rearrange("p b d -> p (b d)"), src[:, cols(b, 1), :].rearrange("p b d -> p (b d)"),
        func, bias=net.shift[:, cols(b, 1)], scale=net.rstd[:, cols(b, 1)]).then_inc(normed, 1))


def block_of(tile, b):
    return tile[:, cols(b, 1), :].rearrange("p b d -> p (b d)")


def split3(dve, hi, mid, lo, src, rest, ready, base):
    dve.tensor_copy(hi, src).then_inc(ready, 1)
    dve.wait_ge(ready, base + 1)
    dve.tensor_tensor(rest, src, hi, ALU.subtract).then_inc(ready, 1)
    dve.wait_ge(ready, base + 2)
    dve.tensor_copy(mid, rest).then_inc(ready, 1)
    dve.wait_ge(ready, base + 3)
    dve.tensor_tensor(lo, rest, mid, ALU.subtract).then_inc(ready, 1)


def nodes0(net, q0):
    nc, a = net.nc, net.a
    with ExitStack() as ctx:
        def sb(name, shape, dt):
            return ctx.enter_context(nc.sbuf_tensor(name, shape, dt))

        (blank, x_loaded, w_loaded, stats, aggr, std_ready, scale_ready, normed, turned, copied, product,
         evacuated, parts, store0, store1) = sems(
            ctx, nc, "n0", "blank", "x_loaded", "w_loaded", "stats", "aggr", "std_ready", "scale_ready", "normed",
            "turned", "copied", "product", "evacuated", "parts", "store0", "store1")
        w = sb("w_qkv0", [P, 3 * D], F32)
        eps = sb("eps", [P, 1], F32)
        ht = sb("ht", [P, 2, P], F32)
        qkv = sb("qkv", [P, 2, 3 * D], F32)
        rest = sb("rest", [P, D], F32)
        stores = (store0, store1)
        ps = net.psum
        block = ctx.enter_context(nc.Block())

        @block.gpsimd
        def _(pool):
            pool.memset(net.x[:, NB - 1, :], 0.0).then_inc(blank, 1)
            pool.memset(eps[:, :], EPS).then_inc(blank, 1)

        @block.sync
        def _(sp):
            x = a["x"]
            for b in range(0, NB - 1, 8):
                sp.dma_start(net.x[:, b:b + 8, :], x[b * P:(b + 8) * P, :].rearrange("(b p) d -> p b d", p=P))\
                    .then_inc(x_loaded, 16)
            sp.wait_ge(blank, 1)
            sp.dma_start(net.x[0:LAST, NB - 1, :], x[(NB - 1) * P:N, :]).then_inc(x_loaded, 16)
            for j, name in enumerate(("L0_gnn_Wq", "L0_gnn_Wk", "L0_gnn_Wv")):
                sp.dma_start(w[:, j * D:(j + 1) * D], a[name]).then_inc(w_loaded, 16)

            def store(b, k, first):
                sp.wait_ge(evacuated, b + 1)
                sp.dma_start(net.kv0[cols(b * P, P), :], qkv[:, k, D:3 * D]).then_inc(stores[k], 16)

            over_blocks(sp, store)
            sp.wait_ge(store0, 16 * ((NB + 1) // 2))
            sp.wait_ge(store1, 16 * (NB // 2))

        @block.vector
        def _(dve):
            dve.wait_ge(x_loaded, 64)
            layer_norm_stats(dve, net, net.x, stats, aggr, 1)
            layer_norm_scale(dve, net, std_ready, scale_ready, 1)

            def split(b, k, first):
                dve.wait_ge(evacuated, b + 1)
                part = [q0[:, cols(b * (3 * D) + s * D, D)] for s in range(3)]
                split3(dve, *part, qkv[:, k, 0:D], rest[:, :], parts, b * 4)

            over_blocks(dve, split)

        @block.scalar
        def _(act):
            act.wait_ge(blank, 2)
            layer_norm_std(act, net, eps, aggr, std_ready, 1)
            normalize(act, net, net.h, net.x, ACT.Relu, scale_ready, 1, normed)

            def evacuate(b, k, first):
                act.wait_ge(turned, b + 1)
                act.copy(ht[:, k, :], ps[:, k * BANK:k * BANK + P]).then_inc(copied, 1)
                act.wait_ge(product, b + 1)
                if not first:
                    act.wait_ge(parts, (b - 1) * 4)
                    act.wait_ge(stores[k], (b - k) * 8)
                act.copy(qkv[:, k, :], ps[:, (2 + k) * BANK:(2 + k) * BANK + 3 * D]).then_inc(evacuated, 1)

            over_blocks(act, evacuate)

        @block.tensor
        def _(pe):
            pe.wait_ge(w_loaded, 48)

            def project(b, k, first):
                pe.wait_ge(normed, b + 1)
                if not first:
                    pe.wait_ge(copied, b - 1)
                pe.transpose(ps[:, k * BANK:k * BANK + P], block_of(net.h, b), net.ident[:, :]).then_inc(turned, 1)
                pe.wait_ge(copied, b + 1)
                if not first:
                    pe.wait_ge(evacuated, b - 1)
                pe.matmul(ps[:, (2 + k) * BANK:(2 + k) * BANK + 3 * D], ht[:, k, :], w[:, :],
                          start=True, stop=True).then_inc(product, 1)

            over_blocks_unrolled(pe, project)


def clear_banks(pe, net, n):
    for k in range(n):
        last = pe.matmul(net.psum[:, k * BANK:(k + 1) * BANK], net.zeros[:, 0:P], net.zeros[:, :],
                         start=True, stop=False, skip_group_check=True)
    return last


class Registers:

    def __init__(self, nc, pe, net):
        self.nc, self.pe, self.net = nc, pe, net

    def load(self, n):
        _, v = self.nc.values_load_multi_w_load_instructions(
            self.net.blocks[0:1, cols(n * G, G)], engines=[PE], min_val=0, max_val=NB - 1,
            skip_runtime_bounds_check_because="blocks of items are below NB")
        return v


def edges0(net, q0):
    nc = net.nc
    Z = NB * D
    with ExitStack() as ctx:
        def sb(name, shape, dt):
            return ctx.enter_context(nc.sbuf_tensor(name, shape, dt))

        (passed_pool, idx_ready, onehot_t, onehot, queries, prod_ready, score_ready, clipped, exp_ready, msg_ready, added,
         ) = sems(ctx, nc, "m0", "passed_pool", "idx_ready", "onehot_t", "onehot", "queries", "prod_ready", "score_ready",
                  "clipped", "exp_ready", "msg_ready", "added")
        gathered = sems(ctx, nc, "m0", *[f"gathered{s}" for s in range(RING)])
        rows_loaded = sems(ctx, nc, "m0", *[f"rows_loaded{s}" for s in range(RING)])
        kv = sb("kv", [P, RING, G, 2 * D], F32)
        idx = sb("idx", [P, RING, G], I32)
        rows = sb("rows", [P, RING, GP], F16)
        oht = sb("oht", [P, 2, GP], BF16)
        oh = sb("oh", [P, RING, G, P], F32)
        prod = sb("prod", [P, 2, GP], F32)
        score = sb("score", [P, 2, G * H], F32)
        clip = sb("clip", [P, 2, G * H], F32)
        msg = sb("msg", [P, RING, G, D + H], F32)
        qe = net.psum[:, 7 * BANK:8 * BANK]
        block = ctx.enter_context(nc.Block())

        @block.gpsimd
        def _(pool):
            def gather(n, s, turn):
                pool.wait_ge(idx_ready, n + 1)
                if there(n - RING):
                    pool.wait_ge(msg_ready, n - (RING - 1))
                settle(pool, passed_pool)
                for i in range(G):
                    pool.indirect_dma_start(kv[:, s, i, :], None, net.kv0,
                                            bass.IndirectOffsetOnAxis(ap=idx[:, s, i:i + 1], axis=0))\
                        .then_inc(gathered[s], 16)

            over_turns(pool, gather)

        @block.sync
        def _(sp):
            def load(n, s, turn):
                if there(n - RING):
                    sp.wait_ge(onehot_t, n - (RING - 1))
                sp.dma_start(rows[:, s, :], net.local_rows[cols(n * GP, GP)].partition_broadcast(P))\
                    .then_inc(rows_loaded[s], 16)

            over_turns(sp, load)

        @block.scalar
        def _(act):
            for s in range(RING):
                act.copy(idx[:, s, :], net.src0[:, s * G:(s + 1) * G]).then_inc(idx_ready, 1)

            def exps(m, s):
                act.wait_ge(clipped, m + 1)
                act.activation(msg[:, s, :, D:D + H], clip[:, s % 2, :].rearrange("p (g h) -> p g h", h=H),
                               ACT.Exp, scale=1.0 / 4).then_inc(exp_ready, 1)

            def step(n, s, turn):
                act.wait_ge(gathered[s], (turn + 1) * (16 * G))
                act.copy(idx[:, s, :], net.src0[:, cols(n * G + TURN, G)]).then_inc(idx_ready, 1)
                if there(n - 1):
                    exps(n - 1, (s - 1) % RING)

            over_turns(act, step)
            exps(STEPS - 1, RING - 1)

        @block.vector
        def _(dve):
            def onehots(n, s, turn):
                dve.wait_ge(rows_loaded[s], (turn + 1) * 16)
                if there(n - 2):
                    dve.wait_ge(queries, n - 1)
                dve.tensor_scalar(oht[:, s % 2, :], rows[:, s, :], net.part1[:, 0:1], None, ALU.is_equal)\
                    .then_inc(onehot_t, 1)
                if there(n - RING):
                    dve.wait_ge(added, n - (RING - 1))
                dve.tensor_tensor(oh[:, s, :, :], spread(net.lane[:, :].unsqueeze(1), [P, G, P]),
                                  spread(net.local[:, cols(n * G, G)].unsqueeze(2), [P, G, P]), ALU.is_equal)\
                    .then_inc(onehot, 1)

            def scores(m, s, turn):
                dve.wait_ge(queries, m + 1)
                dve.wait_ge(gathered[s], turn)
                dve.tensor_tensor(prod[:, s % 2, :].rearrange("p (g d) -> p g d", d=D), kv[:, s, :, 0:D],
                                  qe.rearrange("p (g d) -> p g d", d=D), ALU.mult).then_inc(prod_ready, 1)
                dve.wait_ge(prod_ready, m + 1)
                dve.tensor_reduce(score[:, s % 2, :], prod[:, s % 2, :].rearrange("p (g d) -> p g d", d=DH),
                                  AX_X, ALU.add).then_inc(score_ready, 1)
                dve.wait_ge(score_ready, m + 1)
                dve.tensor_scalar(clip[:, s % 2, :], score[:, s % 2, :], -5.0 * 4, 5.0 * 4, ALU.max, ALU.min)\
                    .then_inc(clipped, 1)

            def messages(m, s):
                dve.wait_ge(exp_ready, m + 1)
                dve.tensor_tensor(msg[:, s, :, 0:D].rearrange("p g (h d) -> p g h d", d=DH),
                                  kv[:, s, :, D:2 * D].rearrange("p g (h d) -> p g h d", d=DH),
                                  spread(msg[:, s, :, D:D + H].unsqueeze(3), [P, G, H, DH]), ALU.mult)\
                    .then_inc(msg_ready, 1)

            def step(n, s, turn):
                onehots(n, s, turn)
                if there(n - 1):
                    scores(n - 1, (s - 1) % RING, (turn + 1 if s else turn) * (16 * G))
                if there(n - 2):
                    messages(n - 2, (s - 2) % RING)

            over_turns(dve, step)
            scores(STEPS - 1, RING - 1, TURNS * 16 * G)
            messages(STEPS - 2, RING - 2)
            messages(STEPS - 1, RING - 1)

        @block.tensor
        def _(pe):
            clear_banks(pe, net, 7)
            registers = Registers(nc, pe, net)

            def expand(n, s):
                blocks = registers.load(n)
                pe.wait_ge(onehot_t, n + 1)
                if there(n - 1):
                    pe.wait_ge(prod_ready, n)
                for i in range(G):
                    for part in range(3):
                        last = pe.matmul(qe[:, i * D:(i + 1) * D], oht[:, s % 2, i * P:(i + 1) * P],
                                         q0[:, cols(blocks[i] * (3 * D) + part * D, D)],
                                         start=(part == 0), stop=(part == 2))
                last.then_inc(queries, 1)

            def add(m, s):
                blocks = registers.load(m)
                pe.wait_ge(onehot, m + 1)
                pe.wait_ge(msg_ready, m + 1)
                for i in range(G):
                    pe.matmul(net.psum[:, cols(blocks[i] * D, D)], oh[:, s, i, :], msg[:, s, i, 0:D],
                              start=False, stop=False, skip_group_check=True)
                    last = pe.matmul(net.psum[:, cols(blocks[i] * H + Z, H)], oh[:, s, i, :], msg[:, s, i, D:D + H],
                                     start=False, stop=False, skip_group_check=True)
                last.then_inc(added, 1)

            def step(n, s, turn):
                expand(n, s)
                if there(n - 2):
                    add(n - 2, (s - 2) % RING)

            over_turns(pe, step)
            add(STEPS - 2, RING - 2)
            add(STEPS - 1, RING - 1)


def nodes1(net, q1):
    nc, a = net.nc, net.a
    Z = NB * D
    with ExitStack() as ctx:
        def sb(name, shape, dt):
            return ctx.enter_context(nc.sbuf_tensor(name, shape, dt))

        (w_loaded, r_loaded, v_done, turned, copied, product, taken, stats, aggr, std_ready, scale_ready, normed,
         ready, hidden, relued, evacuated, parts, store0, store1, blank) = sems(
            ctx, nc, "n1", "w_loaded", "r_loaded", "vector_done", "turned", "copied", "product", "taken", "stats",
            "aggr", "std_ready", "scale_ready", "normed", "ready", "hidden", "relued", "evacuated", "parts",
            "store0", "store1", "blank")
        banked = ctx.enter_context(nc.semaphore("n1_banked"))
        wo = sb("wo", [P, D], F32)
        w1 = sb("w1_", [P, DFF], F32)
        w2 = sb("w2_", [P, 2, D], F32)
        wr = sb("wr", [P, R, 3, D], F32)
        b1 = sb("b1", [P, 2], F32)
        names = ("L0_gnn_bo", "L0_gnn_ln1_g", "L0_gnn_ln1_b", "L0_gnn_b2", "L0_gnn_ln2_g", "L0_gnn_ln2_b")
        vec = sb("vec", [P, len(names), D], F32)
        eps = sb("eps1", [P, 1], F32)
        t1 = sb("t1", [P, NB, D], F32)
        at = sb("at", [P, 2, P], F32)
        f1 = sb("f1", [P, 2, 2, P], F32)
        zr = sb("zr", [P, NB * H], F32)
        qkv = sb("qkv1", [P, 2, R, 3 * D], F32)
        rest = sb("rest1", [P, R * D], F32)
        stores = (store0, store1)
        ps = net.psum
        ALL = [P, NB, D]

        def row(j):
            return spread(vec[:, j, :].unsqueeze(1), ALL)

        block = ctx.enter_context(nc.Block())

        @block.sync
        def _(sp):
            sp.dma_start(wo[:, :], a["L0_gnn_Wo"]).then_inc(w_loaded, 16)
            sp.dma_start(w1[:, :], a["L0_gnn_W1"]).then_inc(w_loaded, 16)
            sp.dma_start(w2[:, :, :], a["L0_gnn_W2"].rearrange("(c p) d -> p c d", p=P)).then_inc(w_loaded, 16)
            with nc.allow_non_contiguous_dma(reason="a short column"):
                sp.dma_start(b1[:, :], a["L0_gnn_b1"].rearrange("(c p) -> p c", p=P)).then_inc(w_loaded, 16)
            for j, name in enumerate(names):
                sp.dma_start(vec[:, j, :], a[name].partition_broadcast(P)).then_inc(w_loaded, 16)
            for j, name in enumerate(("L1_gnn_W_Q", "L1_gnn_W_K", "L1_gnn_W_V")):
                for r in range(R):
                    sp.dma_start(wr[:, r, j, :].rearrange("p (h d) -> p h d", d=DH),
                                 a[name][r].rearrange("h p d -> p h d")).then_inc(r_loaded, 16)

            def store(b, k, first):
                sp.wait_ge(evacuated, (b + 1) * R)
                sp.dma_start(net.kv1[cols(b * (P * R), P * R), :].rearrange("(p r) c -> p r c", r=R),
                             qkv[:, k, :, D:3 * D]).then_inc(stores[k], 16)

            over_blocks(sp, store)
            sp.wait_ge(store0, 16 * ((NB + 1) // 2))
            sp.wait_ge(store1, 16 * (NB // 2))

        @block.gpsimd
        def _(pool):
            pool.memset(eps[:, :], EPS).then_inc(blank, 1)

        @block.vector
        def _(dve):
            done = [0]

            def chain(ins):
                done[0] += 1
                ins.then_inc(v_done, 1)
                dve.wait_ge(v_done, done[0])

            def signal(ins, n):
                ins.then_inc(ready, 1)
                dve.wait_ge(ready, n)

            chain(dve.tensor_scalar(zr[:, :], ps[:, Z:Z + NB * H], 1e-6, None, ALU.add))
            chain(dve.reciprocal(zr[:, :], zr[:, :]))
            dve.tensor_tensor(t1[:, :, :].rearrange("p b (h d) -> p (b h) d", d=DH),
                              ps[:, 0:NB * D].rearrange("p (n d) -> p n d", d=DH),
                              spread(zr[:, :].unsqueeze(2), [P, NB * H, DH]), ALU.mult).then_inc(ready, 1)
            dve.wait_ge(w_loaded, 16 * (4 + len(names)))
            chain(dve.tensor_tensor(net.h[:, :, :], net.h[:, :, :], row(0), ALU.add))

            def take(b, k, first):
                dve.wait_ge(product, b + 1)
                dve.tensor_tensor(block_of(net.h, b), ps[:, (2 + k) * BANK:(2 + k) * BANK + D],
                                  block_of(net.h, b), ALU.add).then_inc(taken, 1)

            over_blocks(dve, take)
            dve.wait_ge(taken, NB)
            layer_norm_stats(dve, net, net.h, stats, aggr, 1)
            layer_norm_scale(dve, net, std_ready, scale_ready, 1)
            dve.wait_ge(normed, NB)
            chain(dve.tensor_tensor(t1[:, :, :], t1[:, :, :], row(1), ALU.mult))
            signal(dve.tensor_tensor(t1[:, :, :], t1[:, :, :], row(2), ALU.add), 2)
            chain(dve.tensor_tensor(net.h[:, :, :], t1[:, :, :], row(3), ALU.add))

            def take2(b, k, first):
                dve.wait_ge(product, b + (NB + 1))
                dve.tensor_tensor(block_of(net.h, b), ps[:, (6 + k) * BANK:(6 + k) * BANK + D],
                                  block_of(net.h, b), ALU.add).then_inc(taken, 1)

            over_blocks(dve, take2)
            dve.wait_ge(taken, 2 * NB)
            layer_norm_stats(dve, net, net.h, stats, aggr, 2)
            layer_norm_scale(dve, net, std_ready, scale_ready, 2)
            dve.wait_ge(normed, 2 * NB)
            chain(dve.tensor_tensor(t1[:, :, :], t1[:, :, :], row(4), ALU.mult))
            chain(dve.tensor_tensor(t1[:, :, :], t1[:, :, :], row(5), ALU.add))
            signal(dve.tensor_tensor(net.x[:, :, :], t1[:, :, :], net.x[:, :, :], ALU.add), 3)
            layer_norm_stats(dve, net, net.x, stats, aggr, 3)
            layer_norm_scale(dve, net, std_ready, scale_ready, 3)

            def split(b, k, first):
                dve.wait_ge(evacuated, (b + 1) * R)
                part = [q1[:, cols(b * (3 * R * D) + s * (R * D), R * D)].rearrange("p (r d) -> p r d", d=D)
                        for s in range(3)]
                split3(dve, *part, qkv[:, k, :, 0:D], rest[:, :].rearrange("p (r d) -> p r d", d=D), parts, b * 4)

            over_blocks(dve, split)

        @block.scalar
        def _(act):
            act.wait_ge(blank, 1)

            def copy(b, k, first):
                act.wait_ge(turned, b + 1)
                act.copy(at[:, k, :], ps[:, k * BANK:k * BANK + P]).then_inc(copied, 1)

            over_blocks(act, copy)
            layer_norm_std(act, net, eps, aggr, std_ready, 1)
            normalize(act, net, t1, net.h, ACT.Identity, scale_ready, 1, normed)

            def ff(b, k, first, do=(True, True)):
                if do[0]:
                    act.wait_ge(turned, b + (NB + 1))
                    act.copy(at[:, k, :], ps[:, k * BANK:k * BANK + P]).then_inc(copied, 1)
                if do[1] and there(b - 1):
                    j = 1 - k
                    act.wait_ge(hidden, b)
                    for c in range(2):
                        act.activation(f1[:, j, c, :], ps[:, (4 + j) * BANK + c * P:(4 + j) * BANK + (c + 1) * P],
                                       ACT.Relu, bias=b1[:, c:c + 1], scale=1.0).then_inc(relued, 1)

            over_blocks(act, ff)
            ff(NB, 1, False, (False, True))
            layer_norm_std(act, net, eps, aggr, std_ready, 2)
            normalize(act, net, t1, net.h, ACT.Identity, scale_ready, 2, normed)
            layer_norm_std(act, net, eps, aggr, std_ready, 3)
            normalize(act, net, net.h, net.x, ACT.Relu, scale_ready, 3, normed)

            def evacuate(b, k, first):
                act.wait_ge(turned, b + (2 * NB + 1))
                act.copy(at[:, k, :], ps[:, k * BANK:k * BANK + P]).then_inc(copied, 1)
                if not first:
                    act.wait_ge(parts, (b - 1) * 4)
                    act.wait_ge(stores[k], (b - k) * 8)
                for r in range(R):
                    act.wait_ge(banked, b * R + (r + 1))
                    act.copy(qkv[:, k, r, :], ps[:, (2 + r) * BANK:(2 + r) * BANK + 3 * D]).then_inc(evacuated, 1)

            over_blocks(act, evacuate)

        @block.tensor
        def _(pe):
            pe.wait_ge(ready, 1)
            pe.wait_ge(w_loaded, 16 * (4 + len(names)))

            def out_proj(b, k, first):
                if not first:
                    pe.wait_ge(copied, b - 1)
                pe.transpose(ps[:, k * BANK:k * BANK + P], block_of(t1, b), net.ident[:, :]).then_inc(turned, 1)
                pe.wait_ge(copied, b + 1)
                if not first:
                    pe.wait_ge(taken, b - 1)
                pe.matmul(ps[:, (2 + k) * BANK:(2 + k) * BANK + D], at[:, k, :], wo[:, :], start=True, stop=True)\
                    .then_inc(product, 1)

            over_blocks_unrolled(pe, out_proj)
            pe.wait_ge(ready, 2)

            def ff(b, k, first, do=(True, True, True)):
                j = 1 - k
                if do[0]:
                    if not first:
                        pe.wait_ge(copied, b + (NB - 1))
                    pe.transpose(ps[:, k * BANK:k * BANK + P], block_of(t1, b), net.ident[:, :])\
                        .then_inc(turned, 1)
                if do[1] and there(b - 1):
                    pe.wait_ge(copied, b + NB)
                    if there(b - 3):
                        pe.wait_ge(relued, (b - 2) * 2)
                    for c in range(2):
                        last = pe.matmul(ps[:, (4 + j) * BANK + c * P:(4 + j) * BANK + (c + 1) * P],
                                         w1[:, c * P:(c + 1) * P], at[:, j, :], start=True, stop=True)
                    last.then_inc(hidden, 1)
                if do[2] and there(b - 2):
                    pe.wait_ge(relued, (b - 1) * 2)
                    if there(b - 4):
                        pe.wait_ge(taken, b + (NB - 3))
                    for c in range(2):
                        last = pe.matmul(ps[:, (6 + k) * BANK:(6 + k) * BANK + D], f1[:, k, c, :], w2[:, c, :],
                                         start=(c == 0), stop=(c == 1))
                    last.then_inc(product, 1)

            over_blocks_unrolled(pe, ff)
            ff(NB, 1, False, (False, True, True))
            ff(NB + 1, 0, False, (False, False, True))
            pe.wait_ge(r_loaded, 16 * 3 * R)
            pe.wait_ge(taken, 2 * NB)

            def project(b, k, first):
                pe.wait_ge(normed, b + (2 * NB + 1))
                if not first:
                    pe.wait_ge(copied, b + (2 * NB - 1))
                pe.transpose(ps[:, k * BANK:k * BANK + P], block_of(net.h, b), net.ident[:, :]).then_inc(turned, 1)
                pe.wait_ge(copied, b + (2 * NB + 1))
                for r in range(R):
                    if there(b - 1):
                        pe.wait_ge(evacuated, b * R + (r + 1 - R))
                    pe.matmul(ps[:, (2 + r) * BANK:(2 + r) * BANK + 3 * D], at[:, k, :],
                              wr[:, r, :, :].rearrange("p a d -> p (a d)"), start=True, stop=True)\
                        .then_inc(banked, 1)

            over_blocks_unrolled(pe, project)


def logits1(net, q1):
    nc, a = net.nc, net.a
    with ExitStack() as ctx:
        def sb(name, shape, dt):
            return ctx.enter_context(nc.sbuf_tensor(name, shape, dt))

        (passed_pool, passed_pe, idx_ready, onehot_t, queries, prod_ready, score_ready, mask_ready, bias_ready, logit_ready, turned,
         scanned, b_loaded, blank) = sems(
            ctx, nc, "m1", "passed_pool", "passed_pe", "idx_ready", "onehot_t", "queries", "prod_ready", "score_ready", "mask_ready",
            "bias_ready", "logit_ready", "turned", "scanned", "b_loaded", "blank")
        gathered = sems(ctx, nc, "m1", *[f"gathered{s}" for s in range(RING)])
        rows_loaded = sems(ctx, nc, "m1", *[f"rows_loaded{s}" for s in range(RING)])
        starts_loaded = sems(ctx, nc, "m1", *[f"starts_loaded{s}" for s in range(RING)])
        v_stored = sems(ctx, nc, "m1", *[f"v_stored{s}" for s in range(RING)])
        l_stored = sems(ctx, nc, "m1", *[f"l_stored{s}" for s in range(RING)])
        m_stored = sems(ctx, nc, "m1", *[f"m_stored{s}" for s in range(RING)])
        kv = sb("kv_", [P, RING, G, 2 * D], F32)
        idx = sb("idx_", [P, RING, G], I32)
        rows = sb("rows_", [P, RING, GP], F16)
        starts = sb("starts", [RH, RING, GP], BF16)
        oht = sb("oht_", [P, 2, R, GP], BF16)
        prod = sb("prod_", [P, 2, GP], F32)
        score = sb("score_", [P, 2, G * H], F32)
        mask = sb("mask", [P, 2, G * R], F32)
        bias = sb("bias", [P, RH], F32)
        shifted = sb("shifted", [P, 2, G, RH], F32)
        logit = sb("logit", [P, RING, G, RH], F32)
        top = sb("top", [RH, RING, GP], F32)
        low = sb("low", [P, 1], F32)
        ps = net.psum
        block = ctx.enter_context(nc.Block())

        @block.gpsimd
        def _(pool):
            pool.memset(low[:, :], -BIG).then_inc(blank, 1)

            def gather(n, s, turn):
                pool.wait_ge(idx_ready, n + 1)
                if there(n - RING):
                    pool.wait_ge(prod_ready, n - (RING - 1))
                    pool.wait_ge(v_stored[s], turn * 16)
                settle(pool, passed_pool)
                for i in range(G):
                    pool.indirect_dma_start(kv[:, s, i, :], None, net.kv1,
                                            bass.IndirectOffsetOnAxis(ap=idx[:, s, i:i + 1], axis=0))\
                        .then_inc(gathered[s], 16)

            over_turns(pool, gather)

        @block.sync
        def _(sp):
            sp.dma_start(bias[:, :], a["L1_gnn_attn_bias"].rearrange("r h -> (r h)").partition_broadcast(P))\
                .then_inc(b_loaded, 16)

            def load(n, s, turn):
                if there(n - RING):
                    sp.wait_ge(onehot_t, n - (RING - 1))
                sp.dma_start(rows[:, s, :], net.key_rows[cols(n * GP, GP)].partition_broadcast(P))\
                    .then_inc(rows_loaded[s], 16)
                if there(n - RING):
                    sp.wait_ge(scanned, n - (RING - 1))
                sp.dma_start(starts[:, s, :], net.start_rows[cols(n * GP, GP)].partition_broadcast(RH))\
                    .then_inc(starts_loaded[s], 16)

            over_turns(sp, load)

        @block.scalar
        def _(act):
            for s in range(RING):
                act.copy(idx[:, s, :], net.src1[:, s * G:(s + 1) * G]).then_inc(idx_ready, 1)

            def store_logits(m, s):
                act.wait_ge(logit_ready, m + 1)
                act.dma_start(net.l_spill[cols(m, 1), :, :].rearrange("a p c -> p (a c)"),
                              logit[:, s, :, :].rearrange("p g c -> p (g c)")).then_inc(l_stored[s], 16)

            def store_maxima(m, s):
                act.wait_ge(scanned, m + 1)
                act.dma_start(net.m_spill[cols(m, 1), :, :].rearrange("a p c -> p (a c)"), top[:, s, :])\
                    .then_inc(m_stored[s], 16)

            def step(n, s, turn):
                act.wait_ge(gathered[s], (turn + 1) * (16 * G))
                act.copy(idx[:, s, :], net.src1[:, cols(n * G + TURN, G)]).then_inc(idx_ready, 1)
                act.dma_start(net.v_spill[cols(n, 1), :, :, :].rearrange("a p g d -> p (a g) d"),
                              kv[:, s, :, D:2 * D]).then_inc(v_stored[s], 16)
                if there(n - 1):
                    store_logits(n - 1, (s - 1) % RING)
                if there(n - 2):
                    store_maxima(n - 2, (s - 2) % RING)

            over_turns(act, step)
            store_logits(STEPS - 1, RING - 1)
            store_maxima(STEPS - 2, RING - 2)
            store_maxima(STEPS - 1, RING - 1)
            for s in range(RING):
                for stored in (v_stored, l_stored, m_stored):
                    act.wait_ge(stored[s], 16 * TURNS)

        @block.vector
        def _(dve):
            dve.wait_ge(b_loaded, 16)
            dve.wait_ge(blank, 1)

            def onehots(n, s, turn):
                dve.wait_ge(rows_loaded[s], (turn + 1) * 16)
                if there(n - 2):
                    dve.wait_ge(queries, n - 1)
                for r in range(R):
                    last = dve.tensor_scalar(oht[:, s % 2, r, :], rows[:, s, :], net.part[:, r:r + 1], None,
                                             ALU.is_equal)
                last.then_inc(onehot_t, 1)

            def scores(m, s, turn):
                o = s % 2
                dve.tensor_tensor(mask[:, o, :].rearrange("p (g r) -> p g r", r=R),
                                  spread(net.rel[:, cols(m * G, G)].unsqueeze(2), [P, G, R]),
                                  spread(net.lane[:, 0:R].unsqueeze(1), [P, G, R]), ALU.not_equal)\
                    .then_inc(mask_ready, 1)
                dve.wait_ge(queries, m + 1)
                dve.wait_ge(gathered[s], (turn + 1) * (16 * G))
                dve.scalar_tensor_tensor(out=prod[:, o, :].rearrange("p (g d) -> p g d", d=D), in0=kv[:, s, :, 0:D],
                                         scalar=DH ** -0.5,
                                         in1=ps[:, o * BANK:(o + 1) * BANK].rearrange("p (g d) -> p g d", d=D),
                                         op0=ALU.mult, op1=ALU.mult).then_inc(prod_ready, 1)
                dve.wait_ge(mask_ready, m + 1)
                dve.scalar_tensor_tensor(
                    out=shifted[:, o, :, :].rearrange("p g (r h) -> p g r h", h=H),
                    in0=spread(mask[:, o, :].rearrange("p (g r) -> p g r", r=R).unsqueeze(3), [P, G, R, H]),
                    scalar=-BIG, in1=spread(bias[:, :].rearrange("p (r h) -> p r h", h=H).unsqueeze(1), [P, G, R, H]),
                    op0=ALU.mult, op1=ALU.add).then_inc(bias_ready, 1)
                dve.wait_ge(prod_ready, m + 1)
                dve.tensor_reduce(score[:, o, :], prod[:, o, :].rearrange("p (g d) -> p g d", d=DH),
                                  AX_X, ALU.add).then_inc(score_ready, 1)
                dve.wait_ge(bias_ready, m + 1)
                dve.wait_ge(score_ready, m + 1)
                if there(m - RING):
                    dve.wait_ge(l_stored[s], turn * 16)
                dve.tensor_tensor(
                    logit[:, s, :, :].rearrange("p g (r h) -> p g r h", h=H),
                    spread(score[:, o, :].rearrange("p (g h) -> p g h", h=H).unsqueeze(2), [P, G, R, H]),
                    shifted[:, o, :, :].rearrange("p g (r h) -> p g r h", h=H), ALU.add).then_inc(logit_ready, 1)

            def maxima(m, s, turn):
                dve.wait_ge(starts_loaded[s], (turn + 1) * 16)
                dve.wait_ge(turned, m + 1)
                if there(m - RING):
                    dve.wait_ge(m_stored[s], turn * 16)
                if there(m - 1):
                    dve.wait_ge(scanned, m)
                    initial = top[:, (s - 1) % RING, GP - 1:GP]
                else:
                    initial = low[0:RH, 0:1]
                o = 2 + s % 2
                dve.tensor_tensor_scan(top[:, s, :], starts[:, s, :], ps[0:RH, o * BANK:(o + 1) * BANK], initial,
                                       ALU.add, ALU.max).then_inc(scanned, 1)

            def step(n, s, turn):
                onehots(n, s, turn)
                if there(n - 1):
                    scores(n - 1, (s - 1) % RING, turn if s else turn - 1)
                if there(n - 2):
                    maxima(n - 2, (s - 2) % RING, turn if s >= 2 else turn - 1)

            over_turns(dve, step)
            scores(STEPS - 1, RING - 1, TURNS - 1)
            maxima(STEPS - 2, RING - 2, TURNS - 1)
            maxima(STEPS - 1, RING - 1, TURNS - 1)

        @block.tensor
        def _(pe):
            registers = Registers(nc, pe, net)

            def expand(n, s):
                blocks = registers.load(n)
                pe.wait_ge(onehot_t, n + 1)
                if there(n - 2):
                    pe.wait_ge(prod_ready, n - 1)
                o = s % 2
                for i in range(G):
                    base = nc.snap(blocks[i] * (3 * R * D), engines=[PE])
                    for r in range(R):
                        for part in range(3):
                            last = pe.matmul(ps[:, o * BANK + i * D:o * BANK + (i + 1) * D],
                                             oht[:, o, r, i * P:(i + 1) * P],
                                             q1[:, cols(base + (part * R + r) * D, D)],
                                             start=(r == 0 and part == 0), stop=(r == R - 1 and part == 2))
                last.then_inc(queries, 1)

            def turn_logits(m, s):
                pe.wait_ge(logit_ready, m + 1)
                if there(m - 2):
                    pe.wait_ge(scanned, m - 1)
                settle(pe, passed_pe)
                o = 2 + s % 2
                for i in range(G):
                    last = pe.transpose(ps[0:RH, o * BANK + i * P:o * BANK + (i + 1) * P], logit[:, s, i, :],
                                        net.ident[:, :])
                last.then_inc(turned, 1)

            def step(n, s, turn):
                expand(n, s)
                if there(n - 1):
                    turn_logits(n - 1, (s - 1) % RING)

            over_turns(pe, step)
            turn_logits(STEPS - 1, RING - 1)


def sums1(net, probs, rsum):
    nc = net.nc
    with ExitStack() as ctx:
        def sb(name, shape, dt):
            return ctx.enter_context(nc.sbuf_tensor(name, shape, dt))

        (passed_sp, passed_pe, passed_dve, scanned, turned, diff_ready, onehot, exp_ready, added, blank, v_done, parts) = sems(
            ctx, nc, "s1", "passed_sp", "passed_pe", "passed_dve", "scanned", "turned", "diff_ready", "onehot", "exp_ready", "added", "blank",
            "vector_done", "parts")
        loaded = sems(ctx, nc, "s1", *[f"loaded{s}" for s in range(RING)])
        starts = sb("starts_", [RH, RING, GP], BF16)
        top = sb("top_", [RH, RING, GP], F32)
        logit = sb("logit_", [P, RING, G * RH], F32)
        diff = sb("diff", [P, 2, G * RH], F32)
        oh = sb("oh_", [P, RING, G, P], F32)
        rs = oh[:, 0:2, :, :].rearrange("p a g e -> p (a g e)")[:, 0:NB * RH]
        rest = oh[:, 2:4, :, :].rearrange("p a g e -> p (a g e)")[:, 0:NB * RH]
        low = sb("low_", [P, 1], F32)
        ps = net.psum
        block = ctx.enter_context(nc.Block())

        def back(n):
            return STEPS - 1 - n if isinstance(n, int) else (STEPS - 1) - n

        @block.gpsimd
        def _(pool):
            pool.memset(low[:, :], -BIG).then_inc(blank, 1)

        @block.sync
        def _(sp):
            def load(n, s, turn):
                at = back(n)
                if there(n - RING):
                    sp.wait_ge(scanned, n - (RING - 1))
                    sp.wait_ge(turned, n - (RING - 1))
                    sp.wait_ge(diff_ready, n - (RING - 1))
                    settle(sp, passed_sp)
                sp.dma_start(starts[:, s, :], net.start_rows[cols(at * GP + 1, GP)].partition_broadcast(RH))\
                    .then_inc(loaded[s], 16)
                sp.dma_start(top[:, s, :], net.m_spill[cols(at, 1), :, :].rearrange("a p c -> p (a c)"))\
                    .then_inc(loaded[s], 16)
                sp.dma_start(logit[:, s, :], net.l_spill[cols(at, 1), :, :].rearrange("a p c -> p (a c)"))\
                    .then_inc(loaded[s], 16)

            over_turns(sp, load)

        @block.vector
        def _(dve):
            dve.wait_ge(blank, 1)

            def maxima(n, s, turn):
                dve.wait_ge(loaded[s], (turn + 1) * 48)
                if there(n - 1):
                    dve.wait_ge(scanned, n)
                    initial = top[:, (s - 1) % RING, 0:1]
                else:
                    initial = low[0:RH, 0:1]
                dve.tensor_tensor_scan(top[:, s, ::-1], starts[:, s, ::-1], top[:, s, ::-1], initial,
                                       ALU.add, ALU.max).then_inc(scanned, 1)
                if there(n - RING):
                    dve.wait_ge(added, n - (RING - 1))
                settle(dve, passed_dve)
                dve.tensor_tensor(oh[:, s, :, :], spread(net.lane[:, :].unsqueeze(1), [P, G, P]),
                                  spread(net.local[:, cols(back(n) * G, G)].unsqueeze(2), [P, G, P]),
                                  ALU.is_equal).then_inc(onehot, 1)

            def diffs(m, s):
                o = s % 2
                dve.wait_ge(turned, m + 1)
                if there(m - 2):
                    dve.wait_ge(exp_ready, m - 1)
                dve.scalar_tensor_tensor(out=diff[:, o, :], in0=ps[:, (4 + o) * BANK:(4 + o) * BANK + G * RH],
                                         scalar=NEG, in1=logit[:, s, :], op0=ALU.max, op1=ALU.subtract)\
                    .then_inc(diff_ready, 1)

            def step(n, s, turn):
                maxima(n, s, turn)
                if there(n - 1):
                    diffs(n - 1, (s - 1) % RING)

            over_turns(dve, step)
            diffs(STEPS - 1, RING - 1)
            dve.wait_ge(added, STEPS)
            rs3 = rs.rearrange("p (b c) -> p b c", c=RH)
            dve.tensor_scalar(rs3, ps[:, 0:NB * SPITCH].rearrange("p (b c) -> p b c", c=SPITCH)[:, :, 0:RH],
                              1e-12, None, ALU.add).then_inc(v_done, 1)
            dve.wait_ge(v_done, 1)
            dve.reciprocal(rs, rs).then_inc(v_done, 1)
            dve.wait_ge(v_done, 2)
            part = [rsum[:, :].rearrange("p (b s c) -> p b s c", s=3, c=RH)[:, :, s, :] for s in range(3)]
            split3(dve, *part, rs3, rest.rearrange("p (b c) -> p b c", c=RH), parts, 0)

        @block.scalar
        def _(act):
            def step(n, s, turn):
                act.wait_ge(diff_ready, n + 1)
                act.activation(probs[:, cols(back(n) * (G * RH), G * RH)], diff[:, s % 2, :], ACT.Exp, scale=-1.0)\
                    .then_inc(exp_ready, 1)

            over_turns(act, step)

        @block.tensor
        def _(pe):
            clear_banks(pe, net, 4)
            registers = Registers(nc, pe, net)

            def turn_maxima(n, s):
                pe.wait_ge(scanned, n + 1)
                if there(n - 2):
                    pe.wait_ge(diff_ready, n - 1)
                settle(pe, passed_pe)
                o = s % 2
                for i in range(G):
                    last = pe.transpose(ps[:, (4 + o) * BANK + i * RH:(4 + o) * BANK + (i + 1) * RH],
                                        top[:, s, i * P:(i + 1) * P], net.ident[0:RH, 0:RH])
                last.then_inc(turned, 1)

            def add(m, s):
                at = back(m)
                blocks = registers.load(at)
                pe.wait_ge(onehot, m + 1)
                pe.wait_ge(exp_ready, m + 1)
                for i in range(G):
                    last = pe.matmul(ps[:, cols(blocks[i] * SPITCH, RH)], oh[:, s, i, :],
                                     probs[:, cols(at * (G * RH) + i * RH, RH)],
                                     start=False, stop=False, skip_group_check=True)
                last.then_inc(added, 1)

            def step(n, s, turn):
                turn_maxima(n, s)
                if there(n - 2):
                    add(n - 2, (s - 2) % RING)

            over_turns(pe, step)
            add(STEPS - 2, RING - 2)
            add(STEPS - 1, RING - 1)


def values1(net, probs, rsum):
    nc = net.nc
    with ExitStack() as ctx:
        def sb(name, shape, dt):
            return ctx.enter_context(nc.sbuf_tensor(name, shape, dt))

        (onehot_t, onehot, scales, scaled, attn_ready, msg_ready, added) = sems(
            ctx, nc, "v1", "onehot_t", "onehot", "scales", "scaled", "attn_ready", "msg_ready", "added")
        loaded = sems(ctx, nc, "v1", *[f"loaded{s}" for s in range(RING)])
        rows = sb("rows2", [P, RING, GP], F16)
        v = sb("v2", [P, RING, G, D], F32)
        oht = sb("oht2", [P, 2, GP], BF16)
        oh = sb("oh2", [P, RING, G, P], F32)
        wide = sb("wide", [P, 2, G, RH], F32)
        attn = sb("attn", [P, 2, G, H], F32)
        ps = net.psum
        se = net.psum[:, 7 * BANK:7 * BANK + G * RH]
        block = ctx.enter_context(nc.Block())

        @block.sync
        def _(sp):
            def load(n, s, turn):
                if there(n - RING):
                    sp.wait_ge(onehot_t, n - (RING - 1))
                    sp.wait_ge(added, n - (RING - 1))
                sp.dma_start(rows[:, s, :], net.local_rows[cols(n * GP, GP)].partition_broadcast(P))\
                    .then_inc(loaded[s], 16)
                sp.dma_start(v[:, s, :, :], net.v_spill[cols(n, 1), :, :, :].rearrange("a p g d -> p (a g) d"))\
                    .then_inc(loaded[s], 16)

            over_turns(sp, load)

        @block.vector
        def _(dve):
            def onehots(n, s, turn):
                dve.wait_ge(loaded[s], (turn + 1) * 32)
                if there(n - 2):
                    dve.wait_ge(scales, n - 1)
                dve.tensor_scalar(oht[:, s % 2, :], rows[:, s, :], net.part1[:, 0:1], None, ALU.is_equal)\
                    .then_inc(onehot_t, 1)
                if there(n - RING):
                    dve.wait_ge(added, n - (RING - 1))
                dve.tensor_tensor(oh[:, s, :, :], spread(net.lane[:, :].unsqueeze(1), [P, G, P]),
                                  spread(net.local[:, cols(n * G, G)].unsqueeze(2), [P, G, P]), ALU.is_equal)\
                    .then_inc(onehot, 1)

            def messages(m, s):
                o = s % 2
                dve.wait_ge(scales, m + 1)
                dve.tensor_tensor(wide[:, o, :, :].rearrange("p g c -> p (g c)"), se,
                                  probs[:, cols(m * (G * RH), G * RH)], ALU.mult).then_inc(scaled, 1)
                dve.wait_ge(scaled, m + 1)
                dve.tensor_reduce(attn[:, o, :, :], wide[:, o, :, :].rearrange("p g (r h) -> p g h r", h=H),
                                  AX_X, ALU.add).then_inc(attn_ready, 1)
                dve.wait_ge(attn_ready, m + 1)
                x = v[:, s, :, :].rearrange("p g (h d) -> p g h d", d=DH)
                dve.tensor_tensor(x, x, spread(attn[:, o, :, :].unsqueeze(3), [P, G, H, DH]), ALU.mult)\
                    .then_inc(msg_ready, 1)

            def step(n, s, turn):
                onehots(n, s, turn)
                if there(n - 1):
                    messages(n - 1, (s - 1) % RING)

            over_turns(dve, step)
            messages(STEPS - 1, RING - 1)

        @block.tensor
        def _(pe):
            clear_banks(pe, net, 7)
            registers = Registers(nc, pe, net)

            def expand(n, s):
                blocks = registers.load(n)
                pe.wait_ge(onehot_t, n + 1)
                if there(n - 1):
                    pe.wait_ge(scaled, n)
                for i in range(G):
                    for part in range(3):
                        last = pe.matmul(se[:, i * RH:(i + 1) * RH], oht[:, s % 2, i * P:(i + 1) * P],
                                         rsum[:, cols(blocks[i] * (3 * RH) + part * RH, RH)],
                                         start=(part == 0), stop=(part == 2))
                last.then_inc(scales, 1)

            def add(m, s):
                blocks = registers.load(m)
                pe.wait_ge(onehot, m + 1)
                pe.wait_ge(msg_ready, m + 1)
                for i in range(G):
                    last = pe.matmul(ps[:, cols(blocks[i] * D, D)], oh[:, s, i, :], v[:, s, i, :],
                                     start=False, stop=False, skip_group_check=True)
                last.then_inc(added, 1)

            def step(n, s, turn):
                expand(n, s)
                if there(n - 2):
                    add(n - 2, (s - 2) % RING)

            over_turns(pe, step)
            add(STEPS - 2, RING - 2)
            add(STEPS - 1, RING - 1)


def nodes2(net):
    nc, a = net.nc, net.a
    with ExitStack() as ctx:
        def sb(name, shape, dt):
            return ctx.enter_context(nc.sbuf_tensor(name, shape, dt))

        (w_loaded, v_done, ready, w_turned, w_copied, turned, copied, product, taken, stats, aggr, std_ready,
         scale_ready, normed, blank, finished, stored) = sems(
            ctx, nc, "n2", "w_loaded", "vector_done", "ready", "w_turned", "w_copied", "turned", "copied",
            "product", "taken", "stats", "aggr", "std_ready", "scale_ready", "normed", "blank", "finished",
            "stored")
        w = sb("w_out", [P, D], F32)
        wt = sb("wt_out", [P, D], F32)
        names = ("L1_gnn_out_proj_b", "L1_gnn_ln_gamma", "L1_gnn_ln_beta")
        vec = sb("vec2", [P, len(names), D], F32)
        eps = sb("eps2", [P, 1], F32)
        t1 = sb("t2", [P, NB, D], F32)
        at = sb("at2", [P, 2, P], F32)
        ps = net.psum
        ALL = [P, NB, D]

        def row(j):
            return spread(vec[:, j, :].unsqueeze(1), ALL)

        block = ctx.enter_context(nc.Block())

        @block.gpsimd
        def _(pool):
            pool.memset(eps[:, :], EPS).then_inc(blank, 1)

        @block.sync
        def _(sp):
            sp.dma_start(w[:, :], a["L1_gnn_out_proj_w"]).then_inc(w_loaded, 16)
            for j, name in enumerate(names):
                sp.dma_start(vec[:, j, :], a[name].partition_broadcast(P)).then_inc(w_loaded, 16)
            sp.wait_ge(finished, 1)
            sp.dma_start(net.out[0:(NB - 1) * P, :].rearrange("(b p) d -> p b d", p=P), t1[:, 0:NB - 1, :])\
                .then_inc(stored, 16)
            sp.dma_start(net.out[(NB - 1) * P:N, :], t1[0:LAST, NB - 1, :]).then_inc(stored, 16)
            sp.wait_ge(stored, 32)

        @block.vector
        def _(dve):
            done = [0]

            def chain(ins):
                done[0] += 1
                ins.then_inc(v_done, 1)
                dve.wait_ge(v_done, done[0])

            dve.tensor_copy(t1[:, :, :].rearrange("p b d -> p (b d)"), ps[:, 0:NB * D]).then_inc(ready, 1)
            dve.wait_ge(w_loaded, 16 * (1 + len(names)))
            chain(dve.tensor_tensor(net.h[:, :, :], net.h[:, :, :], row(0), ALU.add))

            def take(b, k, first):
                dve.wait_ge(product, b + 1)
                dve.tensor_tensor(block_of(net.h, b), ps[:, (2 + k) * BANK:(2 + k) * BANK + D],
                                  block_of(net.h, b), ALU.add).then_inc(taken, 1)

            over_blocks(dve, take)
            dve.wait_ge(taken, NB)
            layer_norm_stats(dve, net, net.h, stats, aggr, 1)
            layer_norm_scale(dve, net, std_ready, scale_ready, 1)
            dve.wait_ge(normed, NB)
            chain(dve.tensor_tensor(t1[:, :, :], t1[:, :, :], row(1), ALU.mult))
            chain(dve.tensor_tensor(t1[:, :, :], t1[:, :, :], row(2), ALU.add))
            dve.tensor_tensor(t1[:, :, :], t1[:, :, :], net.x[:, :, :], ALU.add).then_inc(finished, 1)

        @block.scalar
        def _(act):
            act.wait_ge(blank, 1)
            act.wait_ge(w_turned, 1)
            act.copy(wt[:, :], ps[:, 4 * BANK:4 * BANK + D]).then_inc(w_copied, 1)

            def copy(b, k, first):
                act.wait_ge(turned, b + 1)
                act.copy(at[:, k, :], ps[:, k * BANK:k * BANK + P]).then_inc(copied, 1)

            over_blocks(act, copy)
            layer_norm_std(act, net, eps, aggr, std_ready, 1)
            normalize(act, net, t1, net.h, ACT.Identity, scale_ready, 1, normed)

        @block.tensor
        def _(pe):
            pe.wait_ge(ready, 1)
            pe.wait_ge(w_loaded, 16 * (1 + len(names)))
            pe.transpose(ps[:, 4 * BANK:4 * BANK + D], w[:, :], net.ident[:, :]).then_inc(w_turned, 1)
            pe.wait_ge(w_copied, 1)

            def out_proj(b, k, first):
                if not first:
                    pe.wait_ge(copied, b - 1)
                pe.transpose(ps[:, k * BANK:k * BANK + P], block_of(t1, b), net.ident[:, :]).then_inc(turned, 1)
                pe.wait_ge(copied, b + 1)
                if not first:
                    pe.wait_ge(taken, b - 1)
                pe.matmul(ps[:, (2 + k) * BANK:(2 + k) * BANK + D], at[:, k, :], wt[:, :], start=True, stop=True)\
                    .then_inc(product, 1)

            over_blocks_unrolled(pe, out_proj)


_OUTS = [((N, D), "float32")]


def kernel(**inputs):
    import numpy as _np
    import concourse.bacc as _bacc
    from concourse import mybir as _mybir
    from concourse.bass_utils import run_bass_kernel_spmd as _run

    nc = _bacc.Bacc("TRN2", target_bir_lowering=False, num_devices=1)
    arrays, args = {}, {}
    for name, value in inputs.items():
        v = _np.ascontiguousarray(value)
        arrays[f"in_{name}"] = v
        args[name] = nc.dram_tensor(f"in_{name}", v.shape, _mybir.dt.from_np(v.dtype), kind="ExternalInput").ap()
    out = nc.dram_tensor("out_0", _OUTS[0][0], F32, kind="ExternalOutput").ap()
    build(nc, args, out)
    r = _run(nc, [arrays], core_ids=[0])
    return r.results[0]["out_0"]
```

```python
from contextlib import ExitStack

import numpy as np

import concourse.bass as bass
from concourse import mybir

ALU = mybir.AluOpType
ACT = mybir.ActivationFunctionType
AX_X = mybir.AxisListType.X
PE = mybir.EngineType.PE
F32, BF16, F16, I32 = mybir.dt.float32, mybir.dt.bfloat16, mybir.dt.float16, mybir.dt.int32

P = 128
N = 3125
E = 100000
D = 128
H = 8
DH = D // H
R = 5
RH = R * H
DFF = 2 * D
GROUP = 25
SUBS = 5
NODES = SUBS * GROUP
NB = -(-N // NODES)
NG = NB * SUBS
assert NB * NODES == N and GROUP * R <= P
NPAD = NB * P
T = -(-E // P)
JT = -(-T // P)
TPAD = JT * P
G = 4
RING = 4
GP = G * P
TURN = G * RING


class Pass:

    def __init__(self, size, count):
        self.size, self.count = size, count
        self.turns = -(-(T + count - 1) // TURN)
        self.steps = self.turns * RING
        self.items = self.turns * TURN
        self.cols = -(-(self.items + TURN) // P)


L0 = Pass(NODES, NB)
L1 = Pass(GROUP, NG)
GW = 2 * G
GWP = GW * P
WIDE_STEPS = L1.items // GW
BANK = 512
EPS = 1e-5
BIG = float(2.0 ** 100)
NEG = -1e9
PAD_DST = N
OUTSIDE = 20000.0
ROUND = 1.5 * 2 ** 23
KW = 4


def over_turns(eng, steps, step, peeled=1):
    turns = steps // RING
    for n in range(RING * peeled):
        step(n, n % RING, n // RING)
    with eng.Fori(peeled, turns) as turn:
        for s in range(RING):
            step(turn * RING + s, s, turn)
    for n in range(turns * RING, steps):
        step(n, n % RING, turns)


def over_blocks(eng, body):
    body(0, 0, True)
    body(1, 1, True)
    with eng.Fori(1, (NB - 1) // 2) as i:
        body(i * 2, 0, False)
        body(i * 2 + 1, 1, False)
    body(NB - 1, 0, False)


def over_blocks_unrolled(pe, body):
    for b in range(NB):
        body(b, b % 2, b < 2)


def there(n):
    return not isinstance(n, int) or n >= 0


def settle(eng, passed):
    eng.sem_inc(passed, 1)


def cols(start, size):
    return bass.ds(start, size)


def spread(ap, shape):
    return ap.broadcast_to(shape)


class Net:
    pass


def build(nc, a, out):
    with ExitStack() as ctx:
        net = Net()
        net.nc, net.a, net.out = nc, a, out

        def sb(name, shape, dt):
            return ctx.enter_context(nc.sbuf_tensor(name, shape, dt))

        net.psum = ctx.enter_context(nc.psum_tensor("psum", [P, 8 * BANK], F32))
        net.edges = nc.dram_tensor("edges", [TPAD, KW * P], I32).ap()
        net.local_rows = nc.dram_tensor("local_rows", [L0.cols * P * P], F16).ap()
        net.key_rows = nc.dram_tensor("key_rows", [L1.cols * P * P], F16).ap()
        net.start_rows = nc.dram_tensor("start_rows", [L1.cols * P * P], BF16).ap()
        net.kv0 = nc.dram_tensor("kv0", [NPAD, 2 * D], F32).ap()
        net.kv1 = nc.dram_tensor("kv1", [NPAD * R, 2 * D], F32).ap()
        net.q1_parts = nc.dram_tensor("q1_parts", [NPAD * R, 3 * D], BF16).ap()
        net.v_spill = nc.dram_tensor("v_spill", [L1.steps, P, G, D], F32).ap()
        net.l_spill = nc.dram_tensor("l_spill", [L1.steps, P, G * RH], F32).ap()
        net.m_spill = nc.dram_tensor("m_spill", [L1.steps, RH, GP], F32).ap()

        net.ident = sb("ident", [P, P], F32)
        net.ones = sb("ones", [P, P], F32)
        net.lane = sb("lane", [P, P], F32)
        net.part1 = sb("part1", [P, 1], F32)
        net.ones16 = sb("ones16", [P, 1], BF16)
        net.zeros = sb("zeros", [P, BANK], BF16)
        net.local0 = sb("local0", [P, L0.cols * P], F32)
        net.local1 = sb("local1", [P, L1.cols * P], F32)
        net.rel = sb("rel", [P, L1.cols * P], F32)
        net.key = sb("key", [P, L1.cols * P], F32)
        net.src0 = sb("src0", [P, L0.cols * P], I32)
        net.src1 = sb("src1", [P, L1.cols * P], I32)
        net.blocks0 = sb("blocks0", [1, L0.cols * P], I32)
        net.blocks1 = sb("blocks1", [1, L1.cols * P], I32)
        net.groups1 = sb("groups1", [1, L1.cols * P], I32)
        net.flag = sb("flag", [1, 1], I32)
        net.x = sb("x", [P, NB, D], F32)
        net.h = sb("h", [P, NB, D], F32)
        net.mv = sb("mv", [P, NB, 2], F32)
        net.tmp = sb("tmp", [P, 2, NB], F32)
        net.st = sb("st", [P, NB, 6], F32)
        net.rstd = sb("rstd", [P, NB], F32)
        net.shift = sb("shift", [P, NB], F32)

        def run(stage, *args):
            with nc.cleanup_on_exit():
                stage(net, *args)

        run(constants)
        with nc.sbuf_tensor("raw", [P, JT, KW, P], I32) as raw:
            run(load_edges, raw)
        run(sort_edges)
        run(items, L0)
        run(items, L1)
        with nc.sbuf_tensor("q0", [P, NB * 3 * D], BF16) as q0:
            run(nodes0, q0)
            run(edges0, q0)
        run(nodes1)
        with nc.sbuf_tensor("q1", [P, NG * 3 * D], BF16) as q1:
            run(logits1, q1)
        with nc.sbuf_tensor("probs", [P, L1.items * H], F32) as probs:
            with nc.sbuf_tensor("rsum", [P, NG * 3 * H], BF16) as rsum:
                run(sums1, probs, rsum)
                run(values1, probs, rsum)
        run(nodes2)


def sems(nc, stage, *names):
    return [nc.alloc_semaphore(f"{stage}_{x}") for x in names]


def constants(net):
    nc = net.nc
    with ExitStack() as ctx:
        blank, rows = sems(nc, "c", "blank", "rows")
        block = ctx.enter_context(nc.Block())

        @block.gpsimd
        def _(pool):
            pool.memset(net.ident[:, :], 0.0).then_inc(blank, 1)
            pool.memset(net.ones[:, :], 1.0)
            pool.memset(net.ones16[:, :], 1.0)
            pool.memset(net.zeros[:, :], 0.0)
            pool.wait_ge(blank, 1)
            pool.affine_select(out=net.ident[:, :], in_=net.ident[:, :], compare_op=ALU.not_equal, fill=1.0,
                               base=0, pattern=[[-1, P]], channel_multiplier=1)
            pool.iota(net.lane[:, :], [[1, P]], base=0, channel_multiplier=0,
                      allow_small_or_imprecise_dtypes=True)
            pool.iota(net.part1[:, :], [[0, 1]], base=0, channel_multiplier=1,
                      allow_small_or_imprecise_dtypes=True)


def load_edges(net, raw):
    nc, a = net.nc, net.a
    full = (T - 1) // P
    rows = (E - full * P * P) // P
    rest = E - (full * P + rows) * P
    with ExitStack() as ctx:
        padded, loaded, kept, checked, summed = sems(nc, "e", "padded", "loaded", "kept", "checked", "summed")
        falls = ctx.enter_context(nc.sbuf_tensor("falls", [P, JT, P], F32))
        fall = ctx.enter_context(nc.sbuf_tensor("fall", [P, 1], F32))
        ps = net.psum
        block = ctx.enter_context(nc.Block())

        @block.gpsimd
        def _(pool):
            pool.memset(raw[:, full, 0, :], PAD_DST).then_inc(padded, 1)
            pool.memset(raw[:, full, 1:3, :], 0).then_inc(padded, 1)
            pool.memset(raw[:, full, 3, :], PAD_DST).then_inc(padded, 1)
            pool.memset(raw[0:1, 0, 3, 0:1], -1).then_inc(padded, 1)

        @block.sync
        def _(sp):
            sp.wait_ge(padded, 4)
            body = full * P * P
            for k, name in enumerate(("dst", "src", "edge_type_5")):
                v = a[name]
                sp.dma_start(raw[:, 0:full, k, :],
                             v[0:body].rearrange("(j p e) -> p j e", p=P, e=P)).then_inc(loaded, 16)
                sp.dma_start(raw[0:rows, full, k, :],
                             v[body:body + rows * P].rearrange("(p e) -> p e", e=P)).then_inc(loaded, 16)
                sp.dma_start(raw[rows:rows + 1, full, k, 0:rest],
                             v[E - rest:E].rearrange("(p e) -> p e", p=1)).then_inc(loaded, 16)
            v = a["dst"]
            sp.dma_start(raw[1:P, 0, 3, :],
                         v[P - 1:P * P - 1].rearrange("(p e) -> p e", e=P)).then_inc(loaded, 16)
            sp.dma_start(raw[0:1, 0, 3, 1:P],
                         v[0:P - 1].rearrange("(p e) -> p e", p=1)).then_inc(loaded, 16)
            sp.dma_start(raw[:, 1:full, 3, :],
                         v[P * P - 1:body - 1].rearrange("(j p e) -> p j e", p=P, e=P)).then_inc(loaded, 16)
            sp.dma_start(raw[0:rows, full, 3, :],
                         v[body - 1:body - 1 + rows * P].rearrange("(p e) -> p e", e=P)).then_inc(loaded, 16)
            sp.dma_start(raw[rows:rows + 1, full, 3, 0:rest + 1],
                         v[E - rest - 1:E].rearrange("(p e) -> p e", p=1)).then_inc(loaded, 16)
            sp.wait_ge(loaded, 16 * 14)
            sp.dma_start(net.edges.rearrange("(j p) c -> p j c", p=P),
                         raw[:, :, :, :].rearrange("p j k e -> p j (k e)")).then_inc(kept, 16)
            sp.wait_ge(kept, 16)

        @block.vector
        def _(dve):
            dve.wait_ge(loaded, 16 * 14)
            dve.wait_ge(padded, 4)
            dve.tensor_tensor(falls[:, :, :], raw[:, :, 3, :], raw[:, :, 0, :], ALU.is_gt).then_inc(checked, 1)
            dve.wait_ge(checked, 1)
            dve.tensor_reduce(fall[:, :], falls[:, :, :].rearrange("p j e -> p (j e)"), AX_X, ALU.add)\
                .then_inc(checked, 1)
            dve.wait_ge(summed, 1)
            dve.tensor_scalar(net.flag[:, :], ps[0:1, 0:1], 0.0, None, ALU.is_gt)

        @block.tensor
        def _(pe):
            pe.wait_ge(checked, 2)
            pe.matmul(ps[0:1, 0:1], fall[:, :], net.ones[:, 0:1], start=True, stop=True).then_inc(summed, 1)


def sort_edges(net):
    nc = net.nc
    DUMP = NPAD
    words = KW * P
    counters = nc.dram_tensor("counters", [NPAD + P, 1], F32).ap()
    sorted_ = nc.dram_tensor("sorted_edges", [TPAD * words, 1], I32).ap()
    with ExitStack() as ctx:
        def sb(name, shape, dt):
            return ctx.enter_context(nc.sbuf_tensor(name, shape, dt))

        (blank, cleared, fetched, based, computed, counted, written, v_done, passed_pool, whole, prefixed, final) = sems(
            nc, "o", "blank", "cleared", "fetched", "based", "computed", "counted", "written", "vector_done",
            "passed_pool", "whole", "prefixed", "final")
        col = sb("col", [P, KW], I32)
        row = sb("row", [P, P], I32)
        below = sb("below", [P, P], F32)
        eq = sb("eq", [P, P], F32)
        colf = sb("colf", [P, KW], F32)
        rowf = sb("rowf", [P, P], F32)
        total = sb("total", [P, 1], F32)
        before = sb("before", [P, 1], F32)
        base = sb("base", [P, 1], F32)
        new = sb("new", [P, 1], F32)
        t1 = sb("t1_", [P, 1], F32)
        t2 = sb("t2_", [P, 1], F32)
        wide = sb("wide_", [P, 1], I32)
        at = sb("at_", [P, 8], F32)
        at_i = sb("at_i", [P, 8], I32)
        first = sb("first", [1, 1], I32)
        count = sb("count", [1, NPAD], F32)
        prefix = sb("prefix", [1, NPAD], F32)
        block = ctx.enter_context(nc.Block())

        @block.gpsimd
        def _(pool):
            unsorted = pool.value_load(net.flag[0:1, 0:1], min_val=0, max_val=1)
            with pool.If(unsorted > 0):
                pool.memset(below[:, :], 1.0).then_inc(blank, 1)
                pool.memset(count[:, :], 0.0).then_inc(blank, 1)
                pool.memset(first[:, :], -1).then_inc(blank, 1)
                pool.wait_ge(blank, 3)
                pool.affine_select(out=below[:, :], in_=below[:, :], compare_op=ALU.is_ge, fill=0.0,
                                   base=-1, pattern=[[-1, P]], channel_multiplier=1).then_inc(blank, 1)
                pool.dma_start(counters[0:NPAD, :].rearrange("n a -> a n"), count[:, :]).then_inc(cleared, 16)
                pool.dma_start(counters[NPAD:NPAD + P, :].rearrange("n a -> a n"), count[:, 0:P])\
                    .then_inc(cleared, 16)
                pool.dma_start(sorted_[3 * P:3 * P + 1, :], first[:, :]).then_inc(cleared, 16)
                pool.wait_ge(cleared, 48)

                def sweep(t, moving):
                    done = t + T if moving else t
                    edge = net.edges[cols(t, 1), :]
                    settle(pool, passed_pool)
                    with nc.allow_non_contiguous_dma(reason="one word to a partition"):
                        pool.dma_start(col[:, 0:3], edge.rearrange("a (k p) -> p (a k)", p=P)[:, 0:3])\
                            .then_inc(fetched, 16)
                    pool.dma_start(row[:, :], edge[:, 0:P].rearrange("a e -> (a e)").partition_broadcast(P))\
                        .then_inc(fetched, 16)
                    pool.wait_ge(fetched, (done + 1) * 32)
                    settle(pool, passed_pool)
                    pool.indirect_dma_start(base[:, :], None, counters,
                                            bass.IndirectOffsetOnAxis(ap=col[:, 0:1], axis=0)).then_inc(based, 16)
                    pool.wait_ge(computed, done + 1)
                    settle(pool, passed_pool)
                    pool.indirect_dma_start(counters, bass.IndirectOffsetOnAxis(ap=at_i[:, 0:1], axis=0),
                                            new[:, :], None).then_inc(written if moving else counted, 16)
                    if moving:
                        for k, word in enumerate((0, 1, 2, 0)):
                            pool.indirect_dma_start(
                                sorted_, bass.IndirectOffsetOnAxis(ap=at_i[:, 1 + k:2 + k], axis=0),
                                col[:, word:word + 1], None).then_inc(written, 16)
                        pool.wait_ge(written, (t + 1) * 80)
                    else:
                        pool.wait_ge(counted, (t + 1) * 16)

                with pool.Fori(0, T) as t:
                    sweep(t, False)
                pool.dma_start(count[:, :], counters[0:NPAD, :].rearrange("n a -> a n")).then_inc(whole, 16)
                pool.wait_ge(prefixed, 2)
                pool.dma_start(counters[0:NPAD, :].rearrange("n a -> a n"), prefix[:, :]).then_inc(whole, 16)
                pool.wait_ge(whole, 32)
                with pool.Fori(0, T) as t:
                    sweep(t, True)
                pool.dma_start(net.edges[0:T, :],
                               sorted_[0:T * words, :].rearrange("(t w) a -> t (w a)", w=words)).then_inc(final, 16)
                pool.wait_ge(final, 16)

        @block.vector
        def _(dve):
            unsorted = dve.value_load(net.flag[0:1, 0:1], min_val=0, max_val=1)
            with dve.If(unsorted > 0):
                dve.wait_ge(blank, 4)

                def sweep(t, moving):
                    done = t + T if moving else t
                    steps_before = t * STEP2 + T * STEP1 if moving else t * STEP1
                    count_ = [0]

                    def chain(ins):
                        count_[0] += 1
                        ins.then_inc(v_done, 1)
                        dve.wait_ge(v_done, steps_before + count_[0])

                    dve.wait_ge(fetched, (done + 1) * 32)
                    chain(dve.tensor_copy(colf[:, 0:3], col[:, 0:3]))
                    chain(dve.tensor_copy(rowf[:, :], row[:, :]))
                    chain(dve.tensor_scalar(eq[:, :], rowf[:, :], colf[:, 0:1], None, ALU.is_equal))
                    chain(dve.tensor_reduce(total[:, :], eq[:, :], AX_X, ALU.add))
                    chain(dve.tensor_tensor(eq[:, :], eq[:, :], below[:, :], ALU.mult))
                    chain(dve.tensor_reduce(before[:, :], eq[:, :], AX_X, ALU.add))
                    chain(dve.tensor_scalar(t1[:, :], before[:, :], 0.0, None, ALU.is_gt))
                    chain(dve.tensor_scalar(t2[:, :], net.part1[:, :], float(DUMP), None, ALU.add))
                    chain(dve.tensor_tensor(t2[:, :], t2[:, :], colf[:, 0:1], ALU.subtract))
                    chain(dve.tensor_tensor(t2[:, :], t2[:, :], t1[:, :], ALU.mult))
                    chain(dve.tensor_tensor(at[:, 0:1], t2[:, :], colf[:, 0:1], ALU.add))
                    dve.wait_ge(based, (done + 1) * 16)
                    chain(dve.tensor_tensor(new[:, :], base[:, :], total[:, :], ALU.add))
                    if moving:
                        for k in range(2):
                            chain(dve.scalar_tensor_tensor(out=t1[:, :], in0=base[:, :], scalar=float(k),
                                                           in1=before[:, :], op0=ALU.add, op1=ALU.add))
                            chain(dve.tensor_copy(wide[:, :], t1[:, :]))
                            chain(dve.tensor_scalar(wide[:, :], wide[:, :], 7, None, ALU.logical_shift_right))
                            chain(dve.tensor_copy(t2[:, :], wide[:, :]))
                            chain(dve.scalar_tensor_tensor(out=t1[:, :], in0=t2[:, :], scalar=3.0 * P,
                                                           in1=t1[:, :], op0=ALU.mult, op1=ALU.add))
                            if k == 0:
                                for j in range(3):
                                    chain(dve.tensor_scalar(at[:, 1 + j:2 + j], t1[:, :], float(j * P), None,
                                                            ALU.add))
                            else:
                                chain(dve.tensor_scalar(at[:, 4:5], t1[:, :], 3.0 * P, None, ALU.add))
                    n = 5 if moving else 1
                    dve.tensor_copy(at_i[:, 0:n], at[:, 0:n]).then_inc(computed, 1)
                    assert count_[0] == (STEP2 if moving else STEP1)

                STEP1, STEP2 = 12, 26
                with dve.Fori(0, T) as t:
                    sweep(t, False)
                dve.wait_ge(whole, 16)
                dve.tensor_tensor_scan(prefix[:, :], spread(net.ones[0:1, 0:1], [1, NPAD]), count[:, :], 0.0,
                                       ALU.mult, ALU.add).then_inc(prefixed, 1)
                dve.wait_ge(prefixed, 1)
                dve.tensor_tensor(prefix[:, :], prefix[:, :], count[:, :], ALU.subtract).then_inc(prefixed, 1)
                with dve.Fori(0, T) as t:
                    sweep(t, True)


def items(net, lay):
    nc = net.nc
    J = lay.cols
    one = lay is L1
    name = "l1" if one else "l0"
    with ExitStack() as ctx:
        def sb(what, shape, dt):
            return ctx.enter_context(nc.sbuf_tensor(f"{name}_{what}", shape, dt))

        (numbered, loaded, v_done, compared, counted, located, gathered, floats, rows_ready, stored, made, turned,
         copied, got_blocks) = sems(
            nc, name, "numbered", "loaded", "vector_done", "compared", "counted", "located", "gathered", "floats",
            "rows_ready", "stored", "made", "turned", "copied", "got_blocks")
        own = sb("own", [P, J, KW, P], I32)
        words = sb("words", [P, KW, J, P], F32)
        w1 = sb("w1", [P, J, P], F32)
        w2 = sb("w2", [P, J, P], F32)
        outs = [sb(f"out{n}", [P, J, P], F32) for n in range(4 if one else 2)]
        rows16 = sb("rows16", [P, J, P], F16)
        start16 = sb("start16", [P, J, P], BF16)
        before = sb("before", [P, JT, J * P], BF16)
        last_dst = sb("last_dst", [P, JT], I32)
        last = sb("last", [P, JT], F32)
        tiles = sb("tiles", [P, JT], F32)
        line = sb("line", [P, J * P], F32)
        number = sb("number", [P, J], F32)
        tile_of = sb("tile_of", [P, J], F32)
        which = sb("which", [P, 3, J], F32)
        which_i = sb("which_i", [P, 2, J], I32)
        tile_i = sb("tile_i", [P, J], I32)
        block_rows = nc.dram_tensor(f"{name}_block_rows", [2, J * P], I32).ap()
        ps = net.psum
        block = ctx.enter_context(nc.Block())

        @block.gpsimd
        def _(pool):
            for tile, pattern, step in ((tiles, [[P, JT]], 1), (number, [[P, J]], 1), (line, [[1, J * P]], 0)):
                pool.iota(tile[:, :], pattern, base=0, channel_multiplier=step,
                          allow_small_or_imprecise_dtypes=True).then_inc(numbered, 1)
            pool.wait_ge(located, 1)
            for j in range(J):
                pool.indirect_dma_start(own[:, j, :, :].rearrange("p k e -> p (k e)"), None, net.edges,
                                        bass.IndirectOffsetOnAxis(ap=tile_i[:, j:j + 1], axis=0))\
                    .then_inc(gathered, 16)

        @block.sync
        def _(sp):
            with nc.allow_non_contiguous_dma(reason="one word for each tile"):
                sp.dma_start(last_dst[:, :], net.edges.rearrange("(j p) c -> p j c", p=P)[:, :, P - 1])\
                    .then_inc(loaded, 16)
            sp.wait_ge(located, 2)
            with nc.allow_non_contiguous_dma(reason="one word for each item"):
                for k in range(2):
                    sp.dma_start(block_rows[k].rearrange("(j p) -> p j", p=P), which_i[:, k, :]).then_inc(stored, 16)
            sp.wait_ge(stored, 32)
            firsts = (net.groups1, net.blocks1) if one else (net.blocks0,)
            for k, tile in enumerate(firsts):
                sp.dma_start(tile[:, :], block_rows[k:k + 1, :]).then_inc(got_blocks, 16)
            sp.wait_ge(rows_ready, 1)
            sp.dma_start((net.key_rows if one else net.local_rows).rearrange("(j p e) -> p j e", p=P, e=P),
                         rows16[:, :, :]).then_inc(stored, 16)
            if one:
                sp.wait_ge(rows_ready, 2)
                sp.dma_start(net.start_rows.rearrange("(j p e) -> p j e", p=P, e=P), start16[:, :, :])\
                    .then_inc(stored, 16)
            sp.wait_ge(stored, 64 if one else 48)
            sp.wait_ge(got_blocks, 16 * len(firsts))

        @block.scalar
        def _(act):
            act.wait_ge(gathered, 16 * J)
            for k in range(KW if one else 2):
                act.copy(words[:, k, :, :], own[:, :, k, :]).then_inc(floats, 1)

        @block.vector
        def _(dve):
            done = [0]

            def chain(ins):
                done[0] += 1
                ins.then_inc(v_done, 1)
                dve.wait_ge(v_done, done[0])

            def quotient(dst, src, size):
                chain(dve.tensor_scalar(dst, src, 0.5, 1.0 / size, ALU.add, ALU.mult))
                chain(dve.tensor_scalar(dst, dst, -0.5, ROUND, ALU.add, ALU.add))
                chain(dve.tensor_scalar(dst, dst, -ROUND, None, ALU.add))

            dve.wait_ge(loaded, 16)
            dve.wait_ge(numbered, 3)
            chain(dve.tensor_copy(last[:, :], last_dst[:, :]))
            quotient(last[:, :], last[:, :], lay.size)
            chain(dve.tensor_scalar(last[:, :], last[:, :], float(lay.count - 1), None, ALU.min))
            chain(dve.tensor_tensor(last[:, :], last[:, :], tiles[:, :], ALU.add))
            for j in range(JT):
                dve.tensor_scalar(before[:, j, :], line[:, :], last[:, j:j + 1], None, ALU.is_gt)\
                    .then_inc(compared, 1)
            dve.wait_ge(counted, 1)
            chain(dve.tensor_scalar(tile_of[:, :], ps[:, 0:J], float(TPAD - 1), None, ALU.min))
            dve.tensor_copy(tile_i[:, :], tile_of[:, :]).then_inc(located, 1)
            chain(dve.tensor_tensor(which[:, 0, :], number[:, :], tile_of[:, :], ALU.subtract))
            chain(dve.tensor_scalar(which[:, 0, :], which[:, 0, :], float(lay.count - 1), None, ALU.min))
            quotient(which[:, 1, :], which[:, 0, :], SUBS if one else 1)
            dve.tensor_copy(which_i[:, :, :], which[:, 0:2, :]).then_inc(located, 1)
            chain(dve.tensor_scalar(which[:, 2, :], which[:, 1, :], -float(NODES), None, ALU.mult))
            chain(dve.tensor_scalar(which[:, 0, :], which[:, 0, :], -float(lay.size), None, ALU.mult))

            def less(first):
                return spread(first.unsqueeze(2), [P, J, P])

            dst, src, rel, prev = (words[:, k, :, :] for k in range(KW))
            dve.wait_ge(floats, 1)
            if one:
                sub, outside = w1[:, :, :], w2[:, :, :]
                chain(dve.tensor_tensor(sub, dst, less(which[:, 0, :]), ALU.add))
                chain(dve.tensor_scalar(outside, sub, 0.0, OUTSIDE, ALU.is_lt, ALU.mult))
                chain(dve.tensor_scalar(outs[1][:, :, :], sub, float(GROUP - 1), OUTSIDE, ALU.is_gt, ALU.mult))
                chain(dve.tensor_tensor(outside, outside, outs[1][:, :, :], ALU.add))
                dve.wait_ge(floats, 3)
                chain(dve.tensor_tensor(outs[1][:, :, :], rel, outside, ALU.add))
                chain(dve.scalar_tensor_tensor(out=outs[2][:, :, :], in0=sub, scalar=float(R),
                                               in1=outs[1][:, :, :], op0=ALU.mult, op1=ALU.add))
                dve.tensor_copy(rows16[:, :, :], outs[2][:, :, :]).then_inc(rows_ready, 1)
                chain(dve.tensor_tensor(outside, outside, dst, ALU.add))
                chain(dve.tensor_tensor(outs[0][:, :, :], outside, less(which[:, 2, :]), ALU.add))
                dve.wait_ge(floats, 4)
                chain(dve.tensor_tensor(w1[:, :, :], dst, prev, ALU.is_equal))
                dve.tensor_scalar(start16[:, :, :], w1[:, :, :], -1.0, BIG, ALU.add, ALU.mult)\
                    .then_inc(rows_ready, 1)
            else:
                chain(dve.tensor_tensor(outs[0][:, :, :], dst, less(which[:, 2, :]), ALU.add))
                dve.tensor_copy(rows16[:, :, :], outs[0][:, :, :]).then_inc(rows_ready, 1)
            dve.wait_ge(floats, 2)
            quotient(w2[:, :, :], src, NODES)
            row = w2 if one else outs[1]
            chain(dve.scalar_tensor_tensor(out=row[:, :, :], in0=w2[:, :, :], scalar=float(P - NODES), in1=src,
                                           op0=ALU.mult, op1=ALU.add))
            if one:
                chain(dve.scalar_tensor_tensor(out=outs[3][:, :, :], in0=row[:, :, :], scalar=float(R), in1=rel,
                                               op0=ALU.mult, op1=ALU.add))
            dve.sem_inc(made, 1)
            for n, out in enumerate((net.local1, net.rel, net.key, net.src1) if one else (net.local0, net.src0)):
                base = (n % 2) * 2 * BANK
                dve.wait_ge(turned, n + 1)
                dve.tensor_copy(out[:, :], ps[:, base:base + J * P]).then_inc(copied, 1)

        @block.tensor
        def _(pe):
            pe.wait_ge(compared, JT)
            for c in range(J):
                for j in range(JT):
                    mm = pe.matmul(ps[:, c:c + 1], before[:, j, c * P:(c + 1) * P], net.ones16[:, 0:1],
                                   start=(j == 0), stop=(j == JT - 1))
            mm.then_inc(counted, 1)
            pe.wait_ge(made, 1)
            for n, tile in enumerate(outs):
                if n >= 2:
                    pe.wait_ge(copied, n - 1)
                for j in range(J):
                    base = (n % 2) * 2 * BANK + j * P
                    mm = pe.transpose(ps[:, base:base + P], tile[:, j, :], net.ident[:, :])
                mm.then_inc(turned, 1)


def layer_norm_stats(dve, net, src, stats, aggr, turn):
    over_blocks(dve, lambda b, k, first: dve.bn_stats(block_of(net.st, b), block_of(src, b)).then_inc(stats, 1))
    dve.wait_ge(stats, NB * turn)
    st, mv, tmp = net.st, net.mv, net.tmp
    mean, var, half, both = mv[:, :, 0], mv[:, :, 1], tmp[:, 0, :], tmp[:, 1, :]
    steps = (
        lambda: dve.tensor_tensor(mean, st[:, :, 1], st[:, :, 4], ALU.add),
        lambda: dve.tensor_tensor(half, st[:, :, 1], st[:, :, 4], ALU.subtract),
        lambda: dve.tensor_tensor(both, st[:, :, 2], st[:, :, 5], ALU.add),
        lambda: dve.tensor_scalar(mean, mean, 0.5, None, ALU.mult),
        lambda: dve.tensor_tensor(half, half, half, ALU.mult),
        lambda: dve.tensor_scalar(both, both, 1.0 / D, None, ALU.mult),
        lambda: dve.scalar_tensor_tensor(out=var, in0=half, scalar=0.25, in1=both, op0=ALU.mult, op1=ALU.add),
    )
    for n, step in enumerate(steps):
        if n >= 3:
            dve.wait_ge(aggr, len(steps) * (turn - 1) + n - (0 if n == 6 else 2))
        step().then_inc(aggr, 1)


AGGR = 7


def layer_norm_scale(dve, net, std_ready, scale_ready, turn):
    dve.wait_ge(std_ready, turn)
    dve.reciprocal(net.rstd[:, :], net.rstd[:, :]).then_inc(scale_ready, 1)
    dve.wait_ge(scale_ready, 2 * turn - 1)
    dve.scalar_tensor_tensor(out=net.shift[:, :], in0=net.mv[:, :, 0], scalar=-1.0, in1=net.rstd[:, :],
                             op0=ALU.mult, op1=ALU.mult).then_inc(scale_ready, 1)


def layer_norm_std(act, net, eps, aggr, std_ready, turn):
    act.wait_ge(aggr, AGGR * turn)
    act.activation(net.rstd[:, :], net.mv[:, :, 1], ACT.Sqrt, bias=eps[:, 0:1], scale=1.0).then_inc(std_ready, 1)


def normalize(act, net, dst, src, func, scale_ready, turn, normed):
    act.wait_ge(scale_ready, 2 * turn)
    over_blocks(act, lambda b, k, first: act.activation(
        dst[:, cols(b, 1), :].rearrange("p b d -> p (b d)"), src[:, cols(b, 1), :].rearrange("p b d -> p (b d)"),
        func, bias=net.shift[:, cols(b, 1)], scale=net.rstd[:, cols(b, 1)]).then_inc(normed, 1))


def block_of(tile, b):
    return tile[:, cols(b, 1), :].rearrange("p b d -> p (b d)")


def split3(dve, hi, mid, lo, src, rest, ready, base):
    dve.tensor_copy(hi, src).then_inc(ready, 1)
    dve.wait_ge(ready, base + 1)
    dve.tensor_tensor(rest, src, hi, ALU.subtract).then_inc(ready, 1)
    dve.wait_ge(ready, base + 2)
    dve.tensor_copy(mid, rest).then_inc(ready, 1)
    dve.wait_ge(ready, base + 3)
    dve.tensor_tensor(lo, rest, mid, ALU.subtract).then_inc(ready, 1)


def nodes0(net, q0):
    nc, a = net.nc, net.a
    with ExitStack() as ctx:
        def sb(name, shape, dt):
            return ctx.enter_context(nc.sbuf_tensor(name, shape, dt))

        (blank, x_loaded, w_loaded, stats, aggr, std_ready, scale_ready, normed, turned, copied, product,
         evacuated, parts, store0, store1) = sems(
            nc, "n0", "blank", "x_loaded", "w_loaded", "stats", "aggr", "std_ready", "scale_ready", "normed",
            "turned", "copied", "product", "evacuated", "parts", "store0", "store1")
        w = sb("w_qkv0", [P, 3 * D], F32)
        eps = sb("eps", [P, 1], F32)
        ht = sb("ht", [P, 2, P], F32)
        qkv = sb("qkv", [P, 2, 3 * D], F32)
        rest = sb("rest", [P, D], F32)
        stores = (store0, store1)
        ps = net.psum
        block = ctx.enter_context(nc.Block())

        @block.gpsimd
        def _(pool):
            pool.memset(net.x[:, :, :], 0.0).then_inc(blank, 1)
            pool.memset(eps[:, :], EPS).then_inc(blank, 1)

        @block.sync
        def _(sp):
            x = a["x"]
            sp.wait_ge(blank, 1)
            for b in range(0, NB, NB // 5):
                sp.dma_start(net.x[0:NODES, b:b + NB // 5, :],
                             x[b * NODES:(b + NB // 5) * NODES, :].rearrange("(b p) d -> p b d", p=NODES))\
                    .then_inc(x_loaded, 16)
            for j, name in enumerate(("L0_gnn_Wq", "L0_gnn_Wk", "L0_gnn_Wv")):
                sp.dma_start(w[:, j * D:(j + 1) * D], a[name]).then_inc(w_loaded, 16)

            def store(b, k, first):
                sp.wait_ge(evacuated, b + 1)
                sp.dma_start(net.kv0[cols(b * P, P), :], qkv[:, k, D:3 * D]).then_inc(stores[k], 16)

            over_blocks(sp, store)
            sp.wait_ge(store0, 16 * ((NB + 1) // 2))
            sp.wait_ge(store1, 16 * (NB // 2))

        @block.vector
        def _(dve):
            dve.wait_ge(x_loaded, 80)
            layer_norm_stats(dve, net, net.x, stats, aggr, 1)
            layer_norm_scale(dve, net, std_ready, scale_ready, 1)

            def split(b, k, first):
                dve.wait_ge(evacuated, b + 1)
                part = [q0[:, cols(b * (3 * D) + s * D, D)] for s in range(3)]
                split3(dve, *part, qkv[:, k, 0:D], rest[:, :], parts, b * 4)

            over_blocks(dve, split)

        @block.scalar
        def _(act):
            act.wait_ge(blank, 2)
            layer_norm_std(act, net, eps, aggr, std_ready, 1)
            normalize(act, net, net.h, net.x, ACT.Relu, scale_ready, 1, normed)

            def evacuate(b, k, first):
                act.wait_ge(turned, b + 1)
                act.copy(ht[:, k, :], ps[:, k * BANK:k * BANK + P]).then_inc(copied, 1)
                act.wait_ge(product, b + 1)
                if not first:
                    act.wait_ge(parts, (b - 1) * 4)
                    act.wait_ge(stores[k], (b - k) * 8)
                act.copy(qkv[:, k, :], ps[:, (2 + k) * BANK:(2 + k) * BANK + 3 * D]).then_inc(evacuated, 1)

            over_blocks(act, evacuate)

        @block.tensor
        def _(pe):
            pe.wait_ge(w_loaded, 48)

            def project(b, k, first):
                pe.wait_ge(normed, b + 1)
                if not first:
                    pe.wait_ge(copied, b - 1)
                pe.transpose(ps[:, k * BANK:k * BANK + P], block_of(net.h, b), net.ident[:, :]).then_inc(turned, 1)
                pe.wait_ge(copied, b + 1)
                if not first:
                    pe.wait_ge(evacuated, b - 1)
                pe.matmul(ps[:, (2 + k) * BANK:(2 + k) * BANK + 3 * D], ht[:, k, :], w[:, :],
                          start=True, stop=True).then_inc(product, 1)

            over_blocks_unrolled(pe, project)


def clear_banks(pe, net, n):
    for k in range(n):
        last = pe.matmul(net.psum[:, k * BANK:(k + 1) * BANK], net.zeros[:, 0:P], net.zeros[:, :],
                         start=True, stop=False, skip_group_check=True)
    return last


def block_registers(nc, row, n, most, g=G):
    _, v = nc.values_load_multi_w_load_instructions(
        row[0:1, cols(n * g, g)], engines=[PE], min_val=0, max_val=most,
        skip_runtime_bounds_check_because="blocks of items are clamped when they are made")
    return v


def edges0(net, q0):
    nc = net.nc
    Z = NB * D
    with ExitStack() as ctx:
        def sb(name, shape, dt):
            return ctx.enter_context(nc.sbuf_tensor(name, shape, dt))

        (passed_pool, idx_ready, onehot_t, onehot, queries, prod_ready, score_ready, clipped, exp_ready, msg_ready, added,
         ) = sems(nc, "m0", "passed_pool", "idx_ready", "onehot_t", "onehot", "queries", "prod_ready", "score_ready",
                  "clipped", "exp_ready", "msg_ready", "added")
        gathered = sems(nc, "m0", *[f"gathered{s}" for s in range(RING)])
        rows_loaded = sems(nc, "m0", *[f"rows_loaded{s}" for s in range(RING)])
        kv = sb("kv", [P, RING, G, 2 * D], F32)
        idx = sb("idx", [P, RING, G], I32)
        rows = sb("rows", [P, RING, GP], F16)
        oht = sb("oht", [P, 2, GP], BF16)
        oh = sb("oh", [P, RING, G, P], F32)
        prod = sb("prod", [P, 2, GP], F32)
        score = sb("score", [P, 2, G * H], F32)
        clip = sb("clip", [P, 2, G * H], F32)
        msg = sb("msg", [P, RING, G, D + H], F32)
        qe = net.psum[:, 7 * BANK:8 * BANK]
        block = ctx.enter_context(nc.Block())

        @block.gpsimd
        def _(pool):
            def gather(n, s, turn):
                pool.wait_ge(idx_ready, n + 1)
                if there(n - RING):
                    pool.wait_ge(msg_ready, n - (RING - 1))
                settle(pool, passed_pool)
                for i in range(G):
                    pool.indirect_dma_start(kv[:, s, i, :], None, net.kv0,
                                            bass.IndirectOffsetOnAxis(ap=idx[:, s, i:i + 1], axis=0))\
                        .then_inc(gathered[s], 16)

            over_turns(pool, L0.steps, gather)

        @block.sync
        def _(sp):
            def load(n, s, turn):
                if there(n - RING):
                    sp.wait_ge(onehot_t, n - (RING - 1))
                sp.dma_start(rows[:, s, :], net.local_rows[cols(n * GP, GP)].partition_broadcast(P))\
                    .then_inc(rows_loaded[s], 16)

            over_turns(sp, L0.steps, load)

        @block.scalar
        def _(act):
            for s in range(RING):
                act.copy(idx[:, s, :], net.src0[:, s * G:(s + 1) * G]).then_inc(idx_ready, 1)

            def exps(m, s):
                act.wait_ge(clipped, m + 1)
                act.activation(msg[:, s, :, D:D + H], clip[:, s % 2, :].rearrange("p (g h) -> p g h", h=H),
                               ACT.Exp, scale=1.0 / 4).then_inc(exp_ready, 1)

            def step(n, s, turn):
                act.wait_ge(gathered[s], (turn + 1) * (16 * G))
                act.copy(idx[:, s, :], net.src0[:, cols(n * G + TURN, G)]).then_inc(idx_ready, 1)
                if there(n - 1):
                    exps(n - 1, (s - 1) % RING)

            over_turns(act, L0.steps, step)
            exps(L0.steps - 1, RING - 1)

        @block.vector
        def _(dve):
            def onehots(n, s, turn):
                dve.wait_ge(rows_loaded[s], (turn + 1) * 16)
                if there(n - 2):
                    dve.wait_ge(queries, n - 1)
                dve.tensor_scalar(oht[:, s % 2, :], rows[:, s, :], net.part1[:, 0:1], None, ALU.is_equal)\
                    .then_inc(onehot_t, 1)
                if there(n - RING):
                    dve.wait_ge(added, n - (RING - 1))
                dve.tensor_tensor(oh[:, s, :, :], spread(net.lane[:, :].unsqueeze(1), [P, G, P]),
                                  spread(net.local0[:, cols(n * G, G)].unsqueeze(2), [P, G, P]), ALU.is_equal)\
                    .then_inc(onehot, 1)

            def scores(m, s, turn):
                dve.wait_ge(queries, m + 1)
                dve.wait_ge(gathered[s], turn)
                dve.tensor_tensor(prod[:, s % 2, :].rearrange("p (g d) -> p g d", d=D), kv[:, s, :, 0:D],
                                  qe.rearrange("p (g d) -> p g d", d=D), ALU.mult).then_inc(prod_ready, 1)
                dve.wait_ge(prod_ready, m + 1)
                dve.tensor_reduce(score[:, s % 2, :], prod[:, s % 2, :].rearrange("p (g d) -> p g d", d=DH),
                                  AX_X, ALU.add).then_inc(score_ready, 1)
                dve.wait_ge(score_ready, m + 1)
                dve.tensor_scalar(clip[:, s % 2, :], score[:, s % 2, :], -5.0 * 4, 5.0 * 4, ALU.max, ALU.min)\
                    .then_inc(clipped, 1)

            def messages(m, s):
                dve.wait_ge(exp_ready, m + 1)
                dve.tensor_tensor(msg[:, s, :, 0:D].rearrange("p g (h d) -> p g h d", d=DH),
                                  kv[:, s, :, D:2 * D].rearrange("p g (h d) -> p g h d", d=DH),
                                  spread(msg[:, s, :, D:D + H].unsqueeze(3), [P, G, H, DH]), ALU.mult)\
                    .then_inc(msg_ready, 1)

            def step(n, s, turn):
                onehots(n, s, turn)
                if there(n - 1):
                    scores(n - 1, (s - 1) % RING, (turn + 1 if s else turn) * (16 * G))
                if there(n - 2):
                    messages(n - 2, (s - 2) % RING)

            over_turns(dve, L0.steps, step)
            scores(L0.steps - 1, RING - 1, L0.turns * 16 * G)
            messages(L0.steps - 2, RING - 2)
            messages(L0.steps - 1, RING - 1)

        @block.tensor
        def _(pe):
            clear_banks(pe, net, 7)

            def expand(n, s):
                blocks = block_registers(nc, net.blocks0, n, NB - 1)
                pe.wait_ge(onehot_t, n + 1)
                if there(n - 1):
                    pe.wait_ge(prod_ready, n)
                for i in range(G):
                    for part in range(3):
                        last = pe.matmul(qe[:, i * D:(i + 1) * D], oht[:, s % 2, i * P:(i + 1) * P],
                                         q0[:, cols(blocks[i] * (3 * D) + part * D, D)],
                                         start=(part == 0), stop=(part == 2))
                last.then_inc(queries, 1)

            def add(m, s):
                blocks = block_registers(nc, net.blocks0, m, NB - 1)
                pe.wait_ge(onehot, m + 1)
                pe.wait_ge(msg_ready, m + 1)
                for i in range(G):
                    pe.matmul(net.psum[:, cols(blocks[i] * D, D)], oh[:, s, i, :], msg[:, s, i, 0:D],
                              start=False, stop=False, skip_group_check=True)
                    last = pe.matmul(net.psum[:, cols(blocks[i] * H + Z, H)], oh[:, s, i, :], msg[:, s, i, D:D + H],
                                     start=False, stop=False, skip_group_check=True)
                last.then_inc(added, 1)

            def step(n, s, turn):
                expand(n, s)
                if there(n - 2):
                    add(n - 2, (s - 2) % RING)

            over_turns(pe, L0.steps, step)
            add(L0.steps - 2, RING - 2)
            add(L0.steps - 1, RING - 1)


def nodes1(net):
    nc, a = net.nc, net.a
    Z = NB * D
    with ExitStack() as ctx:
        def sb(name, shape, dt):
            return ctx.enter_context(nc.sbuf_tensor(name, shape, dt))

        (w_loaded, r_loaded, v_done, turned, copied, product, taken, stats, aggr, std_ready, scale_ready, normed,
         ready, hidden, relued, evacuated, parts, store0, store1, blank) = sems(
            nc, "n1", "w_loaded", "r_loaded", "vector_done", "turned", "copied", "product", "taken", "stats",
            "aggr", "std_ready", "scale_ready", "normed", "ready", "hidden", "relued", "evacuated", "parts",
            "store0", "store1", "blank")
        banked, = sems(nc, "n1", "banked")
        wo = sb("wo", [P, D], F32)
        w1 = sb("w1_", [P, DFF], F32)
        w2 = sb("w2_", [P, 2, D], F32)
        wr = sb("wr", [P, R, 3, D], F32)
        b1 = sb("b1", [P, 2], F32)
        names = ("L0_gnn_bo", "L0_gnn_ln1_g", "L0_gnn_ln1_b", "L0_gnn_b2", "L0_gnn_ln2_g", "L0_gnn_ln2_b")
        vec = sb("vec", [P, len(names), D], F32)
        eps = sb("eps1", [P, 1], F32)
        t1 = sb("t1", [P, NB, D], F32)
        at = sb("at", [P, 2, P], F32)
        f1 = sb("f1", [P, 2, 2, P], F32)
        zr = sb("zr", [P, NB * H], F32)
        qkv = sb("qkv1", [P, 2, R, 3 * D], F32)
        rest = sb("rest1", [P, R * D], F32)
        q_parts = sb("q_parts", [P, 2, R, 3, D], BF16)
        stores = (store0, store1)
        ps = net.psum
        ALL = [P, NB, D]

        def row(j):
            return spread(vec[:, j, :].unsqueeze(1), ALL)

        block = ctx.enter_context(nc.Block())

        @block.sync
        def _(sp):
            sp.dma_start(wo[:, :], a["L0_gnn_Wo"]).then_inc(w_loaded, 16)
            sp.dma_start(w1[:, :], a["L0_gnn_W1"]).then_inc(w_loaded, 16)
            sp.dma_start(w2[:, :, :], a["L0_gnn_W2"].rearrange("(c p) d -> p c d", p=P)).then_inc(w_loaded, 16)
            with nc.allow_non_contiguous_dma(reason="a short column"):
                sp.dma_start(b1[:, :], a["L0_gnn_b1"].rearrange("(c p) -> p c", p=P)).then_inc(w_loaded, 16)
            for j, name in enumerate(names):
                sp.dma_start(vec[:, j, :], a[name].partition_broadcast(P)).then_inc(w_loaded, 16)
            for j, name in enumerate(("L1_gnn_W_Q", "L1_gnn_W_K", "L1_gnn_W_V")):
                for r in range(R):
                    sp.dma_start(wr[:, r, j, :].rearrange("p (h d) -> p h d", d=DH),
                                 a[name][r].rearrange("h p d -> p h d")).then_inc(r_loaded, 16)

            def store(b, k, first):
                sp.wait_ge(evacuated, (b + 1) * R)
                sp.dma_start(net.kv1[cols(b * (P * R), P * R), :].rearrange("(p r) c -> p r c", r=R),
                             qkv[:, k, :, D:3 * D]).then_inc(stores[k], 16)
                sp.wait_ge(parts, (b + 1) * 4)
                sp.dma_start(net.q1_parts[cols(b * (P * R), P * R), :].rearrange("(p r) c -> p (r c)", r=R),
                             q_parts[:, k, :, :, :].rearrange("p r s d -> p (r s d)")).then_inc(stores[k], 16)

            over_blocks(sp, store)
            sp.wait_ge(store0, 32 * ((NB + 1) // 2))
            sp.wait_ge(store1, 32 * (NB // 2))

        @block.gpsimd
        def _(pool):
            pool.memset(eps[:, :], EPS).then_inc(blank, 1)

        @block.vector
        def _(dve):
            done = [0]

            def chain(ins):
                done[0] += 1
                ins.then_inc(v_done, 1)
                dve.wait_ge(v_done, done[0])

            def signal(ins, n):
                ins.then_inc(ready, 1)
                dve.wait_ge(ready, n)

            chain(dve.tensor_scalar(zr[:, :], ps[:, Z:Z + NB * H], 1e-6, None, ALU.add))
            chain(dve.reciprocal(zr[:, :], zr[:, :]))
            dve.tensor_tensor(t1[:, :, :].rearrange("p b (h d) -> p (b h) d", d=DH),
                              ps[:, 0:NB * D].rearrange("p (n d) -> p n d", d=DH),
                              spread(zr[:, :].unsqueeze(2), [P, NB * H, DH]), ALU.mult).then_inc(ready, 1)
            dve.wait_ge(w_loaded, 16 * (4 + len(names)))
            chain(dve.tensor_tensor(net.h[:, :, :], net.h[:, :, :], row(0), ALU.add))

            def take(b, k, first):
                dve.wait_ge(product, b + 1)
                dve.tensor_tensor(block_of(net.h, b), ps[:, (2 + k) * BANK:(2 + k) * BANK + D],
                                  block_of(net.h, b), ALU.add).then_inc(taken, 1)

            over_blocks(dve, take)
            dve.wait_ge(taken, NB)
            layer_norm_stats(dve, net, net.h, stats, aggr, 1)
            layer_norm_scale(dve, net, std_ready, scale_ready, 1)
            dve.wait_ge(normed, NB)
            chain(dve.tensor_tensor(t1[:, :, :], t1[:, :, :], row(1), ALU.mult))
            signal(dve.tensor_tensor(t1[:, :, :], t1[:, :, :], row(2), ALU.add), 2)
            chain(dve.tensor_tensor(net.h[:, :, :], t1[:, :, :], row(3), ALU.add))

            def take2(b, k, first):
                dve.wait_ge(product, b + (NB + 1))
                dve.tensor_tensor(block_of(net.h, b), ps[:, (6 + k) * BANK:(6 + k) * BANK + D],
                                  block_of(net.h, b), ALU.add).then_inc(taken, 1)

            over_blocks(dve, take2)
            dve.wait_ge(taken, 2 * NB)
            layer_norm_stats(dve, net, net.h, stats, aggr, 2)
            layer_norm_scale(dve, net, std_ready, scale_ready, 2)
            dve.wait_ge(normed, 2 * NB)
            chain(dve.tensor_tensor(t1[:, :, :], t1[:, :, :], row(4), ALU.mult))
            chain(dve.tensor_tensor(t1[:, :, :], t1[:, :, :], row(5), ALU.add))
            signal(dve.tensor_tensor(net.x[:, :, :], t1[:, :, :], net.x[:, :, :], ALU.add), 3)
            layer_norm_stats(dve, net, net.x, stats, aggr, 3)
            layer_norm_scale(dve, net, std_ready, scale_ready, 3)

            def split(b, k, first):
                dve.wait_ge(evacuated, (b + 1) * R)
                if not first:
                    dve.wait_ge(stores[k], (b - k) * 16)
                part = [q_parts[:, k, :, s, :] for s in range(3)]
                split3(dve, *part, qkv[:, k, :, 0:D], rest[:, :].rearrange("p (r d) -> p r d", d=D), parts, b * 4)

            over_blocks(dve, split)

        @block.scalar
        def _(act):
            act.wait_ge(blank, 1)

            def copy(b, k, first):
                act.wait_ge(turned, b + 1)
                act.copy(at[:, k, :], ps[:, k * BANK:k * BANK + P]).then_inc(copied, 1)

            over_blocks(act, copy)
            layer_norm_std(act, net, eps, aggr, std_ready, 1)
            normalize(act, net, t1, net.h, ACT.Identity, scale_ready, 1, normed)

            def ff(b, k, first, do=(True, True)):
                if do[0]:
                    act.wait_ge(turned, b + (NB + 1))
                    act.copy(at[:, k, :], ps[:, k * BANK:k * BANK + P]).then_inc(copied, 1)
                if do[1] and there(b - 1):
                    j = 1 - k
                    act.wait_ge(hidden, b)
                    for c in range(2):
                        act.activation(f1[:, j, c, :], ps[:, (4 + j) * BANK + c * P:(4 + j) * BANK + (c + 1) * P],
                                       ACT.Relu, bias=b1[:, c:c + 1], scale=1.0).then_inc(relued, 1)

            over_blocks(act, ff)
            ff(NB, 1, False, (False, True))
            layer_norm_std(act, net, eps, aggr, std_ready, 2)
            normalize(act, net, t1, net.h, ACT.Identity, scale_ready, 2, normed)
            layer_norm_std(act, net, eps, aggr, std_ready, 3)
            normalize(act, net, net.h, net.x, ACT.Relu, scale_ready, 3, normed)

            def evacuate(b, k, first):
                act.wait_ge(turned, b + (2 * NB + 1))
                act.copy(at[:, k, :], ps[:, k * BANK:k * BANK + P]).then_inc(copied, 1)
                if not first:
                    act.wait_ge(parts, (b - 1) * 4)
                    act.wait_ge(stores[k], (b - k) * 16)
                for r in range(R):
                    act.wait_ge(banked, b * R + (r + 1))
                    act.copy(qkv[:, k, r, :], ps[:, (2 + r) * BANK:(2 + r) * BANK + 3 * D]).then_inc(evacuated, 1)

            over_blocks(act, evacuate)

        @block.tensor
        def _(pe):
            pe.wait_ge(ready, 1)
            pe.wait_ge(w_loaded, 16 * (4 + len(names)))

            def out_proj(b, k, first):
                if not first:
                    pe.wait_ge(copied, b - 1)
                pe.transpose(ps[:, k * BANK:k * BANK + P], block_of(t1, b), net.ident[:, :]).then_inc(turned, 1)
                pe.wait_ge(copied, b + 1)
                if not first:
                    pe.wait_ge(taken, b - 1)
                pe.matmul(ps[:, (2 + k) * BANK:(2 + k) * BANK + D], at[:, k, :], wo[:, :], start=True, stop=True)\
                    .then_inc(product, 1)

            over_blocks_unrolled(pe, out_proj)
            pe.wait_ge(ready, 2)

            def ff(b, k, first, do=(True, True, True)):
                j = 1 - k
                if do[0]:
                    if not first:
                        pe.wait_ge(copied, b + (NB - 1))
                    pe.transpose(ps[:, k * BANK:k * BANK + P], block_of(t1, b), net.ident[:, :])\
                        .then_inc(turned, 1)
                if do[1] and there(b - 1):
                    pe.wait_ge(copied, b + NB)
                    if there(b - 3):
                        pe.wait_ge(relued, (b - 2) * 2)
                    for c in range(2):
                        last = pe.matmul(ps[:, (4 + j) * BANK + c * P:(4 + j) * BANK + (c + 1) * P],
                                         w1[:, c * P:(c + 1) * P], at[:, j, :], start=True, stop=True)
                    last.then_inc(hidden, 1)
                if do[2] and there(b - 2):
                    pe.wait_ge(relued, (b - 1) * 2)
                    if there(b - 4):
                        pe.wait_ge(taken, b + (NB - 3))
                    for c in range(2):
                        last = pe.matmul(ps[:, (6 + k) * BANK:(6 + k) * BANK + D], f1[:, k, c, :], w2[:, c, :],
                                         start=(c == 0), stop=(c == 1))
                    last.then_inc(product, 1)

            over_blocks_unrolled(pe, ff)
            ff(NB, 1, False, (False, True, True))
            ff(NB + 1, 0, False, (False, False, True))
            pe.wait_ge(r_loaded, 16 * 3 * R)
            pe.wait_ge(taken, 2 * NB)

            def project(b, k, first):
                pe.wait_ge(normed, b + (2 * NB + 1))
                if not first:
                    pe.wait_ge(copied, b + (2 * NB - 1))
                pe.transpose(ps[:, k * BANK:k * BANK + P], block_of(net.h, b), net.ident[:, :]).then_inc(turned, 1)
                pe.wait_ge(copied, b + (2 * NB + 1))
                for r in range(R):
                    if there(b - 1):
                        pe.wait_ge(evacuated, b * R + (r + 1 - R))
                    pe.matmul(ps[:, (2 + r) * BANK:(2 + r) * BANK + 3 * D], at[:, k, :],
                              wr[:, r, :, :].rearrange("p a d -> p (a d)"), start=True, stop=True)\
                        .then_inc(banked, 1)

            over_blocks_unrolled(pe, project)


def logits1(net, q1):
    nc, a = net.nc, net.a
    CHUNKS = 5
    BC = NB // CHUNKS
    assert BC * CHUNKS == NB and TURN <= SUBS * BC
    with ExitStack() as ctx:
        def sb(name, shape, dt):
            return ctx.enter_context(nc.sbuf_tensor(name, shape, dt))

        (passed_pool, passed_pe, idx_ready, onehot_t, queries, prod_ready, score_ready, mask_ready, bias_ready, logit_ready, turned,
         scanned, b_loaded, blank) = sems(
            nc, "m1", "passed_pool", "passed_pe", "idx_ready", "onehot_t", "queries", "prod_ready", "score_ready", "mask_ready",
            "bias_ready", "logit_ready", "turned", "scanned", "b_loaded", "blank")
        gathered = sems(nc, "m1", *[f"gathered{s}" for s in range(RING)])
        rows_loaded = sems(nc, "m1", *[f"rows_loaded{s}" for s in range(RING)])
        starts_loaded = sems(nc, "m1", *[f"starts_loaded{s}" for s in range(RING)])
        v_stored = sems(nc, "m1", *[f"v_stored{s}" for s in range(RING)])
        l_stored = sems(nc, "m1", *[f"l_stored{s}" for s in range(RING)])
        m_stored = sems(nc, "m1", *[f"m_stored{s}" for s in range(RING)])
        q_loaded = sems(nc, "m1", *[f"q_loaded{c}" for c in range(CHUNKS)])
        kv = sb("kv_", [P, RING, G, 2 * D], F32)
        idx = sb("idx_", [P, RING, G], I32)
        rows = sb("rows_", [P, RING, GP], F16)
        starts = sb("starts", [RH, RING, GP], BF16)
        oht = sb("oht_", [P, 2, GP], BF16)
        prod = sb("prod_", [P, 2, GP], F32)
        score = sb("score_", [P, 2, G * H], F32)
        mask = sb("mask", [P, 2, G * R], F32)
        bias = sb("bias", [P, RH], F32)
        shifted = sb("shifted", [P, 2, G, RH], F32)
        logit = sb("logit", [P, RING, G, RH], F32)
        top = sb("top", [RH, RING, GP], F32)
        low = sb("low", [P, 1], F32)
        ps = net.psum
        block = ctx.enter_context(nc.Block())

        @block.gpsimd
        def _(pool):
            pool.memset(low[:, :], -BIG).then_inc(blank, 1)

            def gather(n, s, turn):
                pool.wait_ge(idx_ready, n + 1)
                if there(n - RING):
                    pool.wait_ge(prod_ready, n - (RING - 1))
                    pool.wait_ge(v_stored[s], turn * 16)
                settle(pool, passed_pool)
                for i in range(G):
                    pool.indirect_dma_start(kv[:, s, i, :], None, net.kv1,
                                            bass.IndirectOffsetOnAxis(ap=idx[:, s, i:i + 1], axis=0))\
                        .then_inc(gathered[s], 16)

            over_turns(pool, L1.steps, gather)

        @block.sync
        def _(sp):
            sp.dma_start(bias[:, :], a["L1_gnn_attn_bias"].rearrange("r h -> (r h)").partition_broadcast(P))\
                .then_inc(b_loaded, 16)

            def load_queries(c):
                b = slice(c * BC, (c + 1) * BC)
                for j in range(SUBS):
                    sp.dma_start(q1[:, :].rearrange("p (b j c) -> p b j c", j=SUBS, c=3 * D)[:, b, j, :],
                                 net.q1_parts.rearrange("(b q) c -> q b c", q=P * R)
                                 [j * GROUP * R:j * GROUP * R + P, b, :]).then_inc(q_loaded[c], 16)

            def load(n, s, turn):
                if isinstance(n, int) and s == 0:
                    for c in range(CHUNKS):
                        load_queries(c)
                if there(n - RING):
                    sp.wait_ge(onehot_t, n - (RING - 1))
                sp.dma_start(rows[:, s, :], net.key_rows[cols(n * GP, GP)].partition_broadcast(P))\
                    .then_inc(rows_loaded[s], 16)
                if there(n - RING):
                    sp.wait_ge(scanned, n - (RING - 1))
                sp.dma_start(starts[:, s, :], net.start_rows[cols(n * GP, GP)].partition_broadcast(RH))\
                    .then_inc(starts_loaded[s], 16)

            over_turns(sp, L1.steps, load)

        @block.scalar
        def _(act):
            for s in range(RING):
                act.copy(idx[:, s, :], net.src1[:, s * G:(s + 1) * G]).then_inc(idx_ready, 1)

            def store_logits(m, s):
                act.wait_ge(logit_ready, m + 1)
                act.dma_start(net.l_spill[cols(m, 1), :, :].rearrange("a p c -> p (a c)"),
                              logit[:, s, :, :].rearrange("p g c -> p (g c)")).then_inc(l_stored[s], 16)

            def store_maxima(m, s):
                act.wait_ge(scanned, m + 1)
                act.dma_start(net.m_spill[cols(m, 1), :, :].rearrange("a p c -> p (a c)"), top[:, s, :])\
                    .then_inc(m_stored[s], 16)

            def step(n, s, turn):
                act.wait_ge(gathered[s], (turn + 1) * (16 * G))
                act.copy(idx[:, s, :], net.src1[:, cols(n * G + TURN, G)]).then_inc(idx_ready, 1)
                act.dma_start(net.v_spill[cols(n, 1), :, :, :].rearrange("a p g d -> p (a g) d"),
                              kv[:, s, :, D:2 * D]).then_inc(v_stored[s], 16)
                if there(n - 1):
                    store_logits(n - 1, (s - 1) % RING)
                if there(n - 2):
                    store_maxima(n - 2, (s - 2) % RING)

            over_turns(act, L1.steps, step)
            store_logits(L1.steps - 1, RING - 1)
            store_maxima(L1.steps - 2, RING - 2)
            store_maxima(L1.steps - 1, RING - 1)
            for s in range(RING):
                for stored in (v_stored, l_stored, m_stored):
                    act.wait_ge(stored[s], 16 * L1.turns)

        @block.vector
        def _(dve):
            dve.wait_ge(b_loaded, 16)
            dve.wait_ge(blank, 1)

            def onehots(n, s, turn):
                dve.wait_ge(rows_loaded[s], (turn + 1) * 16)
                if there(n - 2):
                    dve.wait_ge(queries, n - 1)
                dve.tensor_scalar(oht[:, s % 2, :], rows[:, s, :], net.part1[:, 0:1], None, ALU.is_equal)\
                    .then_inc(onehot_t, 1)

            def scores(m, s, turn):
                o = s % 2
                dve.tensor_tensor(mask[:, o, :].rearrange("p (g r) -> p g r", r=R),
                                  spread(net.rel[:, cols(m * G, G)].unsqueeze(2), [P, G, R]),
                                  spread(net.lane[:, 0:R].unsqueeze(1), [P, G, R]), ALU.not_equal)\
                    .then_inc(mask_ready, 1)
                dve.wait_ge(queries, m + 1)
                dve.wait_ge(gathered[s], (turn + 1) * (16 * G))
                dve.scalar_tensor_tensor(out=prod[:, o, :].rearrange("p (g d) -> p g d", d=D), in0=kv[:, s, :, 0:D],
                                         scalar=DH ** -0.5,
                                         in1=ps[:, o * BANK:(o + 1) * BANK].rearrange("p (g d) -> p g d", d=D),
                                         op0=ALU.mult, op1=ALU.mult).then_inc(prod_ready, 1)
                dve.wait_ge(mask_ready, m + 1)
                dve.scalar_tensor_tensor(
                    out=shifted[:, o, :, :].rearrange("p g (r h) -> p g r h", h=H),
                    in0=spread(mask[:, o, :].rearrange("p (g r) -> p g r", r=R).unsqueeze(3), [P, G, R, H]),
                    scalar=-BIG, in1=spread(bias[:, :].rearrange("p (r h) -> p r h", h=H).unsqueeze(1), [P, G, R, H]),
                    op0=ALU.mult, op1=ALU.add).then_inc(bias_ready, 1)
                dve.wait_ge(prod_ready, m + 1)
                dve.tensor_reduce(score[:, o, :], prod[:, o, :].rearrange("p (g d) -> p g d", d=DH),
                                  AX_X, ALU.add).then_inc(score_ready, 1)
                dve.wait_ge(bias_ready, m + 1)
                dve.wait_ge(score_ready, m + 1)
                if there(m - RING):
                    dve.wait_ge(l_stored[s], turn * 16)
                dve.tensor_tensor(
                    logit[:, s, :, :].rearrange("p g (r h) -> p g r h", h=H),
                    spread(score[:, o, :].rearrange("p (g h) -> p g h", h=H).unsqueeze(2), [P, G, R, H]),
                    shifted[:, o, :, :].rearrange("p g (r h) -> p g r h", h=H), ALU.add).then_inc(logit_ready, 1)

            def maxima(m, s, turn):
                dve.wait_ge(starts_loaded[s], (turn + 1) * 16)
                dve.wait_ge(turned, m + 1)
                if there(m - RING):
                    dve.wait_ge(m_stored[s], turn * 16)
                if there(m - 1):
                    dve.wait_ge(scanned, m)
                    initial = top[:, (s - 1) % RING, GP - 1:GP]
                else:
                    initial = low[0:RH, 0:1]
                o = 2 + s % 2
                dve.tensor_tensor_scan(top[:, s, :], starts[:, s, :], ps[0:RH, o * BANK:(o + 1) * BANK], initial,
                                       ALU.add, ALU.max).then_inc(scanned, 1)

            def step(n, s, turn):
                onehots(n, s, turn)
                if there(n - 1):
                    scores(n - 1, (s - 1) % RING, turn if s else turn - 1)
                if there(n - 2):
                    maxima(n - 2, (s - 2) % RING, turn if s >= 2 else turn - 1)

            over_turns(dve, L1.steps, step)
            scores(L1.steps - 1, RING - 1, L1.turns - 1)
            maxima(L1.steps - 2, RING - 2, L1.turns - 1)
            maxima(L1.steps - 1, RING - 1, L1.turns - 1)

        @block.tensor
        def _(pe):
            def expand(n, s):
                groups = block_registers(nc, net.groups1, n, NG - 1)
                pe.wait_ge(onehot_t, n + 1)
                if there(n - 2):
                    pe.wait_ge(prod_ready, n - 1)
                o = s % 2
                for i in range(G):
                    for part in range(3):
                        last = pe.matmul(ps[:, o * BANK + i * D:o * BANK + (i + 1) * D],
                                         oht[:, o, i * P:(i + 1) * P],
                                         q1[:, cols(groups[i] * (3 * D) + part * D, D)],
                                         start=(part == 0), stop=(part == 2))
                last.then_inc(queries, 1)

            def turn_logits(m, s):
                pe.wait_ge(logit_ready, m + 1)
                if there(m - 2):
                    pe.wait_ge(scanned, m - 1)
                settle(pe, passed_pe)
                o = 2 + s % 2
                for i in range(G):
                    last = pe.transpose(ps[0:RH, o * BANK + i * P:o * BANK + (i + 1) * P], logit[:, s, i, :],
                                        net.ident[:, :])
                last.then_inc(turned, 1)

            def step(n, s, turn):
                if isinstance(n, int) and s == 0:
                    pe.wait_ge(q_loaded[turn], 16 * SUBS)
                expand(n, s)
                if there(n - 1):
                    turn_logits(n - 1, (s - 1) % RING)

            over_turns(pe, L1.steps, step, peeled=CHUNKS)
            turn_logits(L1.steps - 1, RING - 1)


def sums1(net, probs, rsum):
    nc = net.nc
    LAST = WIDE_STEPS - 1
    with ExitStack() as ctx:
        def sb(name, shape, dt):
            return ctx.enter_context(nc.sbuf_tensor(name, shape, dt))

        (passed_sp, passed_act, passed_pe, passed_dve, scanned, turned, diff_ready, least_ready, onehot, exp_ready, added, blank, v_done, parts) = sems(
            nc, "s1", "passed_sp", "passed_act", "passed_pe", "passed_dve", "scanned", "turned", "diff_ready", "least_ready", "onehot", "exp_ready", "added", "blank",
            "vector_done", "parts")
        loaded = sems(nc, "s1", *[f"loaded{s}" for s in range(RING)])
        logits_loaded = sems(nc, "s1", *[f"logits_loaded{s}" for s in range(RING)])
        starts = sb("starts_", [RH, RING, GWP], BF16)
        top = sb("top_", [RH, RING, GWP], F32)
        logit = sb("logit_", [P, RING, GW * RH], F32)
        diff = sb("diff", [P, 2, GW * RH], F32)
        least = sb("least", [P, 2, GW, H], F32)
        oh = sb("oh_", [P, RING, GW, P], F32)
        rs = oh[:, 0:2, :, :].rearrange("p a g e -> p (a g e)")[:, 0:NG * H]
        rest = oh[:, 2:4, :, :].rearrange("p a g e -> p (a g e)")[:, 0:NG * H]
        low = sb("low_", [P, 1], F32)
        ps = net.psum
        block = ctx.enter_context(nc.Block())

        def back(n):
            return WIDE_STEPS - 1 - n if isinstance(n, int) else (WIDE_STEPS - 1) - n

        @block.gpsimd
        def _(pool):
            pool.memset(low[:, :], -BIG).then_inc(blank, 1)

        @block.sync
        def _(sp):
            def load(n, s, turn):
                at = back(n)
                if there(n - RING):
                    sp.wait_ge(turned, n - (RING - 1))
                    settle(sp, passed_sp)
                    sp.wait_ge(scanned, n - (RING - 2))
                    settle(sp, passed_sp)
                sp.dma_start(starts[:, s, :], net.start_rows[cols(at * GWP + 1, GWP)].partition_broadcast(RH))\
                    .then_inc(loaded[s], 16)
                sp.dma_start(top[:, s, :].rearrange("p (a c) -> p a c", a=2),
                             net.m_spill[cols(at * 2, 2), :, :].rearrange("a p c -> p a c"))\
                    .then_inc(loaded[s], 16)

            over_turns(sp, WIDE_STEPS, load)

        @block.vector
        def _(dve):
            dve.wait_ge(blank, 1)

            def maxima(n, s, turn):
                dve.wait_ge(loaded[s], (turn + 1) * 32)
                if there(n - 1):
                    dve.wait_ge(scanned, n)
                    initial = top[:, (s - 1) % RING, 0:1]
                else:
                    initial = low[0:RH, 0:1]
                dve.tensor_tensor_scan(top[:, s, ::-1], starts[:, s, ::-1], top[:, s, ::-1], initial,
                                       ALU.add, ALU.max).then_inc(scanned, 1)

            def onehots(n, s):
                if there(n - RING):
                    dve.wait_ge(added, n - (RING - 1))
                settle(dve, passed_dve)
                dve.tensor_tensor(oh[:, s, :, :], spread(net.lane[:, :].unsqueeze(1), [P, GW, P]),
                                  spread(net.key[:, cols(back(n) * GW, GW)].unsqueeze(2), [P, GW, P]),
                                  ALU.is_equal).then_inc(onehot, 1)

            def diffs(m, s, turn):
                o = s % 2
                dve.wait_ge(logits_loaded[s], (turn + 1) * 16)
                dve.wait_ge(turned, m + 1)
                dve.scalar_tensor_tensor(out=diff[:, o, :], in0=ps[:, (4 + o) * BANK:(4 + o) * BANK + GW * RH],
                                         scalar=NEG, in1=logit[:, s, :], op0=ALU.max, op1=ALU.subtract)\
                    .then_inc(diff_ready, 1)

            def choose(m, s):
                o = s % 2
                dve.wait_ge(diff_ready, m + 1)
                if there(m - 2):
                    dve.wait_ge(exp_ready, m - 1)
                dve.tensor_reduce(least[:, o, :, :], diff[:, o, :].rearrange("p (g r h) -> p g h r", r=R, h=H), AX_X,
                                  ALU.min).then_inc(least_ready, 1)

            def step(n, s, turn):
                maxima(n, s, turn)
                if there(n - 1):
                    diffs(n - 1, (s - 1) % RING, turn if s else turn - 1)
                onehots(n, s)
                if there(n - 1):
                    choose(n - 1, (s - 1) % RING)

            over_turns(dve, WIDE_STEPS, step)
            diffs(LAST, LAST % RING, LAST // RING)
            choose(LAST, LAST % RING)
            dve.wait_ge(added, WIDE_STEPS)
            dve.tensor_scalar(rs, ps[:, 0:NG * H], 1e-12, None, ALU.add).then_inc(v_done, 1)
            dve.wait_ge(v_done, 1)
            dve.reciprocal(rs, rs).then_inc(v_done, 1)
            dve.wait_ge(v_done, 2)
            part = [rsum[:, :].rearrange("p (g s h) -> p g s h", s=3, h=H)[:, :, s, :] for s in range(3)]
            split3(dve, *part, rs.rearrange("p (g h) -> p g h", h=H), rest.rearrange("p (g h) -> p g h", h=H),
                   parts, 0)

        @block.scalar
        def _(act):
            def exps(m, s):
                act.wait_ge(least_ready, m + 1)
                settle(act, passed_act)
                act.activation(probs[:, cols(back(m) * (GW * H), GW * H)],
                               least[:, s % 2, :, :].rearrange("p g h -> p (g h)"), ACT.Exp, scale=-1.0)\
                    .then_inc(exp_ready, 1)

            def step(n, s, turn):
                act.dma_start(logit[:, s, :].rearrange("p (a c) -> p a c", a=2),
                              net.l_spill[cols(back(n) * 2, 2), :, :].rearrange("a p c -> p a c"))\
                    .then_inc(logits_loaded[s], 16)
                if there(n - 3):
                    exps(n - 3, (s - 3) % RING)

            over_turns(act, WIDE_STEPS, step)
            for m in range(WIDE_STEPS - 3, WIDE_STEPS):
                exps(m, m % RING)

        @block.tensor
        def _(pe):
            clear_banks(pe, net, -(-NG * H // BANK))

            def turn_maxima(n, s):
                pe.wait_ge(scanned, n + 1)
                if there(n - 2):
                    pe.wait_ge(diff_ready, n - 1)
                settle(pe, passed_pe)
                o = s % 2
                for i in range(GW):
                    last = pe.transpose(ps[:, (4 + o) * BANK + i * RH:(4 + o) * BANK + (i + 1) * RH],
                                        top[:, s, i * P:(i + 1) * P], net.ident[0:RH, 0:RH])
                last.then_inc(turned, 1)

            def add(m, s):
                at = back(m)
                groups = block_registers(nc, net.groups1, at, NG - 1, GW)
                pe.wait_ge(onehot, m + 1)
                pe.wait_ge(exp_ready, m + 1)
                for i in range(GW):
                    last = pe.matmul(ps[:, cols(groups[i] * H, H)], oh[:, s, i, :],
                                     probs[:, cols(at * (GW * H) + i * H, H)],
                                     start=False, stop=False, skip_group_check=True)
                last.then_inc(added, 1)

            def step(n, s, turn):
                turn_maxima(n, s)
                if there(n - 2):
                    add(n - 2, (s - 2) % RING)

            over_turns(pe, WIDE_STEPS, step)
            for m in (LAST - 1, LAST):
                add(m, m % RING)


def values1(net, probs, rsum):
    nc = net.nc
    LAST = WIDE_STEPS - 1
    PG = 2 * GW
    PAIRS = WIDE_STEPS // 2
    assert PAIRS * 2 == WIDE_STEPS and PG * 3 * H <= BANK and (PAIRS + 1) * PG <= L1.cols * P
    with ExitStack() as ctx:
        def sb(name, shape, dt):
            return ctx.enter_context(nc.sbuf_tensor(name, shape, dt))

        (onehot_t, scales, scaled, attn_ready, msg_ready, added, rows_loaded) = sems(
            nc, "v1", "onehot_t", "scales", "scaled", "attn_ready", "msg_ready", "added", "rows_loaded")
        loaded = sems(nc, "v1", *[f"loaded{s}" for s in range(RING)])
        rows = sb("rows2", [P, PG * P], F16)
        v = sb("v2", [P, RING, GW, D], F32)
        msg = sb("msg2", [P, RING, GW, D], F32)
        oht = sb("oht2", [P, PG * P], BF16)
        oh = sb("oh2", [P, RING, GW, P], F32)
        scale = sb("scale", [P, PG, H], F32)
        attn = sb("attn", [P, PG, H], F32)
        ps = net.psum
        se = net.psum[:, 7 * BANK:7 * BANK + PG * 3 * H]
        block = ctx.enter_context(nc.Block())

        @block.sync
        def _(sp):
            def load(n, s, turn):
                if there(n - RING):
                    sp.wait_ge(msg_ready, n - (RING - 1))
                sp.dma_start(v[:, s, :, :].rearrange("p (a g) d -> p a (g d)", a=2),
                             net.v_spill[cols(n * 2, 2), :, :, :].rearrange("a p g d -> p a (g d)"))\
                    .then_inc(loaded[s], 16)

            over_turns(sp, WIDE_STEPS, load)

        @block.scalar
        def _(act):
            def load(pair):
                act.dma_start(rows[:, :], net.key_rows[cols(pair * (PG * P), PG * P)].partition_broadcast(P))\
                    .then_inc(rows_loaded, 16)

            load(0)
            with act.Fori(1, PAIRS + 1) as pair:
                act.wait_ge(onehot_t, pair)
                load(pair)

        @block.vector
        def _(dve):
            def onehots_t(pair):
                dve.wait_ge(rows_loaded, (pair + 1) * 16)
                if there(pair - 1):
                    dve.wait_ge(scales, pair)
                dve.tensor_scalar(oht[:, :], rows[:, :], net.part1[:, 0:1], None, ALU.is_equal)\
                    .then_inc(onehot_t, 1)

            def attention(pair):
                dve.wait_ge(scales, pair + 1)
                dve.tensor_reduce(scale[:, :, :], se.rearrange("p (i s h) -> p i h s", s=3, h=H), AX_X, ALU.add)\
                    .then_inc(scaled, 1)
                onehots_t(pair + 1)
                dve.wait_ge(scaled, pair + 1)
                dve.tensor_tensor(attn[:, :, :].rearrange("p i h -> p (i h)"),
                                  scale[:, :, :].rearrange("p i h -> p (i h)"),
                                  probs[:, cols(pair * (PG * H), PG * H)], ALU.mult).then_inc(attn_ready, 1)

            def step(n, s, turn):
                pair = turn * 2 + s // 2
                if s % 2 == 0:
                    attention(pair)
                if there(n - RING):
                    dve.wait_ge(added, n - (RING - 1))
                dve.tensor_tensor(oh[:, s, :, :], spread(net.lane[:, :].unsqueeze(1), [P, GW, P]),
                                  spread(net.local1[:, cols(n * GW, GW)].unsqueeze(2), [P, GW, P]), ALU.is_equal)
                if s % 2 == 0:
                    dve.wait_ge(attn_ready, pair + 1)
                dve.wait_ge(loaded[s], (turn + 1) * 16)
                dve.tensor_tensor(msg[:, s, :, :].rearrange("p g (h d) -> p g h d", d=DH),
                                  v[:, s, :, :].rearrange("p g (h d) -> p g h d", d=DH),
                                  spread(attn[:, (s % 2) * GW:(s % 2 + 1) * GW, :].unsqueeze(3), [P, GW, H, DH]),
                                  ALU.mult).then_inc(msg_ready, 1)

            onehots_t(0)
            over_turns(dve, WIDE_STEPS, step)

        @block.tensor
        def _(pe):
            clear_banks(pe, net, 7)

            def expand(pair, half):
                groups = block_registers(nc, net.groups1, pair * 2 + half, NG - 1, GW)
                if half == 0:
                    pe.wait_ge(onehot_t, pair + 1)
                    if there(pair - 1):
                        pe.wait_ge(scaled, pair)
                for k in range(GW):
                    i = half * GW + k
                    last = pe.matmul(se[:, i * 3 * H:(i + 1) * 3 * H], oht[:, i * P:(i + 1) * P],
                                     rsum[:, cols(groups[k] * (3 * H), 3 * H)], start=True, stop=True)
                if half == 1:
                    last.then_inc(scales, 1)

            def add(m, s):
                blocks = block_registers(nc, net.blocks1, m, NB - 1, GW)
                pe.wait_ge(msg_ready, m + 1)
                for i in range(GW):
                    last = pe.matmul(ps[:, cols(blocks[i] * D, D)], oh[:, s, i, :], msg[:, s, i, :],
                                     start=False, stop=False, skip_group_check=True)
                last.then_inc(added, 1)

            def step(n, s, turn):
                pair = turn * 2 + s // 2
                if s % 2 == 1:
                    expand(pair + 1, 1)
                if there(n - 1):
                    add(n - 1, (s - 1) % RING)
                if s % 2 == 0:
                    expand(pair + 1, 0)

            expand(0, 0)
            expand(0, 1)
            over_turns(pe, WIDE_STEPS, step)
            add(LAST, LAST % RING)


def nodes2(net):
    nc, a = net.nc, net.a
    with ExitStack() as ctx:
        def sb(name, shape, dt):
            return ctx.enter_context(nc.sbuf_tensor(name, shape, dt))

        (w_loaded, v_done, ready, w_turned, w_copied, turned, copied, product, taken, stats, aggr, std_ready,
         scale_ready, normed, blank, finished, stored) = sems(
            nc, "n2", "w_loaded", "vector_done", "ready", "w_turned", "w_copied", "turned", "copied",
            "product", "taken", "stats", "aggr", "std_ready", "scale_ready", "normed", "blank", "finished",
            "stored")
        w = sb("w_out", [P, D], F32)
        wt = sb("wt_out", [P, D], F32)
        names = ("L1_gnn_out_proj_b", "L1_gnn_ln_gamma", "L1_gnn_ln_beta")
        vec = sb("vec2", [P, len(names), D], F32)
        eps = sb("eps2", [P, 1], F32)
        t1 = sb("t2", [P, NB, D], F32)
        at = sb("at2", [P, 2, P], F32)
        ps = net.psum
        ALL = [P, NB, D]

        def row(j):
            return spread(vec[:, j, :].unsqueeze(1), ALL)

        block = ctx.enter_context(nc.Block())

        @block.gpsimd
        def _(pool):
            pool.memset(eps[:, :], EPS).then_inc(blank, 1)

        @block.sync
        def _(sp):
            sp.dma_start(w[:, :], a["L1_gnn_out_proj_w"]).then_inc(w_loaded, 16)
            for j, name in enumerate(names):
                sp.dma_start(vec[:, j, :], a[name].partition_broadcast(P)).then_inc(w_loaded, 16)
            sp.wait_ge(finished, 1)
            for b in range(0, NB, NB // 5):
                sp.dma_start(net.out[b * NODES:(b + NB // 5) * NODES, :].rearrange("(b p) d -> p b d", p=NODES),
                             t1[0:NODES, b:b + NB // 5, :]).then_inc(stored, 16)
            sp.wait_ge(stored, 16 * 5)

        @block.vector
        def _(dve):
            done = [0]

            def chain(ins):
                done[0] += 1
                ins.then_inc(v_done, 1)
                dve.wait_ge(v_done, done[0])

            dve.tensor_copy(t1[:, :, :].rearrange("p b d -> p (b d)"), ps[:, 0:NB * D]).then_inc(ready, 1)
            dve.wait_ge(w_loaded, 16 * (1 + len(names)))
            chain(dve.tensor_tensor(net.h[:, :, :], net.h[:, :, :], row(0), ALU.add))

            def take(b, k, first):
                dve.wait_ge(product, b + 1)
                dve.tensor_tensor(block_of(net.h, b), ps[:, (2 + k) * BANK:(2 + k) * BANK + D],
                                  block_of(net.h, b), ALU.add).then_inc(taken, 1)

            over_blocks(dve, take)
            dve.wait_ge(taken, NB)
            layer_norm_stats(dve, net, net.h, stats, aggr, 1)
            layer_norm_scale(dve, net, std_ready, scale_ready, 1)
            dve.wait_ge(normed, NB)
            chain(dve.tensor_tensor(t1[:, :, :], t1[:, :, :], row(1), ALU.mult))
            chain(dve.tensor_tensor(t1[:, :, :], t1[:, :, :], row(2), ALU.add))
            dve.tensor_tensor(t1[:, :, :], t1[:, :, :], net.x[:, :, :], ALU.add).then_inc(finished, 1)

        @block.scalar
        def _(act):
            act.wait_ge(blank, 1)
            act.wait_ge(w_turned, 1)
            act.copy(wt[:, :], ps[:, 4 * BANK:4 * BANK + D]).then_inc(w_copied, 1)

            def copy(b, k, first):
                act.wait_ge(turned, b + 1)
                act.copy(at[:, k, :], ps[:, k * BANK:k * BANK + P]).then_inc(copied, 1)

            over_blocks(act, copy)
            layer_norm_std(act, net, eps, aggr, std_ready, 1)
            normalize(act, net, t1, net.h, ACT.Identity, scale_ready, 1, normed)

        @block.tensor
        def _(pe):
            pe.wait_ge(ready, 1)
            pe.wait_ge(w_loaded, 16 * (1 + len(names)))
            pe.transpose(ps[:, 4 * BANK:4 * BANK + D], w[:, :], net.ident[:, :]).then_inc(w_turned, 1)
            pe.wait_ge(w_copied, 1)

            def out_proj(b, k, first):
                if not first:
                    pe.wait_ge(copied, b - 1)
                pe.transpose(ps[:, k * BANK:k * BANK + P], block_of(t1, b), net.ident[:, :]).then_inc(turned, 1)
                pe.wait_ge(copied, b + 1)
                if not first:
                    pe.wait_ge(taken, b - 1)
                pe.matmul(ps[:, (2 + k) * BANK:(2 + k) * BANK + D], at[:, k, :], wt[:, :], start=True, stop=True)\
                    .then_inc(product, 1)

            over_blocks_unrolled(pe, out_proj)


_OUTS = [((N, D), "float32")]


def kernel(**inputs):
    import numpy as _np
    import concourse.bacc as _bacc
    from concourse import mybir as _mybir
    from concourse.bass_utils import run_bass_kernel_spmd as _run

    nc = _bacc.Bacc("TRN2", target_bir_lowering=False, num_devices=1)
    arrays, args = {}, {}
    for name, value in inputs.items():
        v = _np.ascontiguousarray(value)
        arrays[f"in_{name}"] = v
        args[name] = nc.dram_tensor(f"in_{name}", v.shape, _mybir.dt.from_np(v.dtype), kind="ExternalInput").ap()
    out = nc.dram_tensor("out_0", _OUTS[0][0], F32, kind="ExternalOutput").ap()
    build(nc, args, out)
    r = _run(nc, [arrays], core_ids=[0])
    return r.results[0]["out_0"]
```

```python
from contextlib import ExitStack

import numpy as np

import concourse.bass as bass
from concourse import mybir

ALU = mybir.AluOpType
ACT = mybir.ActivationFunctionType
AX_X = mybir.AxisListType.X
PE = mybir.EngineType.PE
F32, BF16, F16, I32 = mybir.dt.float32, mybir.dt.bfloat16, mybir.dt.float16, mybir.dt.int32

P = 128
N = 3125
E = 100000
D = 128
H = 8
DH = D // H
R = 5
RH = R * H
DFF = 2 * D
GROUP = 25
SUBS = 5
NODES = SUBS * GROUP
NB = -(-N // NODES)
NG = NB * SUBS
assert NB * NODES == N and GROUP * R <= P
NPAD = NB * P
T = -(-E // P)
JT = -(-T // P)
TPAD = JT * P
G = 4
RING = 4
GP = G * P
TURN = G * RING


class Pass:

    def __init__(self, size, count, unit):
        self.size, self.count = size, count
        self.steps = -(-(T + count - 1) // (G * unit)) * unit
        self.items = self.steps * G
        self.cols = -(-(self.items + TURN) // P)


L0 = Pass(NODES, NB, 1)
L1 = Pass(GROUP, NG, RING)
GW = 2 * G
GWP = GW * P
WIDE_STEPS = L1.items // GW
CHUNK = NB // 5
BUFS = 4
SHARE = 3
BANK = 512
PER_BANK = BANK // (3 * H)
SUM_BANKS = -(-NG // PER_BANK)
EPS = 1e-5
BIG = float(2.0 ** 100)
NEG = -1e9
PAD_DST = N
OUTSIDE = 20000.0
ROUND = 1.5 * 2 ** 23
KW = 4


def over_turns(eng, steps, step, peeled=1):
    turns = steps // RING
    for n in range(RING * peeled):
        step(n, n % RING, n // RING)
    with eng.Fori(peeled, turns) as turn:
        for s in range(RING):
            step(turn * RING + s, s, turn)
    for n in range(turns * RING, steps):
        step(n, n % RING, turns)


def over_blocks(eng, body, ring=2):
    assert NB % ring == 1
    for b in range(2 * ring):
        body(b, b % ring, b < 2)
    with eng.Fori(2, NB // ring) as i:
        for k in range(ring):
            body(i * ring + k, k, False)
    body(NB - 1, 0, False)


def over_blocks_unrolled(pe, body):
    for b in range(NB):
        body(b, b % 2, b < 2)


def scalar_onehots(act, net, out, away, values, m, first, away_ready, made):
    if there(m - 1):
        act.wait_ge(made, m)
    for i in range(SHARE):
        last = act.activation(away[:, i, :], net.lane[:, :], ACT.Abs, bias=values[:, cols(first + i, 1)],
                              scale=-1.0)
    last.then_inc(away_ready, 1)
    act.wait_ge(away_ready, m + 1)
    act.activation(out, away[:, :, :], ACT.Relu, bias=net.ones[:, 0:1], scale=-1.0).then_inc(made, 1)


def there(n):
    return not isinstance(n, int) or n >= 0


def settle(eng, passed):
    eng.sem_inc(passed, 1)


def cols(start, size):
    return bass.ds(start, size)


def spread(ap, shape):
    return ap.broadcast_to(shape)


class Net:
    pass


def build(nc, a, out):
    with ExitStack() as ctx:
        net = Net()
        net.nc, net.a, net.out = nc, a, out

        def sb(name, shape, dt):
            return ctx.enter_context(nc.sbuf_tensor(name, shape, dt))

        net.psum = ctx.enter_context(nc.psum_tensor("psum", [P, 8 * BANK], F32))
        net.edges = nc.dram_tensor("edges", [TPAD, KW * P], I32).ap()
        net.local_rows = nc.dram_tensor("local_rows", [L0.cols * P * P], F16).ap()
        net.key_rows = nc.dram_tensor("key_rows", [L1.cols * P * P], F16).ap()
        net.start_rows = nc.dram_tensor("start_rows", [L1.cols * P * P], BF16).ap()
        net.kv0 = nc.dram_tensor("kv0", [NPAD, 2 * D], F32).ap()
        net.kv1 = nc.dram_tensor("kv1", [NPAD * R, 2 * D], F32).ap()
        net.q1_parts = nc.dram_tensor("q1_parts", [NPAD * R, 3 * D], BF16).ap()
        net.v_spill = nc.dram_tensor("v_spill", [L1.steps, P, G, D], F32).ap()
        net.l_spill = nc.dram_tensor("l_spill", [L1.steps, P, G * RH], F32).ap()
        net.m_spill = nc.dram_tensor("m_spill", [L1.steps, RH, GP], F32).ap()

        net.ident = sb("ident", [P, P], F32)
        net.ones = sb("ones", [P, P], F32)
        net.lane = sb("lane", [P, P], F32)
        net.part1 = sb("part1", [P, 1], F32)
        net.ones16 = sb("ones16", [P, 1], BF16)
        net.zeros = sb("zeros", [P, BANK], BF16)
        net.local0 = sb("local0", [P, L0.cols * P], F32)
        net.local1 = sb("local1", [P, L1.cols * P], F32)
        net.rel = sb("rel", [P, L1.cols * P], F32)
        net.key = sb("key", [P, L1.cols * P], F32)
        net.src0 = sb("src0", [P, L0.cols * P], I32)
        net.src1 = sb("src1", [P, L1.cols * P], I32)
        net.blocks0 = sb("blocks0", [1, L0.cols * P], I32)
        net.blocks1 = sb("blocks1", [1, L1.cols * P], I32)
        net.groups1 = sb("groups1", [1, L1.cols * P], I32)
        net.sums1 = sb("sums1_columns", [1, L1.cols * P], I32)
        net.lane16 = sb("lane16", [P, P], BF16)
        net.flag = sb("flag", [1, 1], I32)
        net.x = sb("x", [P, NB, D], F32)
        net.h = sb("h", [P, NB, D], F32)
        net.mv = sb("mv", [P, NB, 2], F32)
        net.tmp = sb("tmp", [P, 2, NB], F32)
        net.st = sb("st", [P, NB, 6], F32)
        net.rstd = sb("rstd", [P, NB], F32)
        net.shift = sb("shift", [P, NB], F32)

        def run(stage, *args):
            with nc.cleanup_on_exit():
                stage(net, *args)

        run(constants)
        with nc.sbuf_tensor("raw", [P, JT, KW, P], I32) as raw:
            run(load_edges, raw)
        run(sort_edges)
        run(items, L0)
        with nc.sbuf_tensor("q0", [P, NB * 3 * D], BF16) as q0:
            run(nodes0, q0)
            run(edges0, q0)
        run(nodes1)
        with nc.sbuf_tensor("q1", [P, NG * 3 * D], BF16) as q1:
            run(logits1, q1)
        with nc.sbuf_tensor("probs", [P, L1.items * H], F32) as probs:
            with nc.sbuf_tensor("rsum", [P, NG * 3 * H], BF16) as rsum:
                run(sums1, probs, rsum)
                run(values1, probs, rsum)
        run(nodes2)


def sems(nc, stage, *names):
    return [nc.alloc_semaphore(f"{stage}_{x}") for x in names]


def constants(net):
    nc = net.nc
    with ExitStack() as ctx:
        blank, rows = sems(nc, "c", "blank", "rows")
        block = ctx.enter_context(nc.Block())

        @block.gpsimd
        def _(pool):
            pool.memset(net.ident[:, :], 0.0).then_inc(blank, 1)
            pool.memset(net.ones[:, :], 1.0)
            pool.memset(net.ones16[:, :], 1.0)
            pool.memset(net.zeros[:, :], 0.0)
            pool.wait_ge(blank, 1)
            pool.affine_select(out=net.ident[:, :], in_=net.ident[:, :], compare_op=ALU.not_equal, fill=1.0,
                               base=0, pattern=[[-1, P]], channel_multiplier=1)
            pool.iota(net.lane[:, :], [[1, P]], base=0, channel_multiplier=0,
                      allow_small_or_imprecise_dtypes=True)
            pool.iota(net.lane16[:, :], [[1, P]], base=0, channel_multiplier=0,
                      allow_small_or_imprecise_dtypes=True)
            pool.iota(net.part1[:, :], [[0, 1]], base=0, channel_multiplier=1,
                      allow_small_or_imprecise_dtypes=True)


def load_edges(net, raw):
    nc, a = net.nc, net.a
    full = (T - 1) // P
    rows = (E - full * P * P) // P
    rest = E - (full * P + rows) * P
    with ExitStack() as ctx:
        padded, loaded, kept, checked, summed = sems(nc, "e", "padded", "loaded", "kept", "checked", "summed")
        falls = ctx.enter_context(nc.sbuf_tensor("falls", [P, JT, P], F32))
        fall = ctx.enter_context(nc.sbuf_tensor("fall", [P, 1], F32))
        ps = net.psum
        block = ctx.enter_context(nc.Block())

        @block.gpsimd
        def _(pool):
            pool.memset(raw[:, full, 0, :], PAD_DST).then_inc(padded, 1)
            pool.memset(raw[:, full, 1:3, :], 0).then_inc(padded, 1)
            pool.memset(raw[:, full, 3, :], PAD_DST).then_inc(padded, 1)
            pool.memset(raw[0:1, 0, 3, 0:1], -1).then_inc(padded, 1)

        @block.sync
        def _(sp):
            sp.wait_ge(padded, 4)
            body = full * P * P
            for k, name in enumerate(("dst", "src", "edge_type_5")):
                v = a[name]
                sp.dma_start(raw[:, 0:full, k, :],
                             v[0:body].rearrange("(j p e) -> p j e", p=P, e=P)).then_inc(loaded, 16)
                sp.dma_start(raw[0:rows, full, k, :],
                             v[body:body + rows * P].rearrange("(p e) -> p e", e=P)).then_inc(loaded, 16)
                sp.dma_start(raw[rows:rows + 1, full, k, 0:rest],
                             v[E - rest:E].rearrange("(p e) -> p e", p=1)).then_inc(loaded, 16)
            v = a["dst"]
            sp.dma_start(raw[1:P, 0, 3, :],
                         v[P - 1:P * P - 1].rearrange("(p e) -> p e", e=P)).then_inc(loaded, 16)
            sp.dma_start(raw[0:1, 0, 3, 1:P],
                         v[0:P - 1].rearrange("(p e) -> p e", p=1)).then_inc(loaded, 16)
            sp.dma_start(raw[:, 1:full, 3, :],
                         v[P * P - 1:body - 1].rearrange("(j p e) -> p j e", p=P, e=P)).then_inc(loaded, 16)
            sp.dma_start(raw[0:rows, full, 3, :],
                         v[body - 1:body - 1 + rows * P].rearrange("(p e) -> p e", e=P)).then_inc(loaded, 16)
            sp.dma_start(raw[rows:rows + 1, full, 3, 0:rest + 1],
                         v[E - rest - 1:E].rearrange("(p e) -> p e", p=1)).then_inc(loaded, 16)
            sp.wait_ge(loaded, 16 * 14)
            sp.dma_start(net.edges.rearrange("(j p) c -> p j c", p=P),
                         raw[:, :, :, :].rearrange("p j k e -> p j (k e)")).then_inc(kept, 16)
            sp.wait_ge(kept, 16)

        @block.vector
        def _(dve):
            dve.wait_ge(loaded, 16 * 14)
            dve.wait_ge(padded, 4)
            dve.tensor_tensor(falls[:, :, :], raw[:, :, 3, :], raw[:, :, 0, :], ALU.is_gt).then_inc(checked, 1)
            dve.wait_ge(checked, 1)
            dve.tensor_reduce(fall[:, :], falls[:, :, :].rearrange("p j e -> p (j e)"), AX_X, ALU.add)\
                .then_inc(checked, 1)
            dve.wait_ge(summed, 1)
            dve.tensor_scalar(net.flag[:, :], ps[0:1, 0:1], 0.0, None, ALU.is_gt)

        @block.tensor
        def _(pe):
            pe.wait_ge(checked, 2)
            pe.matmul(ps[0:1, 0:1], fall[:, :], net.ones[:, 0:1], start=True, stop=True).then_inc(summed, 1)


def sort_edges(net):
    nc = net.nc
    DUMP = NPAD
    words = KW * P
    counters = nc.dram_tensor("counters", [NPAD + P, 1], F32).ap()
    sorted_ = nc.dram_tensor("sorted_edges", [TPAD * words, 1], I32).ap()
    with ExitStack() as ctx:
        def sb(name, shape, dt):
            return ctx.enter_context(nc.sbuf_tensor(name, shape, dt))

        (blank, cleared, fetched, based, computed, counted, written, v_done, passed_pool, whole, prefixed,
         final) = sems(
            nc, "o", "blank", "cleared", "fetched", "based", "computed", "counted", "written", "vector_done",
            "passed_pool", "whole", "prefixed", "final")
        col = sb("col", [P, KW], I32)
        row = sb("row", [P, P], I32)
        below = sb("below", [P, P], F32)
        eq = sb("eq", [P, P], F32)
        colf = sb("colf", [P, KW], F32)
        rowf = sb("rowf", [P, P], F32)
        total = sb("total", [P, 1], F32)
        before = sb("before", [P, 1], F32)
        base = sb("base", [P, 1], F32)
        new = sb("new", [P, 1], F32)
        t1 = sb("t1_", [P, 1], F32)
        t2 = sb("t2_", [P, 1], F32)
        wide = sb("wide_", [P, 1], I32)
        at = sb("at_", [P, 8], F32)
        at_i = sb("at_i", [P, 8], I32)
        first = sb("first", [1, 1], I32)
        count = sb("count", [1, NPAD], F32)
        prefix = sb("prefix", [1, NPAD], F32)
        block = ctx.enter_context(nc.Block())

        @block.gpsimd
        def _(pool):
            unsorted = pool.value_load(net.flag[0:1, 0:1], min_val=0, max_val=1)
            with pool.If(unsorted > 0):
                pool.memset(below[:, :], 1.0).then_inc(blank, 1)
                pool.memset(count[:, :], 0.0).then_inc(blank, 1)
                pool.memset(first[:, :], -1).then_inc(blank, 1)
                pool.wait_ge(blank, 3)
                pool.affine_select(out=below[:, :], in_=below[:, :], compare_op=ALU.is_ge, fill=0.0,
                                   base=-1, pattern=[[-1, P]], channel_multiplier=1).then_inc(blank, 1)
                pool.dma_start(counters[0:NPAD, :].rearrange("n a -> a n"), count[:, :]).then_inc(cleared, 16)
                pool.dma_start(counters[NPAD:NPAD + P, :].rearrange("n a -> a n"), count[:, 0:P])\
                    .then_inc(cleared, 16)
                pool.dma_start(sorted_[3 * P:3 * P + 1, :], first[:, :]).then_inc(cleared, 16)
                pool.wait_ge(cleared, 48)

                def sweep(t, moving):
                    done = t + T if moving else t
                    edge = net.edges[cols(t, 1), :]
                    settle(pool, passed_pool)
                    with nc.allow_non_contiguous_dma(reason="one word to a partition"):
                        pool.dma_start(col[:, 0:3], edge.rearrange("a (k p) -> p (a k)", p=P)[:, 0:3])\
                            .then_inc(fetched, 16)
                    pool.dma_start(row[:, :], edge[:, 0:P].rearrange("a e -> (a e)").partition_broadcast(P))\
                        .then_inc(fetched, 16)
                    pool.wait_ge(fetched, (done + 1) * 32)
                    settle(pool, passed_pool)
                    pool.indirect_dma_start(base[:, :], None, counters,
                                            bass.IndirectOffsetOnAxis(ap=col[:, 0:1], axis=0)).then_inc(based, 16)
                    pool.wait_ge(computed, done + 1)
                    settle(pool, passed_pool)
                    pool.indirect_dma_start(counters, bass.IndirectOffsetOnAxis(ap=at_i[:, 0:1], axis=0),
                                            new[:, :], None).then_inc(written if moving else counted, 16)
                    if moving:
                        for k, word in enumerate((0, 1, 2, 0)):
                            pool.indirect_dma_start(
                                sorted_, bass.IndirectOffsetOnAxis(ap=at_i[:, 1 + k:2 + k], axis=0),
                                col[:, word:word + 1], None).then_inc(written, 16)
                        pool.wait_ge(written, (t + 1) * 80)
                    else:
                        pool.wait_ge(counted, (t + 1) * 16)

                with pool.Fori(0, T) as t:
                    sweep(t, False)
                pool.dma_start(count[:, :], counters[0:NPAD, :].rearrange("n a -> a n")).then_inc(whole, 16)
                pool.wait_ge(prefixed, 2)
                pool.dma_start(counters[0:NPAD, :].rearrange("n a -> a n"), prefix[:, :]).then_inc(whole, 16)
                pool.wait_ge(whole, 32)
                with pool.Fori(0, T) as t:
                    sweep(t, True)
                pool.dma_start(net.edges[0:T, :],
                               sorted_[0:T * words, :].rearrange("(t w) a -> t (w a)", w=words)).then_inc(final, 16)
                pool.wait_ge(final, 16)

        @block.vector
        def _(dve):
            unsorted = dve.value_load(net.flag[0:1, 0:1], min_val=0, max_val=1)
            with dve.If(unsorted > 0):
                dve.wait_ge(blank, 4)

                def sweep(t, moving):
                    done = t + T if moving else t
                    steps_before = t * STEP2 + T * STEP1 if moving else t * STEP1
                    count_ = [0]

                    def chain(ins):
                        count_[0] += 1
                        ins.then_inc(v_done, 1)
                        dve.wait_ge(v_done, steps_before + count_[0])

                    dve.wait_ge(fetched, (done + 1) * 32)
                    chain(dve.tensor_copy(colf[:, 0:3], col[:, 0:3]))
                    chain(dve.tensor_copy(rowf[:, :], row[:, :]))
                    chain(dve.tensor_scalar(eq[:, :], rowf[:, :], colf[:, 0:1], None, ALU.is_equal))
                    chain(dve.tensor_reduce(total[:, :], eq[:, :], AX_X, ALU.add))
                    chain(dve.tensor_tensor(eq[:, :], eq[:, :], below[:, :], ALU.mult))
                    chain(dve.tensor_reduce(before[:, :], eq[:, :], AX_X, ALU.add))
                    chain(dve.tensor_scalar(t1[:, :], before[:, :], 0.0, None, ALU.is_gt))
                    chain(dve.tensor_scalar(t2[:, :], net.part1[:, :], float(DUMP), None, ALU.add))
                    chain(dve.tensor_tensor(t2[:, :], t2[:, :], colf[:, 0:1], ALU.subtract))
                    chain(dve.tensor_tensor(t2[:, :], t2[:, :], t1[:, :], ALU.mult))
                    chain(dve.tensor_tensor(at[:, 0:1], t2[:, :], colf[:, 0:1], ALU.add))
                    dve.wait_ge(based, (done + 1) * 16)
                    chain(dve.tensor_tensor(new[:, :], base[:, :], total[:, :], ALU.add))
                    if moving:
                        for k in range(2):
                            chain(dve.scalar_tensor_tensor(out=t1[:, :], in0=base[:, :], scalar=float(k),
                                                           in1=before[:, :], op0=ALU.add, op1=ALU.add))
                            chain(dve.tensor_copy(wide[:, :], t1[:, :]))
                            chain(dve.tensor_scalar(wide[:, :], wide[:, :], 7, None, ALU.logical_shift_right))
                            chain(dve.tensor_copy(t2[:, :], wide[:, :]))
                            chain(dve.scalar_tensor_tensor(out=t1[:, :], in0=t2[:, :], scalar=3.0 * P,
                                                           in1=t1[:, :], op0=ALU.mult, op1=ALU.add))
                            if k == 0:
                                for j in range(3):
                                    chain(dve.tensor_scalar(at[:, 1 + j:2 + j], t1[:, :], float(j * P), None,
                                                            ALU.add))
                            else:
                                chain(dve.tensor_scalar(at[:, 4:5], t1[:, :], 3.0 * P, None, ALU.add))
                    n = 5 if moving else 1
                    dve.tensor_copy(at_i[:, 0:n], at[:, 0:n]).then_inc(computed, 1)
                    assert count_[0] == (STEP2 if moving else STEP1)

                STEP1, STEP2 = 12, 26
                with dve.Fori(0, T) as t:
                    sweep(t, False)
                dve.wait_ge(whole, 16)
                dve.tensor_tensor_scan(prefix[:, :], spread(net.ones[0:1, 0:1], [1, NPAD]), count[:, :], 0.0,
                                       ALU.mult, ALU.add).then_inc(prefixed, 1)
                dve.wait_ge(prefixed, 1)
                dve.tensor_tensor(prefix[:, :], prefix[:, :], count[:, :], ALU.subtract).then_inc(prefixed, 1)
                with dve.Fori(0, T) as t:
                    sweep(t, True)


def items(net, lay):
    with ExitStack() as ctx:
        programs = item_programs(net, lay, ctx)
        block = ctx.enter_context(net.nc.Block())

        @block.gpsimd
        def _(pool):
            programs.pool(pool)

        @block.sync
        def _(sp):
            programs.load(sp)
            programs.store(sp)

        @block.scalar
        def _(act):
            programs.floats(act)

        @block.vector
        def _(dve):
            programs.locate(dve)
            programs.derive(dve)
            programs.take(dve)

        @block.tensor
        def _(pe):
            programs.count(pe)
            programs.turn(pe)


def item_programs(net, lay, ctx):
    nc = net.nc
    J = lay.cols
    one = lay is L1
    name = "l1" if one else "l0"

    def sb(what, shape, dt):
        return ctx.enter_context(nc.sbuf_tensor(f"{name}_{what}", shape, dt))

    (numbered, loaded, v_done, compared, counted, located, gathered, floats, rows_ready, stored, made, turned,
     copied, got_blocks) = sems(
        nc, name, "numbered", "loaded", "vector_done", "compared", "counted", "located", "gathered", "floats",
        "rows_ready", "stored", "made", "turned", "copied", "got_blocks")
    own = sb("own", [P, J, KW, P], I32)
    words = sb("words", [P, KW, J, P], F32)
    w1 = sb("w1", [P, J, P], F32)
    w2 = sb("w2", [P, J, P], F32)
    outs = [sb(f"out{n}", [P, J, P], F32) for n in range(4 if one else 2)]
    rows16 = sb("rows16", [P, J, P], F16)
    start16 = sb("start16", [P, J, P], BF16)
    before = sb("before", [P, JT, J * P], BF16)
    last_dst = sb("last_dst", [P, JT], I32)
    last = sb("last", [P, JT], F32)
    tiles = sb("tiles", [P, JT], F32)
    line = sb("line", [P, J * P], F32)
    number = sb("number", [P, J], F32)
    tile_of = sb("tile_of", [P, J], F32)
    which = sb("which", [P, 4, J], F32)
    which_i = sb("which_i", [P, 3, J], I32)
    tile_i = sb("tile_i", [P, J], I32)
    block_rows = nc.dram_tensor(f"{name}_block_rows", [3, J * P], I32).ap()
    firsts = (net.groups1, net.blocks1, net.sums1) if one else (net.blocks0,)
    ps = net.psum

    def pool_(pool):
        for tile, pattern, step in ((tiles, [[P, JT]], 1), (number, [[P, J]], 1), (line, [[1, J * P]], 0)):
            pool.iota(tile[:, :], pattern, base=0, channel_multiplier=step,
                      allow_small_or_imprecise_dtypes=True).then_inc(numbered, 1)
        pool.wait_ge(located, 1)
        for j in range(J):
            pool.indirect_dma_start(own[:, j, :, :].rearrange("p k e -> p (k e)"), None, net.edges,
                                    bass.IndirectOffsetOnAxis(ap=tile_i[:, j:j + 1], axis=0))\
                .then_inc(gathered, 16)

    def load(sp):
        with nc.allow_non_contiguous_dma(reason="one word for each tile"):
            sp.dma_start(last_dst[:, :], net.edges.rearrange("(j p) c -> p j c", p=P)[:, :, P - 1])\
                .then_inc(loaded, 16)
        sp.wait_ge(located, 2)
        with nc.allow_non_contiguous_dma(reason="one word for each item"):
            for k in range(len(firsts)):
                sp.dma_start(block_rows[k].rearrange("(j p) -> p j", p=P), which_i[:, k, :]).then_inc(stored, 16)
        sp.wait_ge(stored, 16 * len(firsts))
        for k, tile in enumerate(firsts):
            sp.dma_start(tile[:, :], block_rows[k:k + 1, :]).then_inc(got_blocks, 16)

    def store(sp):
        sp.wait_ge(rows_ready, 1)
        sp.dma_start((net.key_rows if one else net.local_rows).rearrange("(j p e) -> p j e", p=P, e=P),
                     rows16[:, :, :]).then_inc(stored, 16)
        if one:
            sp.wait_ge(rows_ready, 2)
            sp.dma_start(net.start_rows.rearrange("(j p e) -> p j e", p=P, e=P), start16[:, :, :])\
                .then_inc(stored, 16)
        sp.wait_ge(stored, 16 * (len(firsts) + (2 if one else 1)))
        sp.wait_ge(got_blocks, 16 * len(firsts))

    def floats_(act):
        act.wait_ge(gathered, 16 * J)
        for k in range(KW if one else 2):
            act.copy(words[:, k, :, :], own[:, :, k, :]).then_inc(floats, 1)

    done = [0]

    def chained(dve):
        def chain(ins):
            done[0] += 1
            ins.then_inc(v_done, 1)
            dve.wait_ge(v_done, done[0])

        def quotient(dst, src, size):
            chain(dve.tensor_scalar(dst, src, 0.5, 1.0 / size, ALU.add, ALU.mult))
            chain(dve.tensor_scalar(dst, dst, -0.5, ROUND, ALU.add, ALU.add))
            chain(dve.tensor_scalar(dst, dst, -ROUND, None, ALU.add))

        return chain, quotient

    def locate(dve):
        chain, quotient = chained(dve)

        dve.wait_ge(loaded, 16)
        dve.wait_ge(numbered, 3)
        chain(dve.tensor_copy(last[:, :], last_dst[:, :]))
        quotient(last[:, :], last[:, :], lay.size)
        chain(dve.tensor_scalar(last[:, :], last[:, :], float(lay.count - 1), None, ALU.min))
        chain(dve.tensor_tensor(last[:, :], last[:, :], tiles[:, :], ALU.add))
        for j in range(JT):
            dve.tensor_scalar(before[:, j, :], line[:, :], last[:, j:j + 1], None, ALU.is_gt)\
                .then_inc(compared, 1)
        dve.wait_ge(counted, 1)
        chain(dve.tensor_scalar(tile_of[:, :], ps[:, 0:J], float(TPAD - 1), None, ALU.min))
        dve.tensor_copy(tile_i[:, :], tile_of[:, :]).then_inc(located, 1)
        chain(dve.tensor_tensor(which[:, 0, :], number[:, :], tile_of[:, :], ALU.subtract))
        chain(dve.tensor_scalar(which[:, 0, :], which[:, 0, :], float(lay.count - 1), None, ALU.min))
        quotient(which[:, 1, :], which[:, 0, :], SUBS if one else 1)
        quotient(which[:, 3, :], which[:, 0, :], PER_BANK)
        chain(dve.tensor_scalar(which[:, 3, :], which[:, 3, :], float(BANK - PER_BANK * 3 * H), None, ALU.mult))
        chain(dve.scalar_tensor_tensor(out=which[:, 2, :], in0=which[:, 0, :], scalar=3.0 * H,
                                       in1=which[:, 3, :], op0=ALU.mult, op1=ALU.add))
        dve.tensor_copy(which_i[:, :, :], which[:, 0:3, :]).then_inc(located, 1)
        chain(dve.tensor_scalar(which[:, 3, :], which[:, 1, :], -float(NODES), None, ALU.mult))
        chain(dve.tensor_scalar(which[:, 0, :], which[:, 0, :], -float(lay.size), None, ALU.mult))

    def derive(dve):
        chain, quotient = chained(dve)

        def less(first):
            return spread(first.unsqueeze(2), [P, J, P])

        dst, src, rel, prev = (words[:, k, :, :] for k in range(KW))
        dve.wait_ge(floats, 1)
        if one:
            sub, outside = w1[:, :, :], w2[:, :, :]
            chain(dve.tensor_tensor(sub, dst, less(which[:, 0, :]), ALU.add))
            chain(dve.tensor_scalar(outside, sub, 0.0, OUTSIDE, ALU.is_lt, ALU.mult))
            chain(dve.tensor_scalar(outs[1][:, :, :], sub, float(GROUP - 1), OUTSIDE, ALU.is_gt, ALU.mult))
            chain(dve.tensor_tensor(outside, outside, outs[1][:, :, :], ALU.add))
            dve.wait_ge(floats, 3)
            chain(dve.tensor_tensor(outs[1][:, :, :], rel, outside, ALU.add))
            chain(dve.scalar_tensor_tensor(out=outs[2][:, :, :], in0=sub, scalar=float(R),
                                           in1=outs[1][:, :, :], op0=ALU.mult, op1=ALU.add))
            dve.tensor_copy(rows16[:, :, :], outs[2][:, :, :]).then_inc(rows_ready, 1)
            chain(dve.tensor_tensor(outside, outside, dst, ALU.add))
            chain(dve.tensor_tensor(outs[0][:, :, :], outside, less(which[:, 3, :]), ALU.add))
            dve.wait_ge(floats, 4)
            chain(dve.tensor_tensor(w1[:, :, :], dst, prev, ALU.is_equal))
            dve.tensor_scalar(start16[:, :, :], w1[:, :, :], -1.0, BIG, ALU.add, ALU.mult)\
                .then_inc(rows_ready, 1)
        else:
            chain(dve.tensor_tensor(outs[0][:, :, :], dst, less(which[:, 3, :]), ALU.add))
            dve.tensor_copy(rows16[:, :, :], outs[0][:, :, :]).then_inc(rows_ready, 1)
        dve.wait_ge(floats, 2)
        quotient(w2[:, :, :], src, NODES)
        row = w2 if one else outs[1]
        chain(dve.scalar_tensor_tensor(out=row[:, :, :], in0=w2[:, :, :], scalar=float(P - NODES), in1=src,
                                       op0=ALU.mult, op1=ALU.add))
        if one:
            chain(dve.scalar_tensor_tensor(out=outs[3][:, :, :], in0=row[:, :, :], scalar=float(R), in1=rel,
                                           op0=ALU.mult, op1=ALU.add))
        dve.sem_inc(made, 1)

    def take(dve):
        for n, out in enumerate((net.local1, net.rel, net.key, net.src1) if one else (net.local0, net.src0)):
            base = (n % 2) * 2 * BANK
            dve.wait_ge(turned, n + 1)
            dve.tensor_copy(out[:, :], ps[:, base:base + J * P]).then_inc(copied, 1)

    def count(pe):
        pe.wait_ge(compared, JT)
        for c in range(J):
            for j in range(JT):
                mm = pe.matmul(ps[:, c:c + 1], before[:, j, c * P:(c + 1) * P], net.ones16[:, 0:1],
                               start=(j == 0), stop=(j == JT - 1))
        mm.then_inc(counted, 1)

    def turn(pe):
        pe.wait_ge(made, 1)
        for n, tile in enumerate(outs):
            if n >= 2:
                pe.wait_ge(copied, n - 1)
            for j in range(J):
                base = (n % 2) * 2 * BANK + j * P
                mm = pe.transpose(ps[:, base:base + P], tile[:, j, :], net.ident[:, :])
            mm.then_inc(turned, 1)

    return Programs(pool_, load, store, floats_, locate, derive, take, count, turn)


class Programs:

    def __init__(self, pool, load, store, floats, locate, derive, take, count, turn):
        self.pool, self.load, self.store, self.floats = pool, load, store, floats
        self.locate, self.derive, self.take = locate, derive, take
        self.count, self.turn = count, turn


def layer_norm_stats(dve, net, src, stats, aggr, turn, collect=True):
    for b in range(NB if collect else 0):
        dve.bn_stats(net.st[:, b, :], src[:, b, :]).then_inc(stats, 1)
    dve.wait_ge(stats, NB * turn)
    st, mv, tmp = net.st, net.mv, net.tmp
    mean, var, half, both = mv[:, :, 0], mv[:, :, 1], tmp[:, 0, :], tmp[:, 1, :]
    steps = (
        lambda: dve.tensor_tensor(mean, st[:, :, 1], st[:, :, 4], ALU.add),
        lambda: dve.tensor_tensor(half, st[:, :, 1], st[:, :, 4], ALU.subtract),
        lambda: dve.tensor_tensor(both, st[:, :, 2], st[:, :, 5], ALU.add),
        lambda: dve.tensor_scalar(mean, mean, 0.5, None, ALU.mult),
        lambda: dve.tensor_tensor(half, half, half, ALU.mult),
        lambda: dve.tensor_scalar(both, both, 1.0 / D, None, ALU.mult),
        lambda: dve.scalar_tensor_tensor(out=var, in0=half, scalar=0.25, in1=both, op0=ALU.mult, op1=ALU.add),
    )
    for n, step in enumerate(steps):
        if n >= 3:
            dve.wait_ge(aggr, len(steps) * (turn - 1) + n - (0 if n == 6 else 2))
        step().then_inc(aggr, 1)


AGGR = 7


def layer_norm_scale(dve, net, std_ready, scale_ready, turn):
    dve.wait_ge(std_ready, turn)
    dve.reciprocal(net.rstd[:, :], net.rstd[:, :]).then_inc(scale_ready, 1)
    dve.wait_ge(scale_ready, 2 * turn - 1)
    dve.scalar_tensor_tensor(out=net.shift[:, :], in0=net.mv[:, :, 0], scalar=-1.0, in1=net.rstd[:, :],
                             op0=ALU.mult, op1=ALU.mult).then_inc(scale_ready, 1)


def layer_norm_std(act, net, eps, aggr, std_ready, turn):
    act.wait_ge(aggr, AGGR * turn)
    act.activation(net.rstd[:, :], net.mv[:, :, 1], ACT.Sqrt, bias=eps[:, 0:1], scale=1.0).then_inc(std_ready, 1)


def normalize(act, net, dst, src, func, scale_ready, turn, normed):
    act.wait_ge(scale_ready, 2 * turn)
    for b in range(NB):
        act.activation(dst[:, b, :], src[:, b, :], func, bias=net.shift[:, b:b + 1], scale=net.rstd[:, b:b + 1])\
            .then_inc(normed, 1)


def block_of(tile, b):
    return tile[:, cols(b, 1), :].rearrange("p b d -> p (b d)")


def split3(dve, hi, mid, lo, src, rest, ready, base):
    dve.tensor_copy(hi, src).then_inc(ready, 1)
    dve.wait_ge(ready, base + 1)
    dve.tensor_tensor(rest, src, hi, ALU.subtract).then_inc(ready, 1)
    dve.wait_ge(ready, base + 2)
    dve.tensor_copy(mid, rest).then_inc(ready, 1)
    dve.wait_ge(ready, base + 3)
    dve.tensor_tensor(lo, rest, mid, ALU.subtract).then_inc(ready, 1)


def nodes0(net, q0):
    nc, a = net.nc, net.a
    with ExitStack() as ctx:
        def sb(name, shape, dt):
            return ctx.enter_context(nc.sbuf_tensor(name, shape, dt))

        (blank, x_loaded, w_loaded, stats, aggr, std_ready, scale_ready, normed, turned, copied, product,
         evacuated, parts) = sems(
            nc, "n0", "blank", "x_loaded", "w_loaded", "stats", "aggr", "std_ready", "scale_ready", "normed",
            "turned", "copied", "product", "evacuated", "parts")
        stores = sems(nc, "n0", *[f"store{k}" for k in range(BUFS)])
        w = sb("w_qkv0", [P, 3 * D], F32)
        eps = sb("eps", [P, 1], F32)
        ht = sb("ht", [P, 2, P], F32)
        qkv = sb("qkv", [P, BUFS, 3 * D], F32)
        rest = sb("rest", [P, D], F32)
        ps = net.psum
        programs = item_programs(net, L1, ctx)
        block = ctx.enter_context(nc.Block())

        @block.gpsimd
        def _(pool):
            pool.memset(net.x[:, :, :], 0.0).then_inc(blank, 1)
            pool.memset(eps[:, :], EPS).then_inc(blank, 1)
            programs.pool(pool)

        @block.sync
        def _(sp):
            x = a["x"]
            sp.wait_ge(blank, 1)
            for b in range(0, NB, NB // 5):
                sp.dma_start(net.x[0:NODES, b:b + NB // 5, :],
                             x[b * NODES:(b + NB // 5) * NODES, :].rearrange("(b p) d -> p b d", p=NODES))\
                    .then_inc(x_loaded, 16)
            for j, name in enumerate(("L0_gnn_Wq", "L0_gnn_Wk", "L0_gnn_Wv")):
                sp.dma_start(w[:, j * D:(j + 1) * D], a[name]).then_inc(w_loaded, 16)

            programs.load(sp)

            def store(b, k, first):
                sp.wait_ge(evacuated, b + 1)
                sp.dma_start(net.kv0[cols(b * P, P), :], qkv[:, k, D:3 * D]).then_inc(stores[k], 16)

            over_blocks(sp, store, BUFS)
            programs.store(sp)
            for k in range(BUFS):
                sp.wait_ge(stores[k], 16 * len(range(k, NB, BUFS)))

        @block.vector
        def _(dve):
            programs.locate(dve)
            dve.wait_ge(x_loaded, 80)
            layer_norm_stats(dve, net, net.x, stats, aggr, 1)
            layer_norm_scale(dve, net, std_ready, scale_ready, 1)
            programs.derive(dve)

            def split(b, k, first):
                dve.wait_ge(evacuated, b + 1)
                part = [q0[:, cols(b * (3 * D) + s * D, D)] for s in range(3)]
                split3(dve, *part, qkv[:, k, 0:D], rest[:, :], parts, b * 4)

            over_blocks(dve, split, BUFS)
            programs.take(dve)

        @block.scalar
        def _(act):
            act.wait_ge(blank, 2)
            layer_norm_std(act, net, eps, aggr, std_ready, 1)
            normalize(act, net, net.h, net.x, ACT.Relu, scale_ready, 1, normed)

            programs.floats(act)

            def evacuate(b, k, first, do=(True, True)):
                if do[0]:
                    act.wait_ge(turned, b + 1)
                    act.copy(ht[:, k % 2, :], ps[:, (4 + k % 2) * BANK:(4 + k % 2) * BANK + P]).then_inc(copied, 1)
                if do[1] and there(b - 1):
                    j = (k - 1) % BUFS
                    act.wait_ge(product, b)
                    if there(b - 1 - BUFS):
                        act.wait_ge(parts, (b - BUFS) * 4)
                        act.wait_ge(stores[j], (b - 1 - j) * (16 // BUFS))
                    act.copy(qkv[:, j, :], ps[:, (6 + j % 2) * BANK:(6 + j % 2) * BANK + 3 * D])\
                        .then_inc(evacuated, 1)

            over_blocks(act, evacuate, BUFS)
            evacuate(NB, 1, False, (False, True))

        @block.tensor
        def _(pe):
            programs.count(pe)
            pe.wait_ge(w_loaded, 48)

            def project(b, k, first, do=(True, True)):
                if do[0]:
                    pe.wait_ge(normed, b + 1)
                    if not first:
                        pe.wait_ge(copied, b - 1)
                    pe.transpose(ps[:, (4 + k) * BANK:(4 + k) * BANK + P], block_of(net.h, b), net.ident[:, :])\
                        .then_inc(turned, 1)
                if do[1] and there(b - 1):
                    j = 1 - k
                    pe.wait_ge(copied, b)
                    if there(b - 3):
                        pe.wait_ge(evacuated, b - 2)
                    pe.matmul(ps[:, (6 + j) * BANK:(6 + j) * BANK + 3 * D], ht[:, j, :], w[:, :],
                              start=True, stop=True).then_inc(product, 1)

            over_blocks_unrolled(pe, project)
            project(NB, 1, False, (False, True))
            programs.turn(pe)


def clear_banks(pe, net, n):
    for k in range(n):
        last = pe.matmul(net.psum[:, k * BANK:(k + 1) * BANK], net.zeros[:, 0:P], net.zeros[:, :],
                         start=True, stop=False, skip_group_check=True)
    return last


def block_registers(nc, row, n, most, g=G):
    _, v = nc.values_load_multi_w_load_instructions(
        row[0:1, cols(n * g, g)], engines=[PE], min_val=0, max_val=most,
        skip_runtime_bounds_check_because="blocks of items are clamped when they are made")
    return v


def edges0(net, q0):
    nc = net.nc
    Z = NB * D
    LAST = L0.steps - 1
    with ExitStack() as ctx:
        def sb(name, shape, dt):
            return ctx.enter_context(nc.sbuf_tensor(name, shape, dt))

        (passed_pool, idx_ready, onehot_t, onehot, queries, prod_ready, score_ready, clipped, exp_ready, msg_ready,
         added) = sems(
            nc, "m0", "passed_pool", "idx_ready", "onehot_t", "onehot", "queries", "prod_ready", "score_ready",
            "clipped", "exp_ready", "msg_ready", "added")
        gathered = sems(nc, "m0", *[f"gathered{s}" for s in range(RING)])
        rows_loaded = sems(nc, "m0", *[f"rows_loaded{s}" for s in range(RING)])
        kv = sb("kv", [P, RING, G, 2 * D], F32)
        idx = sb("idx", [P, RING, G], I32)
        rows = sb("rows", [P, RING, GP], F16)
        oht = sb("oht", [P, 2, GP], BF16)
        oh = sb("oh", [P, RING, G, P], F32)
        prod = sb("prod", [P, 2, GP], F32)
        score = sb("score", [P, 2, G * H], F32)
        clip = sb("clip", [P, 2, G * H], F32)
        msg = sb("msg", [P, RING, G, D + H], F32)
        qe = net.psum[:, 7 * BANK:8 * BANK]
        block = ctx.enter_context(nc.Block())

        @block.gpsimd
        def _(pool):
            def gather(n, s, turn):
                pool.wait_ge(idx_ready, n + 1)
                if there(n - RING):
                    pool.wait_ge(msg_ready, n - (RING - 1))
                settle(pool, passed_pool)
                for i in range(G):
                    pool.indirect_dma_start(kv[:, s, i, :], None, net.kv0,
                                            bass.IndirectOffsetOnAxis(ap=idx[:, s, i:i + 1], axis=0))\
                        .then_inc(gathered[s], 16)

            over_turns(pool, L0.steps, gather)

        @block.sync
        def _(sp):
            def load(n, s, turn):
                if there(n - RING):
                    sp.wait_ge(onehot_t, n - (RING - 1))
                sp.dma_start(rows[:, s, :], net.local_rows[cols(n * GP, GP)].partition_broadcast(P))\
                    .then_inc(rows_loaded[s], 16)

            over_turns(sp, L0.steps, load)

        @block.scalar
        def _(act):
            for s in range(RING):
                act.copy(idx[:, s, :], net.src0[:, s * G:(s + 1) * G]).then_inc(idx_ready, 1)

            def exps(m, s):
                act.wait_ge(clipped, m + 1)
                act.activation(msg[:, s, :, D:D + H], clip[:, s % 2, :].rearrange("p (g h) -> p g h", h=H),
                               ACT.Exp, scale=1.0 / 4).then_inc(exp_ready, 1)

            def step(n, s, turn):
                act.wait_ge(gathered[s], (turn + 1) * (16 * G))
                act.copy(idx[:, s, :], net.src0[:, cols(n * G + TURN, G)]).then_inc(idx_ready, 1)
                if there(n - 1):
                    exps(n - 1, (s - 1) % RING)

            over_turns(act, L0.steps, step)
            exps(LAST, LAST % RING)

        @block.vector
        def _(dve):
            def onehots(n, s, turn):
                dve.wait_ge(rows_loaded[s], (turn + 1) * 16)
                if there(n - 2):
                    dve.wait_ge(queries, n - 1)
                dve.tensor_scalar(oht[:, s % 2, :], rows[:, s, :], net.part1[:, 0:1], None, ALU.is_equal)\
                    .then_inc(onehot_t, 1)
                if there(n - RING):
                    dve.wait_ge(added, n - (RING - 1))
                dve.tensor_tensor(oh[:, s, :, :], spread(net.lane[:, :].unsqueeze(1), [P, G, P]),
                                  spread(net.local0[:, cols(n * G, G)].unsqueeze(2), [P, G, P]), ALU.is_equal)\
                    .then_inc(onehot, 1)

            def scores(m, s, turn):
                dve.wait_ge(queries, m + 1)
                dve.wait_ge(gathered[s], turn)
                dve.tensor_tensor(prod[:, s % 2, :].rearrange("p (g d) -> p g d", d=D), kv[:, s, :, 0:D],
                                  qe.rearrange("p (g d) -> p g d", d=D), ALU.mult).then_inc(prod_ready, 1)
                dve.wait_ge(prod_ready, m + 1)
                dve.tensor_reduce(score[:, s % 2, :], prod[:, s % 2, :].rearrange("p (g d) -> p g d", d=DH),
                                  AX_X, ALU.add).then_inc(score_ready, 1)
                dve.wait_ge(score_ready, m + 1)
                dve.tensor_scalar(clip[:, s % 2, :], score[:, s % 2, :], -5.0 * 4, 5.0 * 4, ALU.max, ALU.min)\
                    .then_inc(clipped, 1)

            def messages(m, s):
                dve.wait_ge(exp_ready, m + 1)
                dve.tensor_tensor(msg[:, s, :, 0:D].rearrange("p g (h d) -> p g h d", d=DH),
                                  kv[:, s, :, D:2 * D].rearrange("p g (h d) -> p g h d", d=DH),
                                  spread(msg[:, s, :, D:D + H].unsqueeze(3), [P, G, H, DH]), ALU.mult)\
                    .then_inc(msg_ready, 1)

            def step(n, s, turn):
                onehots(n, s, turn)
                if there(n - 1):
                    scores(n - 1, (s - 1) % RING, (turn + 1 if s else turn) * (16 * G))
                if there(n - 2):
                    messages(n - 2, (s - 2) % RING)

            over_turns(dve, L0.steps, step)
            scores(LAST, LAST % RING, (LAST // RING + 1) * 16 * G)
            for m in (LAST - 1, LAST):
                messages(m, m % RING)

        @block.tensor
        def _(pe):
            clear_banks(pe, net, 7)

            def expand(n, s):
                blocks = block_registers(nc, net.blocks0, n, NB - 1)
                pe.wait_ge(onehot_t, n + 1)
                if there(n - 1):
                    pe.wait_ge(prod_ready, n)
                for i in range(G):
                    for part in range(3):
                        last = pe.matmul(qe[:, i * D:(i + 1) * D], oht[:, s % 2, i * P:(i + 1) * P],
                                         q0[:, cols(blocks[i] * (3 * D) + part * D, D)],
                                         start=(part == 0), stop=(part == 2))
                last.then_inc(queries, 1)

            def add(m, s):
                blocks = block_registers(nc, net.blocks0, m, NB - 1)
                pe.wait_ge(onehot, m + 1)
                pe.wait_ge(msg_ready, m + 1)
                for i in range(G):
                    pe.matmul(net.psum[:, cols(blocks[i] * D, D)], oh[:, s, i, :], msg[:, s, i, 0:D],
                              start=False, stop=False, skip_group_check=True)
                    last = pe.matmul(net.psum[:, cols(blocks[i] * H + Z, H)], oh[:, s, i, :], msg[:, s, i, D:D + H],
                                     start=False, stop=False, skip_group_check=True)
                last.then_inc(added, 1)

            def step(n, s, turn):
                expand(n, s)
                if there(n - 2):
                    add(n - 2, (s - 2) % RING)

            over_turns(pe, L0.steps, step)
            for m in (LAST - 1, LAST):
                add(m, m % RING)


def nodes1(net):
    nc, a = net.nc, net.a
    Z = NB * D
    with ExitStack() as ctx:
        def sb(name, shape, dt):
            return ctx.enter_context(nc.sbuf_tensor(name, shape, dt))

        (w_loaded, r_loaded, v_done, turned, copied, product, taken, stats, aggr, std_ready, scale_ready, normed,
         ready, hidden, relued, evacuated, parts, blank) = sems(
            nc, "n1", "w_loaded", "r_loaded", "vector_done", "turned", "copied", "product", "taken", "stats",
            "aggr", "std_ready", "scale_ready", "normed", "ready", "hidden", "relued", "evacuated", "parts",
            "blank")
        stores = sems(nc, "n1", *[f"store{k}" for k in range(BUFS)])
        banked, wo_loaded, bo_loaded = sems(nc, "n1", "banked", "wo_loaded", "bo_loaded")
        wo = sb("wo", [P, D], F32)
        w1 = sb("w1_", [P, DFF], F32)
        w2 = sb("w2_", [P, 2, D], F32)
        wr = sb("wr", [P, R, 3, D], F32)
        b1 = sb("b1", [P, 2], F32)
        names = ("L0_gnn_bo", "L0_gnn_ln1_g", "L0_gnn_ln1_b", "L0_gnn_b2", "L0_gnn_ln2_g", "L0_gnn_ln2_b")
        vec = sb("vec", [P, len(names), D], F32)
        eps = sb("eps1", [P, 1], F32)
        t1 = sb("t1", [P, NB, D], F32)
        at = sb("at", [P, 2, P], F32)
        f1 = sb("f1", [P, 2, 2, P], F32)
        zr = sb("zr", [P, NB * H], F32)
        qkv = sb("qkv1", [P, BUFS, R, 3 * D], F32)
        rest = sb("rest1", [P, R * D], F32)
        q_parts = sb("q_parts", [P, BUFS, R, 3, D], BF16)
        ps = net.psum

        def row(j, blocks=NB):
            return spread(vec[:, j, :].unsqueeze(1), [P, blocks, D])

        block = ctx.enter_context(nc.Block())

        @block.sync
        def _(sp):
            sp.dma_start(wo[:, :], a["L0_gnn_Wo"]).then_inc(wo_loaded, 16)
            sp.dma_start(vec[:, 0, :], a[names[0]].partition_broadcast(P)).then_inc(bo_loaded, 16)
            sp.dma_start(w1[:, :], a["L0_gnn_W1"]).then_inc(w_loaded, 16)
            sp.dma_start(w2[:, :, :], a["L0_gnn_W2"].rearrange("(c p) d -> p c d", p=P)).then_inc(w_loaded, 16)
            with nc.allow_non_contiguous_dma(reason="a short column"):
                sp.dma_start(b1[:, :], a["L0_gnn_b1"].rearrange("(c p) -> p c", p=P)).then_inc(w_loaded, 16)
            for j, name in enumerate(names[1:]):
                sp.dma_start(vec[:, j + 1, :], a[name].partition_broadcast(P)).then_inc(w_loaded, 16)
            for j, name in enumerate(("L1_gnn_W_Q", "L1_gnn_W_K", "L1_gnn_W_V")):
                for r in range(R):
                    sp.dma_start(wr[:, r, j, :].rearrange("p (h d) -> p h d", d=DH),
                                 a[name][r].rearrange("h p d -> p h d")).then_inc(r_loaded, 16)

            def store(b, k, first):
                sp.wait_ge(evacuated, (b + 1) * R)
                sp.dma_start(net.kv1[cols(b * (P * R), P * R), :].rearrange("(p r) c -> p r c", r=R),
                             qkv[:, k, :, D:3 * D]).then_inc(stores[k], 16)
                sp.wait_ge(parts, (b + 1) * 4)
                sp.dma_start(net.q1_parts[cols(b * (P * R), P * R), :].rearrange("(p r) c -> p (r c)", r=R),
                             q_parts[:, k, :, :, :].rearrange("p r s d -> p (r s d)")).then_inc(stores[k], 16)

            over_blocks(sp, store, BUFS)
            for k in range(BUFS):
                sp.wait_ge(stores[k], 32 * len(range(k, NB, BUFS)))

        @block.gpsimd
        def _(pool):
            pool.memset(eps[:, :], EPS).then_inc(blank, 1)

        @block.vector
        def _(dve):
            done = [0]

            def chain(ins):
                done[0] += 1
                ins.then_inc(v_done, 1)
                dve.wait_ge(v_done, done[0])

            def signal(ins, n):
                ins.then_inc(ready, 1)
                dve.wait_ge(ready, n)

            chain(dve.tensor_scalar(zr[:, :], ps[:, Z:Z + NB * H], 1e-6, None, ALU.add))
            chain(dve.reciprocal(zr[:, :], zr[:, :]))
            dve.tensor_tensor(t1[:, :, :].rearrange("p b (h d) -> p (b h) d", d=DH),
                              ps[:, 0:NB * D].rearrange("p (n d) -> p n d", d=DH),
                              spread(zr[:, :].unsqueeze(2), [P, NB * H, DH]), ALU.mult).then_inc(ready, 1)
            dve.wait_ge(bo_loaded, 16)
            chain(dve.tensor_tensor(net.h[:, :, :], net.h[:, :, :], row(0), ALU.add))

            def take(b, k, first):
                dve.wait_ge(product, b + 1)
                dve.tensor_tensor(block_of(net.h, b), ps[:, (2 + k) * BANK:(2 + k) * BANK + D],
                                  block_of(net.h, b), ALU.add).then_inc(taken, 1)

            over_blocks(dve, take)
            dve.wait_ge(taken, NB)
            layer_norm_stats(dve, net, net.h, stats, aggr, 1)
            layer_norm_scale(dve, net, std_ready, scale_ready, 1)
            dve.wait_ge(w_loaded, 16 * (2 + len(names)))
            for c in range(0, NB, CHUNK):
                part = slice(c, c + CHUNK)
                dve.wait_ge(normed, c + CHUNK)
                chain(dve.tensor_tensor(t1[:, part, :], t1[:, part, :], row(1, CHUNK), ALU.mult))
                signal(dve.tensor_tensor(t1[:, part, :], t1[:, part, :], row(2, CHUNK), ALU.add), 2 + c // CHUNK)
                chain(dve.tensor_tensor(net.h[:, part, :], t1[:, part, :], row(3, CHUNK), ALU.add))

            def take2(b, k, first):
                dve.wait_ge(product, b + (NB + 1))
                dve.tensor_tensor(block_of(net.h, b), ps[:, (6 + k) * BANK:(6 + k) * BANK + D],
                                  block_of(net.h, b), ALU.add).then_inc(taken, 1)

            over_blocks(dve, take2)
            dve.wait_ge(taken, 2 * NB)
            layer_norm_stats(dve, net, net.h, stats, aggr, 2)
            layer_norm_scale(dve, net, std_ready, scale_ready, 2)
            for c in range(0, NB, CHUNK):
                part = slice(c, c + CHUNK)
                dve.wait_ge(normed, NB + c + CHUNK)
                chain(dve.tensor_tensor(t1[:, part, :], t1[:, part, :], row(4, CHUNK), ALU.mult))
                chain(dve.tensor_tensor(t1[:, part, :], t1[:, part, :], row(5, CHUNK), ALU.add))
                chain(dve.tensor_tensor(net.x[:, part, :], t1[:, part, :], net.x[:, part, :], ALU.add))
                for b in range(c, c + CHUNK):
                    dve.bn_stats(net.st[:, b, :], net.x[:, b, :]).then_inc(stats, 1)
            layer_norm_stats(dve, net, net.x, stats, aggr, 3, collect=False)
            layer_norm_scale(dve, net, std_ready, scale_ready, 3)

            def split(b, k, first):
                dve.wait_ge(evacuated, (b + 1) * R)
                if there(b - BUFS):
                    dve.wait_ge(stores[k], (b - k) * (32 // BUFS))
                part = [q_parts[:, k, :, s, :] for s in range(3)]
                split3(dve, *part, qkv[:, k, :, 0:D], rest[:, :].rearrange("p (r d) -> p r d", d=D), parts, b * 4)

            over_blocks(dve, split, BUFS)

        @block.scalar
        def _(act):
            act.wait_ge(blank, 1)

            def copy(b, k, first):
                act.wait_ge(turned, b + 1)
                act.copy(at[:, k, :], ps[:, k * BANK:k * BANK + P]).then_inc(copied, 1)

            over_blocks(act, copy)
            layer_norm_std(act, net, eps, aggr, std_ready, 1)
            normalize(act, net, t1, net.h, ACT.Identity, scale_ready, 1, normed)

            def ff(b, k, first, do=(True, True)):
                if do[0]:
                    act.wait_ge(turned, b + (NB + 1))
                    act.copy(at[:, k, :], ps[:, k * BANK:k * BANK + P]).then_inc(copied, 1)
                if do[1] and there(b - 1):
                    j = 1 - k
                    act.wait_ge(hidden, b)
                    for c in range(2):
                        act.activation(f1[:, j, c, :], ps[:, (4 + j) * BANK + c * P:(4 + j) * BANK + (c + 1) * P],
                                       ACT.Relu, bias=b1[:, c:c + 1], scale=1.0).then_inc(relued, 1)

            over_blocks(act, ff)
            ff(NB, 1, False, (False, True))
            layer_norm_std(act, net, eps, aggr, std_ready, 2)
            normalize(act, net, t1, net.h, ACT.Identity, scale_ready, 2, normed)
            layer_norm_std(act, net, eps, aggr, std_ready, 3)
            normalize(act, net, net.h, net.x, ACT.Relu, scale_ready, 3, normed)

            def evacuate(b, k, first, do=(True, True)):
                if do[0]:
                    act.wait_ge(turned, b + (2 * NB + 1))
                    act.copy(at[:, k % 2, :], ps[:, k % 2 * BANK:k % 2 * BANK + P]).then_inc(copied, 1)
                if do[1] and there(b - 1):
                    j = (k - 1) % BUFS
                    if there(b - 1 - BUFS):
                        act.wait_ge(parts, (b - BUFS) * 4)
                        act.wait_ge(stores[j], (b - 1 - j) * (32 // BUFS))
                    for r in range(R):
                        act.wait_ge(banked, b * R + (r + 1 - R))
                        act.copy(qkv[:, j, r, :], ps[:, (2 + r) * BANK:(2 + r) * BANK + 3 * D])\
                            .then_inc(evacuated, 1)

            over_blocks(act, evacuate, BUFS)
            evacuate(NB, 1, False, (False, True))

        @block.tensor
        def _(pe):
            pe.wait_ge(ready, 1)
            pe.wait_ge(wo_loaded, 16)

            def out_proj(b, k, first, do=(True, True)):
                if do[0]:
                    if not first:
                        pe.wait_ge(copied, b - 1)
                    pe.transpose(ps[:, k * BANK:k * BANK + P], block_of(t1, b), net.ident[:, :]).then_inc(turned, 1)
                if do[1] and there(b - 1):
                    j = 1 - k
                    pe.wait_ge(copied, b)
                    if there(b - 3):
                        pe.wait_ge(taken, b - 2)
                    pe.matmul(ps[:, (2 + j) * BANK:(2 + j) * BANK + D], at[:, j, :], wo[:, :], start=True,
                              stop=True).then_inc(product, 1)

            over_blocks_unrolled(pe, out_proj)
            out_proj(NB, 1, False, (False, True))

            pe.wait_ge(w_loaded, 16 * (2 + len(names)))

            def ff(b, k, first, do=(True, True, True)):
                j = 1 - k
                if do[0]:
                    if b % CHUNK == 0:
                        pe.wait_ge(ready, 2 + b // CHUNK)
                    if not first:
                        pe.wait_ge(copied, b + (NB - 1))
                    pe.transpose(ps[:, k * BANK:k * BANK + P], block_of(t1, b), net.ident[:, :])\
                        .then_inc(turned, 1)
                if do[1] and there(b - 1):
                    pe.wait_ge(copied, b + NB)
                    if there(b - 3):
                        pe.wait_ge(relued, (b - 2) * 2)
                    for c in range(2):
                        last = pe.matmul(ps[:, (4 + j) * BANK + c * P:(4 + j) * BANK + (c + 1) * P],
                                         w1[:, c * P:(c + 1) * P], at[:, j, :], start=True, stop=True)
                    last.then_inc(hidden, 1)
                if do[2] and there(b - 2):
                    pe.wait_ge(relued, (b - 1) * 2)
                    if there(b - 4):
                        pe.wait_ge(taken, b + (NB - 3))
                    for c in range(2):
                        last = pe.matmul(ps[:, (6 + k) * BANK:(6 + k) * BANK + D], f1[:, k, c, :], w2[:, c, :],
                                         start=(c == 0), stop=(c == 1))
                    last.then_inc(product, 1)

            over_blocks_unrolled(pe, ff)
            ff(NB, 1, False, (False, True, True))
            ff(NB + 1, 0, False, (False, False, True))
            pe.wait_ge(r_loaded, 16 * 3 * R)
            pe.wait_ge(taken, 2 * NB)

            def project(b, k, first, do=(True, True)):
                if do[0]:
                    pe.wait_ge(normed, b + (2 * NB + 1))
                    if not first:
                        pe.wait_ge(copied, b + (2 * NB - 1))
                    pe.transpose(ps[:, k * BANK:k * BANK + P], block_of(net.h, b), net.ident[:, :])\
                        .then_inc(turned, 1)
                if do[1] and there(b - 1):
                    j = 1 - k
                    pe.wait_ge(copied, b + 2 * NB)
                    for r in range(R):
                        if there(b - 2):
                            pe.wait_ge(evacuated, (b - 1) * R + (r + 1 - R))
                        pe.matmul(ps[:, (2 + r) * BANK:(2 + r) * BANK + 3 * D], at[:, j, :],
                                  wr[:, r, :, :].rearrange("p a d -> p (a d)"), start=True, stop=True)\
                            .then_inc(banked, 1)

            over_blocks_unrolled(pe, project)
            project(NB, 1, False, (False, True))


def logits1(net, q1):
    nc, a = net.nc, net.a
    CHUNKS = 5
    BC = NB // CHUNKS
    assert BC * CHUNKS == NB and TURN <= SUBS * BC
    with ExitStack() as ctx:
        def sb(name, shape, dt):
            return ctx.enter_context(nc.sbuf_tensor(name, shape, dt))

        (passed_pool, passed_pe, idx_ready, onehot_t, queries, prod_ready, score_ready, mask_ready, bias_ready,
         logit_ready, turned, scanned, b_loaded, blank) = sems(
            nc, "m1", "passed_pool", "passed_pe", "idx_ready", "onehot_t", "queries", "prod_ready", "score_ready",
            "mask_ready", "bias_ready", "logit_ready", "turned", "scanned", "b_loaded", "blank")
        gathered = sems(nc, "m1", *[f"gathered{s}" for s in range(RING)])
        rows_loaded = sems(nc, "m1", *[f"rows_loaded{s}" for s in range(RING)])
        starts_loaded = sems(nc, "m1", *[f"starts_loaded{s}" for s in range(RING)])
        v_stored = sems(nc, "m1", *[f"v_stored{s}" for s in range(RING)])
        l_stored = sems(nc, "m1", *[f"l_stored{s}" for s in range(RING)])
        m_stored = sems(nc, "m1", *[f"m_stored{s}" for s in range(RING)])
        q_loaded = sems(nc, "m1", *[f"q_loaded{c}" for c in range(CHUNKS)])
        kv = sb("kv_", [P, RING, G, 2 * D], F32)
        idx = sb("idx_", [P, RING, G], I32)
        rows = sb("rows_", [P, RING, GP], F16)
        starts = sb("starts", [RH, RING, GP], BF16)
        oht = sb("oht_", [P, 2, GP], BF16)
        prod = sb("prod_", [P, 2, GP], F32)
        score = sb("score_", [P, 2, G * H], F32)
        mask = sb("mask", [P, 2, G * R], F32)
        bias = sb("bias", [P, RH], F32)
        shifted = sb("shifted", [P, 2, G, RH], F32)
        logit = sb("logit", [P, RING, G, RH], F32)
        top = sb("top", [RH, RING, GP], F32)
        low = sb("low", [P, 1], F32)
        ps = net.psum
        block = ctx.enter_context(nc.Block())

        @block.gpsimd
        def _(pool):
            pool.memset(low[:, :], -BIG).then_inc(blank, 1)

            def gather(n, s, turn):
                pool.wait_ge(idx_ready, n + 1)
                if there(n - RING):
                    pool.wait_ge(prod_ready, n - (RING - 1))
                    pool.wait_ge(v_stored[s], turn * 16)
                settle(pool, passed_pool)
                for i in range(G):
                    pool.indirect_dma_start(kv[:, s, i, :], None, net.kv1,
                                            bass.IndirectOffsetOnAxis(ap=idx[:, s, i:i + 1], axis=0))\
                        .then_inc(gathered[s], 16)

            over_turns(pool, L1.steps, gather)

        @block.sync
        def _(sp):
            sp.dma_start(bias[:, :], a["L1_gnn_attn_bias"].rearrange("r h -> (r h)").partition_broadcast(P))\
                .then_inc(b_loaded, 16)

            def load_queries(c):
                b = slice(c * BC, (c + 1) * BC)
                for j in range(SUBS):
                    sp.dma_start(q1[:, :].rearrange("p (b j c) -> p b j c", j=SUBS, c=3 * D)[:, b, j, :],
                                 net.q1_parts.rearrange("(b q) c -> q b c", q=P * R)
                                 [j * GROUP * R:j * GROUP * R + P, b, :]).then_inc(q_loaded[c], 16)

            def load(n, s, turn):
                if isinstance(n, int) and s == 0:
                    for c in range(CHUNKS):
                        load_queries(c)
                if there(n - RING):
                    sp.wait_ge(onehot_t, n - (RING - 1))
                sp.dma_start(rows[:, s, :], net.key_rows[cols(n * GP, GP)].partition_broadcast(P))\
                    .then_inc(rows_loaded[s], 16)
                if there(n - RING):
                    sp.wait_ge(scanned, n - (RING - 1))
                sp.dma_start(starts[:, s, :], net.start_rows[cols(n * GP, GP)].partition_broadcast(RH))\
                    .then_inc(starts_loaded[s], 16)

            over_turns(sp, L1.steps, load)

        @block.scalar
        def _(act):
            for s in range(RING):
                act.copy(idx[:, s, :], net.src1[:, s * G:(s + 1) * G]).then_inc(idx_ready, 1)

            def store_logits(m, s):
                act.wait_ge(logit_ready, m + 1)
                act.dma_start(net.l_spill[cols(m, 1), :, :].rearrange("a p c -> p (a c)"),
                              logit[:, s, :, :].rearrange("p g c -> p (g c)")).then_inc(l_stored[s], 16)

            def store_maxima(m, s):
                act.wait_ge(scanned, m + 1)
                act.dma_start(net.m_spill[cols(m, 1), :, :].rearrange("a p c -> p (a c)"), top[:, s, :])\
                    .then_inc(m_stored[s], 16)

            def step(n, s, turn):
                act.wait_ge(gathered[s], (turn + 1) * (16 * G))
                act.copy(idx[:, s, :], net.src1[:, cols(n * G + TURN, G)]).then_inc(idx_ready, 1)
                act.dma_start(net.v_spill[cols(n, 1), :, :, :].rearrange("a p g d -> p (a g) d"),
                              kv[:, s, :, D:2 * D]).then_inc(v_stored[s], 16)
                if there(n - 1):
                    store_logits(n - 1, (s - 1) % RING)
                if there(n - 2):
                    store_maxima(n - 2, (s - 2) % RING)

            over_turns(act, L1.steps, step)
            store_logits(L1.steps - 1, RING - 1)
            store_maxima(L1.steps - 2, RING - 2)
            store_maxima(L1.steps - 1, RING - 1)
            for s in range(RING):
                for stored in (v_stored, l_stored, m_stored):
                    act.wait_ge(stored[s], 16 * (L1.steps // RING))

        @block.vector
        def _(dve):
            dve.wait_ge(b_loaded, 16)
            dve.wait_ge(blank, 1)

            def onehots(n, s, turn):
                dve.wait_ge(rows_loaded[s], (turn + 1) * 16)
                if there(n - 2):
                    dve.wait_ge(queries, n - 1)
                dve.tensor_scalar(oht[:, s % 2, :], rows[:, s, :], net.part1[:, 0:1], None, ALU.is_equal)\
                    .then_inc(onehot_t, 1)

            def scores(m, s, turn):
                o = s % 2
                dve.tensor_tensor(mask[:, o, :].rearrange("p (g r) -> p g r", r=R),
                                  spread(net.rel[:, cols(m * G, G)].unsqueeze(2), [P, G, R]),
                                  spread(net.lane[:, 0:R].unsqueeze(1), [P, G, R]), ALU.not_equal)\
                    .then_inc(mask_ready, 1)
                dve.wait_ge(queries, m + 1)
                dve.wait_ge(gathered[s], (turn + 1) * (16 * G))
                dve.scalar_tensor_tensor(out=prod[:, o, :].rearrange("p (g d) -> p g d", d=D), in0=kv[:, s, :, 0:D],
                                         scalar=DH ** -0.5,
                                         in1=ps[:, o * BANK:(o + 1) * BANK].rearrange("p (g d) -> p g d", d=D),
                                         op0=ALU.mult, op1=ALU.mult).then_inc(prod_ready, 1)
                dve.wait_ge(mask_ready, m + 1)
                dve.scalar_tensor_tensor(
                    out=shifted[:, o, :, :].rearrange("p g (r h) -> p g r h", h=H),
                    in0=spread(mask[:, o, :].rearrange("p (g r) -> p g r", r=R).unsqueeze(3), [P, G, R, H]),
                    scalar=-BIG, in1=spread(bias[:, :].rearrange("p (r h) -> p r h", h=H).unsqueeze(1), [P, G, R, H]),
                    op0=ALU.mult, op1=ALU.add).then_inc(bias_ready, 1)
                dve.wait_ge(prod_ready, m + 1)
                dve.tensor_reduce(score[:, o, :], prod[:, o, :].rearrange("p (g d) -> p g d", d=DH),
                                  AX_X, ALU.add).then_inc(score_ready, 1)
                dve.wait_ge(bias_ready, m + 1)
                dve.wait_ge(score_ready, m + 1)
                if there(m - RING):
                    dve.wait_ge(l_stored[s], turn * 16)
                dve.tensor_tensor(
                    logit[:, s, :, :].rearrange("p g (r h) -> p g r h", h=H),
                    spread(score[:, o, :].rearrange("p (g h) -> p g h", h=H).unsqueeze(2), [P, G, R, H]),
                    shifted[:, o, :, :].rearrange("p g (r h) -> p g r h", h=H), ALU.add).then_inc(logit_ready, 1)

            def maxima(m, s, turn):
                dve.wait_ge(starts_loaded[s], (turn + 1) * 16)
                dve.wait_ge(turned, m + 1)
                if there(m - RING):
                    dve.wait_ge(m_stored[s], turn * 16)
                if there(m - 1):
                    dve.wait_ge(scanned, m)
                    initial = top[:, (s - 1) % RING, GP - 1:GP]
                else:
                    initial = low[0:RH, 0:1]
                o = 2 + s % 2
                dve.tensor_tensor_scan(top[:, s, :], starts[:, s, :], ps[0:RH, o * BANK:(o + 1) * BANK], initial,
                                       ALU.add, ALU.max).then_inc(scanned, 1)

            def step(n, s, turn):
                onehots(n, s, turn)
                if there(n - 1):
                    scores(n - 1, (s - 1) % RING, turn if s else turn - 1)
                if there(n - 2):
                    maxima(n - 2, (s - 2) % RING, turn if s >= 2 else turn - 1)

            over_turns(dve, L1.steps, step)
            scores(L1.steps - 1, RING - 1, (L1.steps // RING) - 1)
            maxima(L1.steps - 2, RING - 2, (L1.steps // RING) - 1)
            maxima(L1.steps - 1, RING - 1, (L1.steps // RING) - 1)

        @block.tensor
        def _(pe):
            def expand(n, s):
                groups = block_registers(nc, net.groups1, n, NG - 1)
                pe.wait_ge(onehot_t, n + 1)
                if there(n - 2):
                    pe.wait_ge(prod_ready, n - 1)
                o = s % 2
                for i in range(G):
                    for part in range(3):
                        last = pe.matmul(ps[:, o * BANK + i * D:o * BANK + (i + 1) * D],
                                         oht[:, o, i * P:(i + 1) * P],
                                         q1[:, cols(groups[i] * (3 * D) + part * D, D)],
                                         start=(part == 0), stop=(part == 2))
                last.then_inc(queries, 1)

            def turn_logits(m, s):
                pe.wait_ge(logit_ready, m + 1)
                if there(m - 2):
                    pe.wait_ge(scanned, m - 1)
                settle(pe, passed_pe)
                o = 2 + s % 2
                for i in range(G):
                    last = pe.transpose(ps[0:RH, o * BANK + i * P:o * BANK + (i + 1) * P], logit[:, s, i, :],
                                        net.ident[:, :])
                last.then_inc(turned, 1)

            def step(n, s, turn):
                if isinstance(n, int) and s == 0:
                    pe.wait_ge(q_loaded[turn], 16 * SUBS)
                expand(n, s)
                if there(n - 1):
                    turn_logits(n - 1, (s - 1) % RING)

            over_turns(pe, L1.steps, step, peeled=CHUNKS)
            turn_logits(L1.steps - 1, RING - 1)


def sums1(net, probs, rsum):
    nc = net.nc
    LAST = WIDE_STEPS - 1
    with ExitStack() as ctx:
        def sb(name, shape, dt):
            return ctx.enter_context(nc.sbuf_tensor(name, shape, dt))

        passed_sp, passed_act, passed_pe, passed_dve, passed_pool = sems(
            nc, "s1", "passed_sp", "passed_act", "passed_pe", "passed_dve", "passed_pool")
        (blank, key_ready, scanned, turned, diff_ready, least_ready, exp_ready, hi_ready, left_ready, parts_ready,
         away_ready, shared, added, v_done, split) = sems(
            nc, "s1", "blank", "key_ready", "scanned", "turned", "diff_ready", "least_ready", "exp_ready",
            "hi_ready", "left_ready", "parts_ready", "away_ready", "shared", "added", "vector_done", "split")
        loaded = sems(nc, "s1", *[f"loaded{s}" for s in range(RING)])
        logits_loaded = sems(nc, "s1", *[f"logits_loaded{s}" for s in range(RING)])
        starts = sb("starts_", [RH, RING, GWP], BF16)
        top = sb("top_", [RH, RING, GWP], F32)
        logit = sb("logit_", [P, RING, GW * RH], F32)
        diff = sb("diff", [P, 2, GW * RH], F32)
        least = sb("least", [P, 2, GW, H], F32)
        oh = sb("oh_", [P, RING, GW, P], BF16)
        key16 = sb("key16", [P, L1.items], BF16)
        exps = sb("exps", [P, RING, GW * H], F32)
        parts = sb("parts", [P, RING, GW, 3, H], BF16)
        away = sb("away", [P, SHARE, P], F32)
        left = sb("left", [P, GW, H], F32)
        rs = sb("rs", [P, NG * H], F32)
        rest = sb("rest_s", [P, NG * H], F32)
        low = sb("low_", [P, 1], F32)
        ps = net.psum
        block = ctx.enter_context(nc.Block())

        def back(n):
            return WIDE_STEPS - 1 - n if isinstance(n, int) else (WIDE_STEPS - 1) - n

        @block.gpsimd
        def _(pool):
            pool.memset(low[:, :], -BIG).then_inc(blank, 1)

            def split_(n, s, turn):
                hi, mid, lo = (parts[:, s, :, k, :] for k in range(3))
                pool.wait_ge(hi_ready, n + 1)
                if there(n - 1):
                    pool.wait_ge(parts_ready, n)
                pool.tensor_tensor(left[:, :, :], exps[:, s, :].rearrange("p (g h) -> p g h", h=H), hi, ALU.subtract)\
                    .then_inc(left_ready, 1)
                pool.wait_ge(left_ready, n * 2 + 1)
                settle(pool, passed_pool)
                pool.tensor_copy(mid, left[:, :, :]).then_inc(left_ready, 1)
                pool.wait_ge(left_ready, n * 2 + 2)
                pool.tensor_tensor(lo, left[:, :, :], mid, ALU.subtract).then_inc(parts_ready, 1)

            over_turns(pool, WIDE_STEPS, split_)

        @block.sync
        def _(sp):
            def load(n, s, turn):
                at = back(n)
                if there(n - RING):
                    sp.wait_ge(turned, n - (RING - 1))
                    settle(sp, passed_sp)
                    sp.wait_ge(scanned, n - (RING - 2))
                    settle(sp, passed_sp)
                sp.dma_start(starts[:, s, :], net.start_rows[cols(at * GWP + 1, GWP)].partition_broadcast(RH))\
                    .then_inc(loaded[s], 16)
                sp.dma_start(top[:, s, :].rearrange("p (a c) -> p a c", a=2),
                             net.m_spill[cols(at * 2, 2), :, :].rearrange("a p c -> p a c"))\
                    .then_inc(loaded[s], 16)

            over_turns(sp, WIDE_STEPS, load)

        @block.vector
        def _(dve):
            dve.wait_ge(blank, 1)
            dve.tensor_copy(key16[:, :], net.key[:, 0:L1.items]).then_inc(key_ready, 1)
            dve.wait_ge(key_ready, 1)

            def maxima(n, s, turn):
                dve.wait_ge(loaded[s], (turn + 1) * 32)
                if there(n - 1):
                    dve.wait_ge(scanned, n)
                    initial = top[:, (s - 1) % RING, 0:1]
                else:
                    initial = low[0:RH, 0:1]
                dve.tensor_tensor_scan(top[:, s, ::-1], starts[:, s, ::-1], top[:, s, ::-1], initial,
                                       ALU.add, ALU.max).then_inc(scanned, 1)

            def onehots(n, s):
                if there(n - RING):
                    dve.wait_ge(added, n - (RING - 1))
                settle(dve, passed_dve)
                dve.tensor_tensor(oh[:, s, SHARE:, :], spread(net.lane16[:, :].unsqueeze(1), [P, GW - SHARE, P]),
                                  spread(key16[:, cols(back(n) * GW + SHARE, GW - SHARE)].unsqueeze(2),
                                         [P, GW - SHARE, P]),
                                  ALU.is_equal)

            def diffs(m, s, turn):
                o = s % 2
                dve.wait_ge(logits_loaded[s], (turn + 1) * 16)
                dve.wait_ge(turned, m + 1)
                maxima_t = ps[:, (SUM_BANKS + o) * BANK:(SUM_BANKS + o) * BANK + GW * RH]
                dve.scalar_tensor_tensor(out=diff[:, o, :], in0=maxima_t,
                                         scalar=NEG, in1=logit[:, s, :], op0=ALU.max, op1=ALU.subtract)\
                    .then_inc(diff_ready, 1)

            def choose(m, s):
                o = s % 2
                dve.wait_ge(diff_ready, m + 1)
                if there(m - 2):
                    dve.wait_ge(exp_ready, m - 1)
                dve.tensor_reduce(least[:, o, :, :], diff[:, o, :].rearrange("p (g r h) -> p g h r", r=R, h=H), AX_X,
                                  ALU.min).then_inc(least_ready, 1)

            def step(n, s, turn):
                maxima(n, s, turn)
                if there(n - 1):
                    diffs(n - 1, (s - 1) % RING, turn if s else turn - 1)
                onehots(n, s)
                if there(n - 1):
                    choose(n - 1, (s - 1) % RING)

            over_turns(dve, WIDE_STEPS, step)
            diffs(LAST, LAST % RING, LAST // RING)
            choose(LAST, LAST % RING)
            dve.wait_ge(added, WIDE_STEPS)
            for k in range(SUM_BANKS):
                g = slice(k * PER_BANK, min((k + 1) * PER_BANK, NG))
                n = g.stop - g.start
                dve.tensor_reduce(rs[:, g.start * H:g.stop * H],
                                  ps[:, k * BANK:k * BANK + n * 3 * H].rearrange("p (g s h) -> p g h s", s=3, h=H),
                                  AX_X, ALU.add).then_inc(v_done, 1)
            dve.wait_ge(v_done, SUM_BANKS)
            dve.tensor_scalar(rs[:, :], rs[:, :], 1e-12, None, ALU.add).then_inc(v_done, 1)
            dve.wait_ge(v_done, SUM_BANKS + 1)
            dve.reciprocal(rs[:, :], rs[:, :]).then_inc(v_done, 1)
            dve.wait_ge(v_done, SUM_BANKS + 2)
            part = [rsum[:, :].rearrange("p (g s h) -> p g s h", s=3, h=H)[:, :, s, :] for s in range(3)]
            split3(dve, *part, rs[:, :].rearrange("p (g h) -> p g h", h=H),
                   rest[:, :].rearrange("p (g h) -> p g h", h=H), split, 0)

        @block.scalar
        def _(act):
            def exponentials(m, s):
                act.wait_ge(least_ready, m + 1)
                if there(m - RING):
                    act.wait_ge(added, m - (RING - 1))
                act.activation(exps[:, s, :], least[:, s % 2, :, :].rearrange("p g h -> p (g h)"), ACT.Exp,
                               scale=-1.0).then_inc(exp_ready, 1)
                act.wait_ge(exp_ready, m + 1)
                act.copy(parts[:, s, :, 0, :], exps[:, s, :].rearrange("p (g h) -> p g h", h=H))\
                    .then_inc(hi_ready, 1)
                settle(act, passed_act)
                act.copy(probs[:, cols(back(m) * (GW * H), GW * H)], exps[:, s, :])

            def onehots(m, s):
                if there(m - RING):
                    act.wait_ge(added, m - (RING - 1))
                settle(act, passed_act)
                scalar_onehots(act, net, oh[:, s, 0:SHARE, :], away, net.key, m, back(m) * GW, away_ready, shared)

            def step(n, s, turn):
                act.dma_start(logit[:, s, :].rearrange("p (a c) -> p a c", a=2),
                              net.l_spill[cols(back(n) * 2, 2), :, :].rearrange("a p c -> p a c"))\
                    .then_inc(logits_loaded[s], 16)
                if there(n - 3):
                    exponentials(n - 3, (s - 3) % RING)
                if there(n - 2):
                    onehots(n - 2, (s - 2) % RING)

            over_turns(act, WIDE_STEPS, step, peeled=2)
            for m in range(WIDE_STEPS - 3, WIDE_STEPS):
                exponentials(m, m % RING)
                if m < LAST:
                    onehots(m + 1, (m + 1) % RING)

        @block.tensor
        def _(pe):
            clear_banks(pe, net, SUM_BANKS)

            def turn_maxima(n, s):
                pe.wait_ge(scanned, n + 1)
                if there(n - 2):
                    pe.wait_ge(diff_ready, n - 1)
                settle(pe, passed_pe)
                o = s % 2
                for i in range(GW):
                    last = pe.transpose(ps[:, (SUM_BANKS + o) * BANK + i * RH:(SUM_BANKS + o) * BANK + (i + 1) * RH],
                                        top[:, s, i * P:(i + 1) * P], net.ident[0:RH, 0:RH])
                last.then_inc(turned, 1)

            def add(m, s):
                at = back(m)
                sums = block_registers(nc, net.sums1, at, (SUM_BANKS - 1) * BANK + (PER_BANK - 1) * 3 * H, GW)
                pe.wait_ge(shared, m + 1)
                pe.wait_ge(parts_ready, m + 1)
                for i in range(GW):
                    last = pe.matmul(ps[:, cols(sums[i], 3 * H)], oh[:, s, i, :],
                                     parts[:, s, i, :, :].rearrange("p a h -> p (a h)"),
                                     start=False, stop=False, skip_group_check=True)
                last.then_inc(added, 1)

            def step(n, s, turn):
                turn_maxima(n, s)
                if there(n - 2):
                    add(n - 2, (s - 2) % RING)

            over_turns(pe, WIDE_STEPS, step)
            for m in (LAST - 1, LAST):
                add(m, m % RING)


def values1(net, probs, rsum):
    nc = net.nc
    LAST = WIDE_STEPS - 1
    PG = 2 * GW
    PAIRS = WIDE_STEPS // 2
    assert PAIRS * 2 == WIDE_STEPS and PG * 3 * H <= BANK and (PAIRS + 1) * PG <= L1.cols * P
    with ExitStack() as ctx:
        def sb(name, shape, dt):
            return ctx.enter_context(nc.sbuf_tensor(name, shape, dt))

        (onehot_t, scales, scaled, attn_ready, msg_ready, added, rows_loaded) = sems(
            nc, "v1", "onehot_t", "scales", "scaled", "attn_ready", "msg_ready", "added", "rows_loaded")
        loaded = sems(nc, "v1", *[f"loaded{s}" for s in range(RING)])
        rows = sb("rows2", [P, PG * P], F16)
        v = sb("v2", [P, RING, GW, D], F32)
        msg = sb("msg2", [P, RING, GW, D], F32)
        oht = sb("oht2", [P, PG * P], BF16)
        oh = sb("oh2", [P, RING, GW, P], F32)
        scale = sb("scale", [P, PG, H], F32)
        attn = sb("attn", [P, PG, H], F32)
        ps = net.psum
        se = net.psum[:, 7 * BANK:7 * BANK + PG * 3 * H]
        block = ctx.enter_context(nc.Block())

        @block.sync
        def _(sp):
            def load(n, s, turn):
                if there(n - RING):
                    sp.wait_ge(msg_ready, n - (RING - 1))
                sp.dma_start(v[:, s, :, :].rearrange("p (a g) d -> p a (g d)", a=2),
                             net.v_spill[cols(n * 2, 2), :, :, :].rearrange("a p g d -> p a (g d)"))\
                    .then_inc(loaded[s], 16)

            over_turns(sp, WIDE_STEPS, load)

        @block.scalar
        def _(act):
            def load(pair):
                act.dma_start(rows[:, :], net.key_rows[cols(pair * (PG * P), PG * P)].partition_broadcast(P))\
                    .then_inc(rows_loaded, 16)

            load(0)
            with act.Fori(1, PAIRS + 1) as pair:
                act.wait_ge(onehot_t, pair)
                load(pair)

        @block.vector
        def _(dve):
            def onehots_t(pair):
                dve.wait_ge(rows_loaded, (pair + 1) * 16)
                if there(pair - 1):
                    dve.wait_ge(scales, pair)
                dve.tensor_scalar(oht[:, :], rows[:, :], net.part1[:, 0:1], None, ALU.is_equal)\
                    .then_inc(onehot_t, 1)

            def attention(pair):
                dve.wait_ge(scales, pair + 1)
                dve.tensor_reduce(scale[:, :, :], se.rearrange("p (i s h) -> p i h s", s=3, h=H), AX_X, ALU.add)\
                    .then_inc(scaled, 1)
                onehots_t(pair + 1)
                dve.wait_ge(scaled, pair + 1)
                dve.tensor_tensor(attn[:, :, :].rearrange("p i h -> p (i h)"),
                                  scale[:, :, :].rearrange("p i h -> p (i h)"),
                                  probs[:, cols(pair * (PG * H), PG * H)], ALU.mult).then_inc(attn_ready, 1)

            def step(n, s, turn):
                pair = turn * 2 + s // 2
                if s % 2 == 0:
                    attention(pair)
                if there(n - RING):
                    dve.wait_ge(added, n - (RING - 1))
                dve.tensor_tensor(oh[:, s, :, :], spread(net.lane[:, :].unsqueeze(1), [P, GW, P]),
                                  spread(net.local1[:, cols(n * GW, GW)].unsqueeze(2), [P, GW, P]), ALU.is_equal)
                if s % 2 == 0:
                    dve.wait_ge(attn_ready, pair + 1)
                dve.wait_ge(loaded[s], (turn + 1) * 16)
                dve.tensor_tensor(msg[:, s, :, :].rearrange("p g (h d) -> p g h d", d=DH),
                                  v[:, s, :, :].rearrange("p g (h d) -> p g h d", d=DH),
                                  spread(attn[:, (s % 2) * GW:(s % 2 + 1) * GW, :].unsqueeze(3), [P, GW, H, DH]),
                                  ALU.mult).then_inc(msg_ready, 1)

            onehots_t(0)
            over_turns(dve, WIDE_STEPS, step)

        @block.tensor
        def _(pe):
            clear_banks(pe, net, 7)

            def expand(pair):
                groups = block_registers(nc, net.groups1, pair, NG - 1, PG)
                pe.wait_ge(onehot_t, pair + 1)
                if there(pair - 1):
                    pe.wait_ge(scaled, pair)
                for i in range(PG):
                    last = pe.matmul(se[:, i * 3 * H:(i + 1) * 3 * H], oht[:, i * P:(i + 1) * P],
                                     rsum[:, cols(groups[i] * (3 * H), 3 * H)], start=True, stop=True)
                last.then_inc(scales, 1)

            def add(m, s):
                blocks = block_registers(nc, net.blocks1, m, NB - 1, GW)
                pe.wait_ge(msg_ready, m + 1)
                for i in range(GW):
                    last = pe.matmul(ps[:, cols(blocks[i] * D, D)], oh[:, s, i, :], msg[:, s, i, :],
                                     start=False, stop=False, skip_group_check=True)
                last.then_inc(added, 1)

            def step(n, s, turn):
                if there(n - 1):
                    add(n - 1, (s - 1) % RING)
                if s % 2 == 0:
                    expand(turn * 2 + s // 2 + 1)

            expand(0)
            over_turns(pe, WIDE_STEPS, step)
            add(LAST, LAST % RING)


def nodes2(net):
    nc, a = net.nc, net.a
    with ExitStack() as ctx:
        def sb(name, shape, dt):
            return ctx.enter_context(nc.sbuf_tensor(name, shape, dt))

        (w_loaded, v_done, ready, w_turned, w_copied, turned, copied, product, taken, stats, aggr, std_ready,
         scale_ready, normed, blank, finished, stored) = sems(
            nc, "n2", "w_loaded", "vector_done", "ready", "w_turned", "w_copied", "turned", "copied",
            "product", "taken", "stats", "aggr", "std_ready", "scale_ready", "normed", "blank", "finished",
            "stored")
        w = sb("w_out", [P, D], F32)
        wt = sb("wt_out", [P, D], F32)
        names = ("L1_gnn_out_proj_b", "L1_gnn_ln_gamma", "L1_gnn_ln_beta")
        vec = sb("vec2", [P, len(names), D], F32)
        eps = sb("eps2", [P, 1], F32)
        t1 = sb("t2", [P, NB, D], F32)
        at = sb("at2", [P, 2, P], F32)
        ps = net.psum

        def row(j, blocks=NB):
            return spread(vec[:, j, :].unsqueeze(1), [P, blocks, D])

        block = ctx.enter_context(nc.Block())

        @block.gpsimd
        def _(pool):
            pool.memset(eps[:, :], EPS).then_inc(blank, 1)

        @block.sync
        def _(sp):
            sp.dma_start(w[:, :], a["L1_gnn_out_proj_w"]).then_inc(w_loaded, 16)
            for j, name in enumerate(names):
                sp.dma_start(vec[:, j, :], a[name].partition_broadcast(P)).then_inc(w_loaded, 16)
            for b in range(0, NB, CHUNK):
                sp.wait_ge(finished, b // CHUNK + 1)
                sp.dma_start(net.out[b * NODES:(b + NB // 5) * NODES, :].rearrange("(b p) d -> p b d", p=NODES),
                             t1[0:NODES, b:b + NB // 5, :]).then_inc(stored, 16)
            sp.wait_ge(stored, 16 * 5)

        @block.vector
        def _(dve):
            done = [0]

            def chain(ins):
                done[0] += 1
                ins.then_inc(v_done, 1)
                dve.wait_ge(v_done, done[0])

            dve.tensor_copy(t1[:, :, :].rearrange("p b d -> p (b d)"), ps[:, 0:NB * D]).then_inc(ready, 1)
            dve.wait_ge(w_loaded, 16 * (1 + len(names)))
            chain(dve.tensor_tensor(net.h[:, :, :], net.h[:, :, :], row(0), ALU.add))

            def take(b, k, first):
                dve.wait_ge(product, b + 1)
                dve.tensor_tensor(block_of(net.h, b), ps[:, (2 + k) * BANK:(2 + k) * BANK + D],
                                  block_of(net.h, b), ALU.add).then_inc(taken, 1)

            over_blocks(dve, take)
            dve.wait_ge(taken, NB)
            layer_norm_stats(dve, net, net.h, stats, aggr, 1)
            layer_norm_scale(dve, net, std_ready, scale_ready, 1)
            for c in range(0, NB, CHUNK):
                part = slice(c, c + CHUNK)
                dve.wait_ge(normed, c + CHUNK)
                chain(dve.tensor_tensor(t1[:, part, :], t1[:, part, :], row(1, CHUNK), ALU.mult))
                chain(dve.tensor_tensor(t1[:, part, :], t1[:, part, :], row(2, CHUNK), ALU.add))
                dve.tensor_tensor(t1[:, part, :], t1[:, part, :], net.x[:, part, :], ALU.add).then_inc(finished, 1)

        @block.scalar
        def _(act):
            act.wait_ge(blank, 1)
            act.wait_ge(w_turned, 1)
            act.copy(wt[:, :], ps[:, 4 * BANK:4 * BANK + D]).then_inc(w_copied, 1)

            def copy(b, k, first):
                act.wait_ge(turned, b + 1)
                act.copy(at[:, k, :], ps[:, k * BANK:k * BANK + P]).then_inc(copied, 1)

            over_blocks(act, copy)
            layer_norm_std(act, net, eps, aggr, std_ready, 1)
            normalize(act, net, t1, net.h, ACT.Identity, scale_ready, 1, normed)

        @block.tensor
        def _(pe):
            pe.wait_ge(ready, 1)
            pe.wait_ge(w_loaded, 16 * (1 + len(names)))
            pe.transpose(ps[:, 4 * BANK:4 * BANK + D], w[:, :], net.ident[:, :]).then_inc(w_turned, 1)
            pe.wait_ge(w_copied, 1)

            def out_proj(b, k, first, do=(True, True)):
                if do[0]:
                    if not first:
                        pe.wait_ge(copied, b - 1)
                    pe.transpose(ps[:, k * BANK:k * BANK + P], block_of(t1, b), net.ident[:, :]).then_inc(turned, 1)
                if do[1] and there(b - 1):
                    j = 1 - k
                    pe.wait_ge(copied, b)
                    if there(b - 3):
                        pe.wait_ge(taken, b - 2)
                    pe.matmul(ps[:, (2 + j) * BANK:(2 + j) * BANK + D], at[:, j, :], wt[:, :], start=True,
                              stop=True).then_inc(product, 1)

            over_blocks_unrolled(pe, out_proj)
            out_proj(NB, 1, False, (False, True))


_OUTS = [((N, D), "float32")]


def kernel(**inputs):
    import numpy as _np
    import concourse.bacc as _bacc
    from concourse import mybir as _mybir
    from concourse.bass_utils import run_bass_kernel_spmd as _run

    nc = _bacc.Bacc("TRN2", target_bir_lowering=False, num_devices=1)
    arrays, args = {}, {}
    for name, value in inputs.items():
        v = _np.ascontiguousarray(value)
        arrays[f"in_{name}"] = v
        args[name] = nc.dram_tensor(f"in_{name}", v.shape, _mybir.dt.from_np(v.dtype), kind="ExternalInput").ap()
    out = nc.dram_tensor("out_0", _OUTS[0][0], F32, kind="ExternalOutput").ap()
    build(nc, args, out)
    r = _run(nc, [arrays], core_ids=[0])
    return r.results[0]["out_0"]
```
